# Optimizing a Trainium2 kernel written in Bass

```python
import numpy as np
import jax
import jax.numpy as jnp

def _softmax(x, axis=-1):
    return jax.nn.softmax(x, axis=axis)

def _gelu(x):
    return jax.nn.gelu(x, approximate=True)

def _silu(x):
    return jax.nn.silu(x)

def _sigmoid(x):
    return jax.nn.sigmoid(x)

def _layernorm(x, axis=-1, eps=1e-05):
    m = jnp.mean(x, axis=axis, keepdims=True)
    v = jnp.var(x, axis=axis, keepdims=True)
    return (x - m) / jnp.sqrt(v + eps)

def _scatter_add(tgt, idx, src, axis=0):
    return tgt.at[idx].add(src)

def _segment_sum(src, seg, n):
    return jax.ops.segment_sum(src, seg, n)
kernel_name = 'mk_decoder_postln_d2_seqx_r8_f0df78'

def setup_inputs(seed: int=0):
    np.random.seed(seed)
    _w = jnp.asarray

    def _rec_inputs():
        import jax
        import jax.numpy as jnp
        _rk = jax.random.key(seed)
        x = -0.000125 + 0.9999 * jax.random.normal(jax.random.fold_in(_rk, 1), (8, 128, 512), jnp.float32)
        _lenS = 128 - jax.random.randint(jax.random.fold_in(_rk, 7), (8,), 0, max(1, 128 // 4) + 1, jnp.int32)
        _lenS2 = 128 - jax.random.randint(jax.random.fold_in(_rk, 8), (8,), 0, max(1, 128 // 4) + 1, jnp.int32)
        _ctx_4096P = jax.random.normal(jax.random.fold_in(_rk, 11), (8, 16, 512), jnp.float32)
        _ctx_4096c = jax.random.dirichlet(jax.random.fold_in(_rk, 511), 0.3 * jnp.ones((16,), jnp.float32), (8, 128))
        _ctx_4096t = jnp.einsum('bsk,bkd->bsd', _ctx_4096c, _ctx_4096P)
        _ctx_4096t = _ctx_4096t * jax.lax.rsqrt(jnp.mean(jnp.square(_ctx_4096t)) + 1e-12) * 0.953939
        ctx_4096 = -1.52775e-05 + 0.999936 * (_ctx_4096t + 0.3 * jax.random.normal(jax.random.fold_in(_rk, 611), (8, 128, 512), jnp.float32))
        return (x, ctx_4096)
    x, ctx_4096 = _rec_inputs()

    def _L0_attn_setup():
        import jax, jax.numpy as jnp
        import numpy as np
        H = 512
        D_IN = 1024
        N = 16
        K = 4
        R = 32
        EPS = 1e-06

        def rms_forward(x, eps=EPS):
            xf = x.astype(jnp.float32)
            var = jnp.mean(xf * xf, axis=-1, keepdims=True)
            return (xf * jax.lax.rsqrt(var + eps)).astype(x.dtype)
        key = jax.random.key(seed)
        ks = jax.random.split(key, 10)
        s = 0.02
        hidden_states = jax.random.normal(ks[0], (2, 128, H), dtype=jnp.float32)
        W_in = jax.random.normal(ks[1], (2 * D_IN, H), dtype=jnp.float32) * s
        conv_w = jax.random.normal(ks[2], (D_IN, K), dtype=jnp.float32) * 0.2
        conv_b = jax.random.normal(ks[3], (D_IN,), dtype=jnp.float32) * 0.02
        W_x = jax.random.normal(ks[4], (R + 2 * N, D_IN), dtype=jnp.float32) * s
        W_dt = jax.random.normal(ks[5], (D_IN, R), dtype=jnp.float32) * s
        b_dt = jax.random.normal(ks[6], (D_IN,), dtype=jnp.float32) * 0.02
        A_log = jnp.log(jnp.broadcast_to(jnp.arange(1, N + 1, dtype=jnp.float32)[None, :], (D_IN, N)))
        D = jnp.ones((D_IN,), dtype=jnp.float32)
        W_out = jax.random.normal(ks[7], (H, D_IN), dtype=jnp.float32) * s
        return {'hidden_states': hidden_states, 'W_in': W_in, 'conv_w': conv_w, 'conv_b': conv_b, 'W_x': W_x, 'W_dt': W_dt, 'b_dt': b_dt, 'A_log': A_log, 'D': D, 'W_out': W_out}
    _L0_attn_all = _L0_attn_setup()
    _L0_attn_in = {k: v for k, v in _L0_attn_all.items() if k in ('W_in', 'conv_w', 'conv_b', 'W_x', 'W_dt', 'b_dt', 'A_log', 'D', 'W_out')}
    del _L0_attn_all

    def _L0_xattn_setup():
        import jax, jax.numpy as jnp
        import numpy as np
        H = 8
        C = 2

        def _autocorrelation(Q, K, V):
            B, L, D = Q.shape
            d = D // H
            q = Q.reshape(B, L, H, d).transpose(0, 2, 1, 3)
            k = K.reshape(B, L, H, d).transpose(0, 2, 1, 3)
            v = V.reshape(B, L, H, d).transpose(0, 2, 1, 3)
            qf = jnp.fft.fft(q, axis=2)
            kf = jnp.fft.fft(k, axis=2)
            corr = jnp.fft.ifft(qf * jnp.conj(kf), axis=2).real
            topk = int(C * np.log(L))
            w, idx = jax.lax.top_k(corr.transpose(0, 1, 3, 2), topk)
            w = jax.nn.softmax(w, axis=-1)
            pos = jnp.arange(L)[:, None]
            out = jnp.zeros_like(v)
            for i in range(topk):
                g = jnp.minimum(idx[:, :, None, :, i] + pos, L - 1)
                out = out + w[:, :, None, :, i] * jnp.take_along_axis(v, g, axis=2)
            return out.transpose(0, 2, 1, 3).reshape(B, L, D)
        key = jax.random.key(seed)
        k1, k2, k3 = jax.random.split(key, 3)
        B, L, D = (16, 64, 512)
        Q = jax.random.normal(k1, (B, L, D), dtype=jnp.float32)
        K = jax.random.normal(k2, (B, L, D), dtype=jnp.float32)
        V = jax.random.normal(k3, (B, L, D), dtype=jnp.float32)
        return {'Q': Q, 'K': K, 'V': V}
    _L0_xattn_all = _L0_xattn_setup()
    _L0_xattn_in = {k: v for k, v in _L0_xattn_all.items() if k in ()}
    del _L0_xattn_all

    def _L0_ffn_setup():
        import jax, jax.numpy as jnp
        import numpy as np
        GROUP_SIZE = 64
        RANK = 16
        ALPHA = 1.0

        def _dequant(qweight, scales, zeros):
            O, I = qweight.shape
            G = I // GROUP_SIZE
            q = qweight.astype(scales.dtype).reshape(O, G, GROUP_SIZE)
            w = (q - zeros[:, :, None]) * scales[:, :, None]
            return w.reshape(O, I)
        key = jax.random.key(seed)
        ks = jax.random.split(key, 7)
        B, S, D_in, D_out = (4, 256, 512, 512)
        n_groups = D_in // GROUP_SIZE
        x = jax.random.normal(ks[0], (B, S, D_in), dtype=jnp.float32)
        qweight = jax.random.randint(ks[1], (D_out, D_in), 0, 16, dtype=jnp.int32)
        scales = jax.random.uniform(ks[2], (D_out, n_groups), dtype=jnp.float32) * 0.02
        zeros = jax.random.uniform(ks[3], (D_out, n_groups), dtype=jnp.float32) * 16.0
        lora_A = jax.random.normal(ks[4], (RANK, D_in), dtype=jnp.float32) / np.sqrt(D_in)
        lora_B = jax.random.normal(ks[5], (D_out, RANK), dtype=jnp.float32) * 0.01
        bias = jax.random.normal(ks[6], (D_out,), dtype=jnp.float32) * 0.02
        return {'x': x, 'qweight': qweight, 'scales': scales, 'zeros': zeros, 'lora_A': lora_A, 'lora_B': lora_B, 'bias': bias}
    _L0_ffn_all = _L0_ffn_setup()
    _L0_ffn_in = {k: v for k, v in _L0_ffn_all.items() if k in ('qweight', 'scales', 'zeros', 'lora_A', 'lora_B', 'bias')}
    del _L0_ffn_all

    def _L1_attn_setup():
        import jax, jax.numpy as jnp
        import numpy as np
        DEPTH, DIM, DFF, VOCAB = (4, 64, 256, 512)
        EPS = 1e-05

        def layernorm(x, w, b):
            mu = jnp.mean(x, axis=-1, keepdims=True)
            var = jnp.mean((x - mu) ** 2, axis=-1, keepdims=True)
            return (x - mu) * jax.lax.rsqrt(var + EPS) * w + b

        def sconv(x, phazor_c, last_conv_c):
            B, L, D = x.shape
            r = jnp.abs(phazor_c)
            p = jnp.tanh(r) * jnp.exp(1j * jnp.angle(phazor_c))
            prog = p[None, :] ** jnp.arange(L, dtype=jnp.float32)[:, None]
            filt_fft = jnp.fft.fft(prog, n=2 * L, axis=0)
            x_fft = jnp.fft.fft(x.astype(jnp.complex64), n=2 * L, axis=1)
            conv = jnp.fft.ifft(filt_fft[None] * x_fft, axis=1)[:, :L]
            conv = conv + last_conv_c[None, None, :] * prog[None] * p[None, None, :]
            return conv.real.astype(x.dtype)

        def _forward(x, Win, bin, ln1_w, ln1_b, phz_re, phz_im, lc_re, lc_im, sc_lin, ln2_w, ln2_b, W1, b1, W2, b2, lnl_w, lnl_b, Wout, bout):
            h = jnp.einsum('blv,dv->bld', x, Win) + bin

            def body(h, p):
                l1w, l1b, pr, pi, lr, li, scl, l2w, l2b, w1, b1_, w2, b2_ = p
                y = jax.nn.silu(layernorm(h, l1w, l1b))
                y = sconv(y, pr + 1j * pi, lr + 1j * li)
                h = h + y * scl
                y = layernorm(h, l2w, l2b)
                y = jax.nn.silu(jnp.einsum('bld,fd->blf', y, w1) + b1_)
                y = jnp.einsum('blf,df->bld', y, w2) + b2_
                return (h + y, None)
            xs = (ln1_w, ln1_b, phz_re, phz_im, lc_re, lc_im, sc_lin, ln2_w, ln2_b, W1, b1, W2, b2)
            h, _ = jax.lax.scan(body, h, xs)
            h = layernorm(h, lnl_w, lnl_b)
            return jnp.einsum('bld,vd->blv', h, Wout) + bout
        key = jax.random.key(seed)
        ks = jax.random.split(key, 20)
        f32 = jnp.float32
        inp = {}
        inp['x'] = jax.random.normal(ks[0], (2, 512, VOCAB), dtype=f32)
        inp['Win'] = jax.random.normal(ks[1], (DIM, VOCAB), dtype=f32) * VOCAB ** (-0.5)
        inp['bin'] = jnp.zeros((DIM,), f32)
        inp['ln1_w'] = jnp.ones((DEPTH, DIM), f32)
        inp['ln1_b'] = jnp.zeros((DEPTH, DIM), f32)
        ang = 2 * np.pi * jnp.arange(DIM, dtype=f32) / DIM
        mag = jnp.abs(jax.random.normal(ks[2], (DEPTH, DIM), dtype=f32))
        inp['phz_re'] = mag * jnp.cos(ang)[None]
        inp['phz_im'] = mag * jnp.sin(ang)[None]
        inp['lc_re'] = jax.random.normal(ks[3], (DEPTH, DIM), dtype=f32)
        inp['lc_im'] = jax.random.normal(ks[4], (DEPTH, DIM), dtype=f32)
        inp['sc_lin'] = jnp.ones((DEPTH, DIM), f32)
        inp['ln2_w'] = jnp.ones((DEPTH, DIM), f32)
        inp['ln2_b'] = jnp.zeros((DEPTH, DIM), f32)
        inp['W1'] = jax.random.normal(ks[5], (DEPTH, DFF, DIM), dtype=f32) * DIM ** (-0.5)
        inp['b1'] = jnp.zeros((DEPTH, DFF), f32)
        inp['W2'] = jax.random.normal(ks[6], (DEPTH, DIM, DFF), dtype=f32) * DFF ** (-0.5)
        inp['b2'] = jnp.zeros((DEPTH, DIM), f32)
        inp['lnl_w'] = jnp.ones((DIM,), f32)
        inp['lnl_b'] = jnp.zeros((DIM,), f32)
        inp['Wout'] = jax.random.normal(ks[7], (VOCAB, DIM), dtype=f32) * DIM ** (-0.5)
        inp['bout'] = jnp.zeros((VOCAB,), f32)
        return inp
    _L1_attn_all = _L1_attn_setup()
    _L1_attn_in = {k: v for k, v in _L1_attn_all.items() if k in ('Win', 'bin', 'ln1_w', 'ln1_b', 'phz_re', 'phz_im', 'lc_re', 'lc_im', 'sc_lin', 'ln2_w', 'ln2_b', 'W1', 'b1', 'W2', 'b2', 'lnl_w', 'lnl_b', 'Wout', 'bout')}
    del _L1_attn_all

    def _L1_xattn_setup():
        import jax, jax.numpy as jnp
        import numpy as np
        HID = 512
        NHEAD = 32
        NKV = 8
        HDIM = 128
        G = NHEAD // NKV
        key = jax.random.key(seed)
        ks = jax.random.split(key, 6)
        s = 0.02
        B, L = (2, 256)
        return {'query': jax.random.normal(ks[0], (B, L, HID), jnp.float32), 'kv': jax.random.normal(ks[1], (B, L, HID), jnp.float32), 'Wq': jax.random.normal(ks[2], (HID, NHEAD * HDIM), jnp.float32) * s, 'bq': jnp.zeros((NHEAD * HDIM,), jnp.float32), 'Wkv': jax.random.normal(ks[3], (HID, 2 * NKV * HDIM), jnp.float32) * s, 'bkv': jnp.zeros((2 * NKV * HDIM,), jnp.float32), 'Wo': jax.random.normal(ks[4], (NHEAD * HDIM, HID), jnp.float32) * s, 'bo': jnp.zeros((HID,), jnp.float32)}
    _L1_xattn_all = _L1_xattn_setup()
    _L1_xattn_in = {k: v for k, v in _L1_xattn_all.items() if k in ('Wq', 'bq', 'Wkv', 'bkv', 'Wo', 'bo')}
    del _L1_xattn_all

    def _L1_ffn_setup():
        import jax, jax.numpy as jnp
        import numpy as np
        R = 16
        LORA_ALPHA = 16
        SCALING = LORA_ALPHA / R
        key = jax.random.key(seed)
        kx, kr, ka = jax.random.split(key, 3)
        B, S, D, DO, E = (4, 256, 512, 512, 8)
        x = jax.random.normal(kx, (B, S, D), dtype=jnp.float32)
        bound_r = 1.0 / np.sqrt(D)
        route_w = jax.random.uniform(kr, (E, D), jnp.float32, -bound_r, bound_r)
        bound_a = 1.0 / np.sqrt(D)
        A = jax.random.uniform(ka, (E, R, D), jnp.float32, -bound_a, bound_a)
        kb = jax.random.fold_in(key, 7)
        Bw = jax.random.normal(kb, (E, DO, R), dtype=jnp.float32) * 0.02
        return {'x': x, 'route_w': route_w, 'A': A, 'Bw': Bw}
    _L1_ffn_all = _L1_ffn_setup()
    _L1_ffn_in = {k: v for k, v in _L1_ffn_all.items() if k in ('route_w', 'A', 'Bw')}
    del _L1_ffn_all
    return {'x': x, 'ctx_4096': ctx_4096, 'L0_attn_W_in': _L0_attn_in['W_in'], 'L0_attn_conv_w': _L0_attn_in['conv_w'], 'L0_attn_conv_b': _L0_attn_in['conv_b'], 'L0_attn_W_x': _L0_attn_in['W_x'], 'L0_attn_W_dt': _L0_attn_in['W_dt'], 'L0_attn_b_dt': _L0_attn_in['b_dt'], 'L0_attn_A_log': _L0_attn_in['A_log'], 'L0_attn_D': _L0_attn_in['D'], 'L0_attn_W_out': _L0_attn_in['W_out'], 'L0_ffn_qweight': _L0_ffn_in['qweight'], 'L0_ffn_scales': _L0_ffn_in['scales'], 'L0_ffn_zeros': _L0_ffn_in['zeros'], 'L0_ffn_lora_A': _L0_ffn_in['lora_A'], 'L0_ffn_lora_B': _L0_ffn_in['lora_B'], 'L0_ffn_bias': _L0_ffn_in['bias'], 'L1_attn_Win': _L1_attn_in['Win'], 'L1_attn_bin': _L1_attn_in['bin'], 'L1_attn_ln1_w': _L1_attn_in['ln1_w'], 'L1_attn_ln1_b': _L1_attn_in['ln1_b'], 'L1_attn_phz_re': _L1_attn_in['phz_re'], 'L1_attn_phz_im': _L1_attn_in['phz_im'], 'L1_attn_lc_re': _L1_attn_in['lc_re'], 'L1_attn_lc_im': _L1_attn_in['lc_im'], 'L1_attn_sc_lin': _L1_attn_in['sc_lin'], 'L1_attn_ln2_w': _L1_attn_in['ln2_w'], 'L1_attn_ln2_b': _L1_attn_in['ln2_b'], 'L1_attn_W1': _L1_attn_in['W1'], 'L1_attn_b1': _L1_attn_in['b1'], 'L1_attn_W2': _L1_attn_in['W2'], 'L1_attn_b2': _L1_attn_in['b2'], 'L1_attn_lnl_w': _L1_attn_in['lnl_w'], 'L1_attn_lnl_b': _L1_attn_in['lnl_b'], 'L1_attn_Wout': _L1_attn_in['Wout'], 'L1_attn_bout': _L1_attn_in['bout'], 'L1_xattn_Wq': _L1_xattn_in['Wq'], 'L1_xattn_bq': _L1_xattn_in['bq'], 'L1_xattn_Wkv': _L1_xattn_in['Wkv'], 'L1_xattn_bkv': _L1_xattn_in['bkv'], 'L1_xattn_Wo': _L1_xattn_in['Wo'], 'L1_xattn_bo': _L1_xattn_in['bo'], 'L1_ffn_route_w': _L1_ffn_in['route_w'], 'L1_ffn_A': _L1_ffn_in['A'], 'L1_ffn_Bw': _L1_ffn_in['Bw']}

def reference(x, ctx_4096, L0_attn_W_in, L0_attn_conv_w, L0_attn_conv_b, L0_attn_W_x, L0_attn_W_dt, L0_attn_b_dt, L0_attn_A_log, L0_attn_D, L0_attn_W_out, L0_ffn_qweight, L0_ffn_scales, L0_ffn_zeros, L0_ffn_lora_A, L0_ffn_lora_B, L0_ffn_bias, L1_attn_Win, L1_attn_bin, L1_attn_ln1_w, L1_attn_ln1_b, L1_attn_phz_re, L1_attn_phz_im, L1_attn_lc_re, L1_attn_lc_im, L1_attn_sc_lin, L1_attn_ln2_w, L1_attn_ln2_b, L1_attn_W1, L1_attn_b1, L1_attn_W2, L1_attn_b2, L1_attn_lnl_w, L1_attn_lnl_b, L1_attn_Wout, L1_attn_bout, L1_xattn_Wq, L1_xattn_bq, L1_xattn_Wkv, L1_xattn_bkv, L1_xattn_Wo, L1_xattn_bo, L1_ffn_route_w, L1_ffn_A, L1_ffn_Bw):
    import jax
    import jax.numpy as jnp

    def _L0_attn_ref(hidden_states, W_in, conv_w, conv_b, W_x, W_dt, b_dt, A_log, D, W_out):
        import jax, jax.numpy as jnp
        import numpy as np
        H = 512
        D_IN = 1024
        N = 16
        K = 4
        R = 32
        EPS = 1e-06

        def rms_forward(x, eps=EPS):
            xf = x.astype(jnp.float32)
            var = jnp.mean(xf * xf, axis=-1, keepdims=True)
            return (xf * jax.lax.rsqrt(var + eps)).astype(x.dtype)
        b, L, _ = hidden_states.shape
        proj = hidden_states @ W_in.T
        x, gate = (proj[..., :D_IN], proj[..., D_IN:])
        xpad = jnp.pad(x, ((0, 0), (K - 1, 0), (0, 0)))
        xc = conv_b
        for j in range(K):
            xc = xc + conv_w[:, j] * xpad[:, j:j + L, :]
        x = jax.nn.silu(xc)
        ssm = x @ W_x.T
        ts, Bm, Cm = (ssm[..., :R], ssm[..., R:R + N], ssm[..., R + N:])
        ts = rms_forward(ts)
        Bm = rms_forward(Bm)
        Cm = rms_forward(Cm)
        dt = jax.nn.softplus(ts @ W_dt.T + b_dt)
        A = -jnp.exp(A_log.astype(jnp.float32))

        def step(state, inp):
            dt_t, B_t, C_t, u_t = inp
            dA = jnp.exp(dt_t[..., None] * A)
            state = state * dA + (dt_t * u_t)[..., None] * B_t[:, None, :]
            y = jnp.einsum('bdn,bn->bd', state, C_t)
            return (state, y)
        init = jnp.zeros((b, D_IN, N), dtype=jnp.float32)
        xs = (dt.transpose(1, 0, 2), Bm.transpose(1, 0, 2), Cm.transpose(1, 0, 2), x.transpose(1, 0, 2))
        _, ys = jax.lax.scan(step, init, xs)
        y = ys.transpose(1, 0, 2) + x * D
        y = y * jax.nn.silu(gate)
        return y @ W_out.T

    def _L0_xattn_ref(Q, K, V):
        import jax, jax.numpy as jnp
        import numpy as np
        H = 8
        C = 2

        def _autocorrelation(Q, K, V):
            B, L, D = Q.shape
            d = D // H
            q = Q.reshape(B, L, H, d).transpose(0, 2, 1, 3)
            k = K.reshape(B, L, H, d).transpose(0, 2, 1, 3)
            v = V.reshape(B, L, H, d).transpose(0, 2, 1, 3)
            qf = jnp.fft.fft(q, axis=2)
            kf = jnp.fft.fft(k, axis=2)
            corr = jnp.fft.ifft(qf * jnp.conj(kf), axis=2).real
            topk = int(C * np.log(L))
            w, idx = jax.lax.top_k(corr.transpose(0, 1, 3, 2), topk)
            w = jax.nn.softmax(w, axis=-1)
            pos = jnp.arange(L)[:, None]
            out = jnp.zeros_like(v)
            for i in range(topk):
                g = jnp.minimum(idx[:, :, None, :, i] + pos, L - 1)
                out = out + w[:, :, None, :, i] * jnp.take_along_axis(v, g, axis=2)
            return out.transpose(0, 2, 1, 3).reshape(B, L, D)
        return _autocorrelation(Q, K, V)

    def _L0_ffn_ref(x, qweight, scales, zeros, lora_A, lora_B, bias):
        import jax, jax.numpy as jnp
        import numpy as np
        GROUP_SIZE = 64
        RANK = 16
        ALPHA = 1.0

        def _dequant(qweight, scales, zeros):
            O, I = qweight.shape
            G = I // GROUP_SIZE
            q = qweight.astype(scales.dtype).reshape(O, G, GROUP_SIZE)
            w = (q - zeros[:, :, None]) * scales[:, :, None]
            return w.reshape(O, I)
        W = _dequant(qweight, scales, zeros)
        y = jnp.einsum('bsi,oi->bso', x, W)
        scaling = ALPHA / RANK
        lora = jnp.einsum('bsr,or->bso', jnp.einsum('bsi,ri->bsr', x, lora_A), lora_B)
        return y + scaling * lora + bias

    def _L1_attn_ref(x, Win, bin, ln1_w, ln1_b, phz_re, phz_im, lc_re, lc_im, sc_lin, ln2_w, ln2_b, W1, b1, W2, b2, lnl_w, lnl_b, Wout, bout):
        import jax, jax.numpy as jnp
        import numpy as np
        DEPTH, DIM, DFF, VOCAB = (4, 64, 256, 512)
        EPS = 1e-05

        def layernorm(x, w, b):
            mu = jnp.mean(x, axis=-1, keepdims=True)
            var = jnp.mean((x - mu) ** 2, axis=-1, keepdims=True)
            return (x - mu) * jax.lax.rsqrt(var + EPS) * w + b

        def sconv(x, phazor_c, last_conv_c):
            B, L, D = x.shape
            r = jnp.abs(phazor_c)
            p = jnp.tanh(r) * jnp.exp(1j * jnp.angle(phazor_c))
            prog = p[None, :] ** jnp.arange(L, dtype=jnp.float32)[:, None]
            filt_fft = jnp.fft.fft(prog, n=2 * L, axis=0)
            x_fft = jnp.fft.fft(x.astype(jnp.complex64), n=2 * L, axis=1)
            conv = jnp.fft.ifft(filt_fft[None] * x_fft, axis=1)[:, :L]
            conv = conv + last_conv_c[None, None, :] * prog[None] * p[None, None, :]
            return conv.real.astype(x.dtype)

        def _forward(x, Win, bin, ln1_w, ln1_b, phz_re, phz_im, lc_re, lc_im, sc_lin, ln2_w, ln2_b, W1, b1, W2, b2, lnl_w, lnl_b, Wout, bout):
            h = jnp.einsum('blv,dv->bld', x, Win) + bin

            def body(h, p):
                l1w, l1b, pr, pi, lr, li, scl, l2w, l2b, w1, b1_, w2, b2_ = p
                y = jax.nn.silu(layernorm(h, l1w, l1b))
                y = sconv(y, pr + 1j * pi, lr + 1j * li)
                h = h + y * scl
                y = layernorm(h, l2w, l2b)
                y = jax.nn.silu(jnp.einsum('bld,fd->blf', y, w1) + b1_)
                y = jnp.einsum('blf,df->bld', y, w2) + b2_
                return (h + y, None)
            xs = (ln1_w, ln1_b, phz_re, phz_im, lc_re, lc_im, sc_lin, ln2_w, ln2_b, W1, b1, W2, b2)
            h, _ = jax.lax.scan(body, h, xs)
            h = layernorm(h, lnl_w, lnl_b)
            return jnp.einsum('bld,vd->blv', h, Wout) + bout
        return _forward(x, Win, bin, ln1_w, ln1_b, phz_re, phz_im, lc_re, lc_im, sc_lin, ln2_w, ln2_b, W1, b1, W2, b2, lnl_w, lnl_b, Wout, bout)

    def _L1_xattn_ref(query, kv, Wq, bq, Wkv, bkv, Wo, bo):
        import jax, jax.numpy as jnp
        import numpy as np
        HID = 512
        NHEAD = 32
        NKV = 8
        HDIM = 128
        G = NHEAD // NKV
        B, L, _ = query.shape
        Lk = kv.shape[1]
        scale = jnp.asarray(1.0 / np.sqrt(HDIM), query.dtype)
        q = (query @ Wq + bq).reshape(B, L, NKV, G, HDIM)
        k_, v_ = jnp.split(kv @ Wkv + bkv, 2, axis=-1)
        k = k_.reshape(B, Lk, NKV, HDIM)
        v = v_.reshape(B, Lk, NKV, HDIM)
        scores = jnp.einsum('blkgd,bmkd->bkglm', q, k) * scale
        attn = jax.nn.softmax(scores, axis=-1)
        o = jnp.einsum('bkglm,bmkd->blkgd', attn, v).reshape(B, L, NHEAD * HDIM)
        return o @ Wo + bo

    def _L1_ffn_ref(x, route_w, A, Bw):
        import jax, jax.numpy as jnp
        import numpy as np
        R = 16
        LORA_ALPHA = 16
        SCALING = LORA_ALPHA / R
        logits = jnp.einsum('bsd,ed->bse', x, route_w)
        topk_v, topk_idx = jax.lax.top_k(logits, 1)
        E = logits.shape[-1]
        route_weight = jax.nn.one_hot(topk_idx[..., 0], E, dtype=logits.dtype) * topk_v
        h = jnp.einsum('bsd,erd->bser', x, A)
        wh = route_weight[..., None] * h
        out = jnp.einsum('bser,eor->bso', wh, Bw) * SCALING
        return out
    x = _layernorm(x + _L0_attn_ref(x, L0_attn_W_in, L0_attn_conv_w, L0_attn_conv_b, L0_attn_W_x, L0_attn_W_dt, L0_attn_b_dt, L0_attn_A_log, L0_attn_D, L0_attn_W_out), axis=-1)
    x = _layernorm(x + _L0_xattn_ref(x, ctx_4096, ctx_4096), axis=-1)
    x = _layernorm(x + _L0_ffn_ref(x, L0_ffn_qweight, L0_ffn_scales, L0_ffn_zeros, L0_ffn_lora_A, L0_ffn_lora_B, L0_ffn_bias), axis=-1)
    x = _layernorm(x + _L1_attn_ref(x, L1_attn_Win, L1_attn_bin, L1_attn_ln1_w, L1_attn_ln1_b, L1_attn_phz_re, L1_attn_phz_im, L1_attn_lc_re, L1_attn_lc_im, L1_attn_sc_lin, L1_attn_ln2_w, L1_attn_ln2_b, L1_attn_W1, L1_attn_b1, L1_attn_W2, L1_attn_b2, L1_attn_lnl_w, L1_attn_lnl_b, L1_attn_Wout, L1_attn_bout), axis=-1)
    x = _layernorm(x + _L1_xattn_ref(x, ctx_4096, L1_xattn_Wq, L1_xattn_bq, L1_xattn_Wkv, L1_xattn_bkv, L1_xattn_Wo, L1_xattn_bo), axis=-1)
    x = _layernorm(x + _L1_ffn_ref(x, L1_ffn_route_w, L1_ffn_A, L1_ffn_Bw), axis=-1)
    return x

_drawn_inputs = setup_inputs


def setup_inputs(seed=0):
    import zlib

    import numpy as np

    out = dict(_drawn_inputs(seed))
    spreads = {'L0_attn_D': (1.0, 0.6),
     'L1_attn_bin': (0.0, 0.1),
     'L1_attn_ln1_w': (1.0, 0.2),
     'L1_attn_ln1_b': (0.0, 0.1),
     'L1_attn_sc_lin': (1.0, 0.2),
     'L1_attn_ln2_w': (1.0, 0.2),
     'L1_attn_ln2_b': (0.0, 0.279),
     'L1_attn_b1': (0.0, 0.308),
     'L1_attn_b2': (0.0, 0.1),
     'L1_attn_lnl_w': (1.0, 0.2),
     'L1_attn_lnl_b': (0.0, 0.1),
     'L1_attn_bout': (0.0, 0.1),
     'L1_xattn_bq': (0.0, 0.8),
     'L1_xattn_bkv': (0.0, 0.1),
     'L1_xattn_bo': (0.0, 0.1)}
    factors = {'L0_attn_conv_b': 5.426,
     'L0_attn_W_dt': 8.0,
     'L0_attn_b_dt': 40.834,
     'L0_attn_A_log': 13.213,
     'L0_ffn_lora_A': 8.0,
     'L0_ffn_lora_B': 8.0,
     'L0_ffn_bias': 5.105}
    for name, (base, spread) in spreads.items():
        noise = np.random.default_rng([zlib.crc32(name.encode()), seed]).standard_normal(out[name].shape)
        drawn = base * np.exp(spread * noise) if base else spread * noise
        out[name] = jnp.asarray(drawn.astype(out[name].dtype))
    for name, factor in factors.items():
        out[name] = (out[name] * factor).astype(out[name].dtype)
    return out
```

```python
from contextlib import ExitStack

import numpy as np

import concourse.bass as bass
from concourse import mybir

F32 = mybir.dt.float32
I32 = mybir.dt.int32
U32 = mybir.dt.uint32
ALU = mybir.AluOpType
ACT = mybir.ActivationFunctionType
AX = mybir.AxisListType

P = 128
B = 8
L = 128
D = 512
KD = D // P
HB = B // 2
HT = HB * L
DI = 1024
MD = DI // P
NS = 16
NG = 2
GS = NS // NG
RK = 32
SSM = RK + 2 * NS
CV = 4
DEPTH, DIM, DFF = 4, 64, 256
NKV, GQ = 8, 4
TOPK = int(2 * np.log(L))
BIG = 3.0e38
SQ = float(1.0 / np.sqrt(128.0))

_COLS = [("convw", MD * CV), ("convb", MD), ("bdt", MD), ("alog", MD * NS), ("dskip", MD),
         ("bq", NKV * GQ), ("bk", NKV), ("bv", NKV), ("ln1w", DEPTH), ("ln1b", DEPTH),
         ("ln2w", DEPTH), ("ln2b", DEPTH), ("lnlw", 1), ("lnlb", 1), ("b1", DEPTH * 2),
         ("pre", DEPTH), ("pim", DEPTH), ("lre", DEPTH), ("lim", DEPTH), ("ident", P),
         ("twoI", DIM), ("iota8", 8)]
COL = {}
_at = 0
for _n, _w in _COLS:
    COL[_n] = (_at, _at + _w)
    _at += _w
NPAR = _at
_ROWS = [("fbias", D), ("bout", D), ("bo", D), ("bin", DIM), ("b2", DEPTH * DIM), ("scl", DEPTH * DIM)]
ROW = {}
_at = 0
for _n, _w in _ROWS:
    ROW[_n] = (_at, _at + _w)
    _at += _w
NROW = _at
FOUR = ["q", "k_swap", "c_re", "c_im", "w_re", "w_im", "v_re", "v_im", "o_rr", "o_ii", "o_ri", "o_ir"]


def fourier():
    n = np.arange(L)[:, None].astype(np.float64)
    m = {}
    f = np.arange(64)[None, :]
    re, im = np.cos(2 * np.pi * n * f / L), -np.sin(2 * np.pi * n * f / L)
    im[:, 0] = np.cos(np.pi * n[:, 0])
    m["q"] = np.concatenate([re, im], 1)
    m["k_swap"] = np.concatenate([im, re], 1)
    t = np.arange(L)[None, :]
    fc = np.arange(64)[:, None]
    w = np.where(fc == 0, 1.0, 2.0) / L
    cos, sin = w * np.cos(2 * np.pi * fc * t / L), w * np.sin(2 * np.pi * fc * t / L)
    lower = cos.copy()
    lower[0] = np.cos(np.pi * t[0]) / L
    m["c_re"] = np.concatenate([cos, lower], 0)
    m["c_im"] = np.concatenate([sin * (fc > 0), -sin * (fc > 0)], 0)
    f = np.arange(128)[None, :]
    re, im = np.cos(np.pi * n * f / L), -np.sin(np.pi * n * f / L)
    im[:, 0] = np.cos(np.pi * n[:, 0])
    m["w_re"], m["w_im"] = re, im
    s = np.arange(2 * L)[:, None].astype(np.float64)
    re, im = np.cos(np.pi * s * f / L), -np.sin(np.pi * s * f / L)
    im[:, 0] = np.cos(np.pi * s[:, 0])
    for name, full in (("v_re", re), ("v_im", im)):
        fold = full[:L].copy()
        fold[L - 1] += full[L:].sum(0)
        m[name] = fold
    fc = np.arange(128)[:, None]
    w = np.where(fc == 0, 1.0, 2.0) / (2 * L)
    cos, sin = w * np.cos(np.pi * fc * t / L), w * np.sin(np.pi * fc * t / L)
    ii = cos.copy()
    ii[0] = np.cos(np.pi * t[0]) / (2 * L)
    m["o_rr"], m["o_ii"] = cos, ii
    m["o_ri"], m["o_ir"] = -sin * (fc > 0), sin * (fc > 0)
    return np.ascontiguousarray(np.stack([m[k] for k in FOUR], 1).astype(np.float32))


def decoder_kernel(nc, xT, xtok, ctxT, ctxtok, par, rows, four, win, wx, wdt, wout, qw, sc, ze,
                   loraA, loraBT, dwin, dw1, dw2, dwout, wq, wk, wv, wo, ra, bwT, out):
    scratch = nc.dram_tensor("bc_scratch", [2, 2 * NS, HT], F32, kind="Internal").ap()
    with ExitStack() as ctx:
        def sb(name, shape, dt=F32):
            return ctx.enter_context(nc.sbuf_tensor(name, shape, dt))

        names = {}

        def sem(name):
            names[name] = ctx.enter_context(nc.semaphore(name))
            return names[name]

        KB = 256
        arena = sb("arena", [P, 172 * KB])

        def part(at, size, parts=P):
            return arena[0:parts, int(at * KB):int(at * KB) + size]

        x_tok = sb("x_tok", [P, B, D])
        prm = sb("prm", [P, NPAR])
        row = sb("row", [P, NROW])
        amat = sb("amat", [P, MD * NS])
        lnst = sb("lnst", [P, B, 6])
        lnmv = sb("lnmv", [P, B, 2])
        lnve = sb("lnve", [P, B])
        lnrs = sb("lnrs", [P, B])
        halfneg = sb("halfneg", [P, 16])

        def pc(name):
            a, b = COL[name]
            return prm[:, a:b]

        def rw(name):
            a, b = ROW[name]
            return row[:, a:b]

        ident = pc("ident")
        psum = ctx.enter_context(nc.psum_tensor("psum", [P, 8 * 512], F32))
        bank = [psum[:, i * 512:(i + 1) * 512] for i in range(8)]

        xTh = part(0, KD * HT).rearrange("p (k n) -> p k n", k=KD)
        wring = part(8, 4 * 512).rearrange("p (s n) -> p s n", s=4)
        xpad = part(16, 2 * HB * (L + CV - 1)).rearrange("p (s b n) -> p s b n", s=2, b=HB)
        conv = part(21, 2 * HT).rearrange("p (s n) -> p s n", s=2)
        ssmsq = part(26, HB * SSM)
        ssmn = part(27, HB * SSM).rearrange("p (b c) -> p b c", b=HB)
        ssm_ss = part(28, 64)
        ssm_ms = part(28.5, 16)
        ssm_rs = part(28.75, 16)
        Brep = part(0, NS * HT).rearrange("p (n t) -> p n t", n=NS)
        Crep = part(32, NS * HT).rearrange("p (n t) -> p n t", n=NS)
        dA = psum[:, 0:2 * NG * HT].rearrange("p (s n t) -> p s n t", s=2, n=NG)
        state = psum[:, 2 * NG * HT:3 * NG * HT]
        bu = part(80, 2 * NG * HT).rearrange("p (s n t) -> p s n t", s=2, n=NG)
        prod = part(88, 2 * NG * HT).rearrange("p (s n t) -> p s n t", s=2, n=NG)
        sp_w = part(64, MD * HT).rearrange("p (m t) -> p m t", m=MD)
        sp_r = part(96, MD * HT).rearrange("p (m t) -> p m t", m=MD)
        u = part(112, MD * HT).rearrange("p (m t) -> p m t", m=MD)
        dt = part(128, MD * HT).rearrange("p (m t) -> p m t", m=MD)
        g = part(144, MD * HT).rearrange("p (m t) -> p m t", m=MD)
        wout_sb = dt
        wx_sb = part(160, MD * SSM).rearrange("p (k o) -> p k o", k=MD)
        wdt_sb = part(162, DI, RK)
        dtu = part(166, 2 * HT).rearrange("p (s n) -> p s n", s=2)
        ytmp = part(170, HT)
        ssmT = sb("ssmT", [SSM, HT])
        ctx_sb = part(0, B * D).rearrange("p (b d) -> p b d", b=B)
        four_sb = part(16, len(FOUR) * P).rearrange("p (i n) -> p i n", i=len(FOUR))
        fm = {k: four_sb[:, i, :] for i, k in enumerate(FOUR)}
        qf = part(22, D)
        m12 = part(24, 2 * D).rearrange("p (i n) -> p i n", i=2)
        es = part(28, D)
        ee = part(30, D)
        rep1 = part(32, D)
        rep2 = part(34, D)
        wn = part(36, 2 * D).rearrange("p (s n) -> p s n", s=2)
        wT = part(40, D)
        vri = part(42, 2 * D).rearrange("p (i n) -> p i n", i=2)
        m4 = part(46, 4 * D).rearrange("p (i n) -> p i n", i=4)
        mx8 = part(54, 4 * 8)
        nx8 = part(54.25, 4 * 8)
        m9 = part(54.5, 4 * 8)
        wsum = part(54.75, 8)
        winv = part(55, 8)
        ctxT_sb = part(64, KD * B * L).rearrange("p (k n) -> p k n", k=KD)
        sz = part(80, 2 * KD * D).rearrange("p (i k n) -> p i k n", i=2, k=KD)
        weff = part(96, KD * D).rearrange("p (k n) -> p k n", k=KD)
        qw_sb = sb("qw_sb", [P, 1, D], I32)
        lora = part(104, 2 * D, 16).rearrange("p (i n) -> p i n", i=2)
        x2T = part(112, KD * B * L).rearrange("p (k n) -> p k n", k=KD)
        rtab = part(128, DEPTH * HT).rearrange("p (l t) -> p l t", l=DEPTH)
        ctab = part(136, DEPTH * (L + 1)).rearrange("p (l t) -> p l t", l=DEPTH)
        stab = part(138.25, DEPTH * (L + 1)).rearrange("p (l t) -> p l t", l=DEPTH)
        ttmp = part(140.5, DEPTH * P).rearrange("p (l t) -> p l t", l=DEPTH)
        tsm = sb("tsm", [P, 12, DEPTH])
        dh = part(144, B * DIM).rearrange("p (b c) -> p b c", b=B)
        dhc = part(146, B * DIM).rearrange("p (b c) -> p b c", b=B)
        dyn = part(148, 2 * HB * P).rearrange("p (h b c) -> p h b c", h=2, b=HB)
        dys = part(152, 2 * HT).rearrange("p (h t) -> p h t", h=2)
        dz = part(156, 2 * HT).rearrange("p (h t) -> p h t", h=2)
        df = part(160, 2 * 2 * HT).rearrange("p (h k t) -> p h k t", h=2, k=2)
        dw1_sb = part(168, DEPTH * DFF, DIM).rearrange("p (l f) -> p l f", l=DEPTH)
        dw2_sb = part(104, DEPTH * 2 * DIM).rearrange("p (l k o) -> p l k o", l=DEPTH, k=2)
        dwin_sb = part(106, KD * DIM).rearrange("p (k o) -> p k o", k=KD)
        dwout_sb = part(107, D, DIM)
        dsc = part(109, DEPTH * DIM).rearrange("p (l o) -> p l o", l=DEPTH)
        dst = sb("dst", [P, B, 6])
        dmv = sb("dmv", [P, B, 2])
        dve_ = sb("dve_", [P, B])
        drs = sb("drs", [P, B])
        KT = part(0, NKV * B * L).rearrange("p (g n) -> p g n", g=NKV)
        V = part(32, B * NKV * P).rearrange("p (b n) -> p b n", b=B)
        wk_sb = part(32, 2 * 512).rearrange("p (s n) -> p s n", s=2)
        wv_sb = part(80, KD * 1024).rearrange("p (k n) -> p k n", k=KD)
        qT = part(80, 2 * GQ * HT).rearrange("p (s j n) -> p s j n", s=2, j=GQ)
        oT = part(96, 2 * GQ * HT).rearrange("p (s j n) -> p s j n", s=2, j=GQ)
        wq_sb = part(128, 2 * GQ * 512).rearrange("p (s n) -> p s n", s=2)
        wo_sb = part(144, 2 * GQ * D).rearrange("p (s j n) -> p s j n", s=2, j=GQ)
        pe_ = part(160, 2 * 512).rearrange("p (s n) -> p s n", s=2)
        pn = part(164, 512)
        pT = part(166, 2 * 512).rearrange("p (s n) -> p s n", s=2)
        amax = sb("amax", [P, 4])
        asum = sb("asum", [P, 2, 4])
        ainv = sb("ainv", [P, 4])
        ra_sb = part(0, KD * 136).rearrange("p (k n) -> p k n", k=KD)
        bw_sb = part(3, D)
        logits = part(6, 8)
        rt8 = part(6.25, 8)
        ri8 = sb("ri8", [P, 8], U32)
        rif = part(6.5, 8)
        rwt = part(6.75, 8)
        wh = part(7, P)
        whT = part(8, P)

        ls = {n: sem(n) for n in (
            "par_in", "row_in", "xtok_in", "wx_in", "xT_in", "w_in0", "w_in1", "w_in2", "w_in3",
            "bc_out", "b_in0", "b_in1", "b_in2", "b_in3", "c_in0", "c_in1", "c_in2", "c_in3", "wout_in",
            "ctxtok_in", "four_in", "ctxT_in", "sz_in", "qw_in", "lora_in", "dwt_in", "wk_in0", "wk_in1",
            "wv_in", "wq_in0", "wq_in1", "wo_in0", "wo_in1", "ra_in", "stored",
            "dve_chain", "act_chain", "pool_chain",
            "pad_zero", "dA_zero", "amat_done", "deq_done",
            "inproj", "in_evac", "conv_done", "u_done", "ssm_done", "ssm_sq", "ssm_ve", "ssm_rs", "ssm_norm",
            "ssmT_done", "ssmT_sb", "dt_proj", "dt_abs", "dt_exp", "dt_relu", "dt_w0", "dt_w", "dt_ln",
            "dt_done", "dtu_done", "dA_done", "bu_done", "scan_done", "prod_done", "ysum", "y_done",
            "wout_done",
            "x_sum", "ln_ve", "ln_rs", "x_done",
            "kf_done", "qf_done", "qf_sb", "m12_done", "corr", "es_done", "corr_read", "ee_done", "wn_done",
            "vf_done", "vri_sb", "wT_done", "wT_sb", "wf_done", "m4_done", "xat_done",
            "lora_done", "weff_done", "xTt", "xT_sb", "xbias", "ffn_done",
            "tab_a", "tab_b", "tab_c", "tab_d", "tab_done",
            "h0_done", "h0_read", "d_ve", "d_rs", "d_yn", "d_tr", "d_ys", "d_z", "d_conv", "d_hread", "d_yT",
            "d_f1", "d_f", "d_f2", "d_f2read", "d_out",
            "kv_ps", "kv_sb", "q_ps", "q_sb", "s_ps", "s_read", "p_es", "p_exp", "p_norm", "t_ps", "t_sb",
            "av_ps", "o_sb", "op_ps",
            "r_ps", "r_wh", "wh_ps", "whT_done", "rf_ps",
        )}
        S = type("S", (), ls)

        block = ctx.enter_context(nc.Block())

        def lnc(stage, b):
            return stage * B + b + 1

        @block.sync
        def _(sp):
            def load(dst, src, s):
                sp.dma_start(dst, src).then_inc(s, 16)

            load(prm[:, :], par, S.par_in)
            for h in range(2):
                if h:
                    sp.wait_ge(S.y_done, MD)
                load(xTh, xT[h], S.xT_in)
                for m in range(16):
                    i = h * 16 + m
                    if m >= 4:
                        sp.wait_ge(S.inproj, i - 3)
                    load(wring[:, i % 4, :], win[m], (S.w_in0, S.w_in1, S.w_in2, S.w_in3)[i % 4])
                    if i == 1:
                        load(wx_sb, wx, S.wx_in)
                        load(wdt_sb, wdt, S.wx_in)
                        load(row[:, :], rows.partition_broadcast(P), S.row_in)
                        load(x_tok[:, :, :], xtok, S.xtok_in)
                sp.wait_ge(S.ssmT_sb, h + 1)
                sp.dma_start(scratch[h], ssmT[RK:SSM, :]).then_inc(S.bc_out, 16)
                sp.wait_ge(S.bc_out, 16 * (h + 1))
                for q in range(4):
                    for c, (dst, s) in enumerate(((Brep, (S.b_in0, S.b_in1, S.b_in2, S.b_in3)),
                                                  (Crep, (S.c_in0, S.c_in1, S.c_in2, S.c_in3)))):
                        src = scratch[h, c * NS + q * 4:c * NS + (q + 1) * 4, :]
                        load(dst[:, q * 4:(q + 1) * 4, :].rearrange("p n t -> p (n t)"),
                             src.rearrange("n t -> (n t)").partition_broadcast(P), s[q])
                for m in range(MD):
                    sp.wait_ge(S.y_done, h * MD + m + 1)
                    load(wout_sb[:, m, :], wout[m], S.wout_in)
            load(ctx_sb, ctxtok, S.ctxtok_in)
            load(four_sb, four, S.four_in)
            for i, t in enumerate((sc, ze)):
                for half in range(2):
                    load(sz[64 * half:64 * half + 64, i, :, :], t[half].partition_broadcast(64), S.sz_in)
            load(lora[:, 0, :], loraA, S.lora_in)
            load(lora[:, 1, :], loraBT, S.lora_in)
            load(ctxT_sb, ctxT, S.ctxT_in)
            for k in range(KD):
                if k:
                    sp.wait_ge(S.deq_done, k)
                load(qw_sb[:, 0, :], qw[k], S.qw_in)
            sp.wait_ge(S.weff_done, KD)
            load(dw2_sb, dw2, S.dwt_in)
            load(dwin_sb, dwin, S.dwt_in)
            load(dwout_sb, dwout, S.dwt_in)
            load(dw1_sb, dw1, S.dwt_in)
            load(wv_sb, wv, S.wv_in)
            for i in range(NKV):
                if i >= 2:
                    sp.wait_ge(S.kv_ps, 2 * (i - 1))
                load(wk_sb[:, i % 2, :], wk[i], (S.wk_in0, S.wk_in1)[i % 2])
            sp.wait_ge(S.d_out, 2 * HB)
            for i in range(-1, 2 * NKV):
                if i + 1 < 2 * NKV:
                    if i >= 1:
                        sp.wait_ge(S.q_ps, i * GQ)
                    load(wq_sb[:, (i + 1) % 2, :], wq[(i + 1) % NKV], (S.wq_in0, S.wq_in1)[(i + 1) % 2])
                if i >= 0:
                    if i >= 2:
                        sp.wait_ge(S.op_ps, (i - 1) * HB)
                    load(wo_sb[:, i % 2, :, :], wo[i % NKV], (S.wo_in0, S.wo_in1)[i % 2])
            sp.wait_ge(S.s_ps, 2 * NKV * HB)
            load(ra_sb, ra, S.ra_in)
            load(bw_sb, bwT, S.ra_in)
            for b in range(B):
                sp.wait_ge(S.x_done, lnc(5, b))
                sp.dma_start(out[b], x_tok[:, b, :]).then_inc(S.stored, 16)
            sp.wait_ge(S.stored, 16 * B)

        @block.tensor
        def _(pe):
            mm = nc.tensor.matmul

            for h in range(2):
                for m in range(16):
                    i = h * 16 + m
                    if m == 0:
                        pe.wait_ge(S.xT_in, 16 * (h + 1))
                    pe.wait_ge((S.w_in0, S.w_in1, S.w_in2, S.w_in3)[i % 4], 16 * (i // 4 + 1))
                    if i >= 2:
                        pe.wait_ge(S.in_evac, i - 1)
                    if h and m == 0:
                        pe.wait_ge(S.x_sum, lnc(0, HB - 1))
                    for k in range(KD):
                        last = mm(bank[m % 2][:, :], wring[:, i % 4, k * P:(k + 1) * P], xTh[:, k, :],
                                  start=(k == 0), stop=(k == KD - 1))
                    last.then_inc(S.inproj, 1)
                pe.wait_ge(S.u_done, MD * (h + 1))
                pe.wait_ge(S.wx_in, 32)
                for b in range(HB):
                    for k in range(MD):
                        last = mm(bank[2][:, b * SSM:(b + 1) * SSM], u[:, k, b * L:(b + 1) * L], wx_sb[:, k, :],
                                  start=(k == 0), stop=(k == MD - 1))
                last.then_inc(S.ssm_done, 1)
                pe.wait_ge(S.ssm_norm, h + 1)
                for b in range(HB):
                    last = nc.tensor.transpose(bank[3][0:SSM, b * L:(b + 1) * L], ssmn[:, b, :], ident)
                last.then_inc(S.ssmT_done, 1)
                pe.wait_ge(S.ssmT_sb, h + 1)
                for m in range(MD):
                    i = h * MD + m
                    if m >= 2:
                        pe.wait_ge(S.dt_relu, i - 1)
                    last = mm(bank[4 + m % 2][:, :], wdt_sb[:, m * P:(m + 1) * P], ssmT[0:RK, :],
                              start=True, stop=True)
                    last.then_inc(S.dt_proj, 1)
                for m in range(MD):
                    if h * MD + m >= 2:
                        pe.wait_ge(S.y_done, h * MD + m - 1)
                    for q in range(GS):
                        i = (h * MD + m) * GS + q
                        pe.wait_ge(S.prod_done, i + 1)
                        for n in range(NG):
                            last = mm(bank[6 + m % 2][:, :], ident, prod[:, i % 2, n, :],
                                      start=(q == 0 and n == 0), stop=(q == GS - 1 and n == NG - 1))
                        last.then_inc(S.ysum, 1)
                pe.wait_ge(S.y_done, MD * (h + 1))
                pe.wait_ge(S.wout_in, 16 * MD * (h + 1))
                for b in range(HB):
                    if b >= 2:
                        pe.wait_ge(S.x_sum, lnc(0, h * HB + b - 2))
                    for k in range(MD):
                        last = mm(bank[b % 2][:, :], g[:, k, b * L:(b + 1) * L], wout_sb[:, k, :],
                                  start=(k == 0), stop=(k == MD - 1))
                    last.then_inc(S.wout_done, 1)

            def correlate(b):
                pe.wait_ge(S.ctxtok_in, 16)
                pe.wait_ge(S.four_in, 16)
                if b == 0:
                    pe.wait_ge(S.x_sum, lnc(0, B - 1))
                    pe.wait_ge(S.y_done, 2 * MD)
                if b >= 1:
                    pe.wait_ge(S.m12_done, b)
                mm(bank[1][:, :], fm["q"], ctx_sb[:, b, :], start=True, stop=True)
                mm(bank[2][:, :], fm["k_swap"], ctx_sb[:, b, :], start=True, stop=True).then_inc(S.kf_done, 1)
                pe.wait_ge(S.x_done, lnc(0, b))
                mm(bank[0][:, :], fm["q"], x_tok[:, b, :], start=True, stop=True).then_inc(S.qf_done, 1)
                pe.wait_ge(S.m12_done, b + 1)
                if b >= 1:
                    pe.wait_ge(S.corr_read, b)
                for t in range(KD):
                    o = bank[3][:, t * P:(t + 1) * P]
                    mm(o, m12[:, 0, t * P:(t + 1) * P], fm["c_re"], start=True, stop=False)
                    last = mm(o, m12[:, 1, t * P:(t + 1) * P], fm["c_im"], start=False, stop=True)
                last.then_inc(S.corr, 1)

            def aggregate(b):
                if b >= 1:
                    pe.wait_ge(S.m4_done, b)
                mm(bank[5][:, :], fm["v_re"], ctx_sb[:, b, :], start=True, stop=True)
                mm(bank[6][:, :], fm["v_im"], ctx_sb[:, b, :], start=True, stop=True).then_inc(S.vf_done, 1)
                pe.wait_ge(S.wn_done, b + 1)
                for t in range(KD):
                    last = nc.tensor.transpose(bank[4][:, t * P:(t + 1) * P], wn[:, b % 2, t * P:(t + 1) * P], ident)
                last.then_inc(S.wT_done, 1)
                pe.wait_ge(S.vri_sb, b + 1)
                pe.wait_ge(S.wT_sb, b + 1)
                mm(bank[5][:, :], fm["w_re"], wT, start=True, stop=True)
                mm(bank[6][:, :], fm["w_im"], wT, start=True, stop=True).then_inc(S.wf_done, 1)
                pe.wait_ge(S.m4_done, b + 1)
                if b >= 1:
                    pe.wait_ge(S.x_sum, lnc(1, b - 1))
                for i, k in enumerate(("o_rr", "o_ii", "o_ri", "o_ir")):
                    last = mm(bank[7][:, :], fm[k], m4[:, i, :], start=(i == 0), stop=(i == 3))
                last.then_inc(S.xat_done, 1)

            correlate(0)
            for b in range(B):
                if b + 1 < B:
                    correlate(b + 1)
                aggregate(b)

            def turn(stage, b, n, bk):
                pe.wait_ge(S.x_done, lnc(stage, b))
                if n >= 2:
                    pe.wait_ge(S.xT_sb, n - 1)
                for k in range(KD):
                    last = nc.tensor.transpose(bank[bk][:, k * P:(k + 1) * P], x_tok[:, b, k * P:(k + 1) * P], ident)
                last.then_inc(S.xTt, 1)

            pe.wait_ge(S.lora_in, 32)
            for k in range(KD):
                if k >= 1:
                    pe.wait_ge(S.weff_done, k)
                mm(bank[4][:, :], lora[:, 0, k * P:(k + 1) * P], lora[:, 1, :], start=True, stop=True).then_inc(S.lora_done, 1)
            turn(1, 0, 0, 0)
            for b in range(B):
                if b + 1 < B:
                    turn(1, b + 1, b + 1, (b + 1) % 2)
                pe.wait_ge(S.xT_sb, b + 1)
                pe.wait_ge(S.weff_done, KD)
                if b >= 2:
                    pe.wait_ge(S.x_sum, lnc(2, b - 2))
                for k in range(KD):
                    last = mm(bank[2 + b % 2][:, :], x2T[:, k, b * L:(b + 1) * L], weff[:, k, :],
                              start=(k == 0), stop=(k == KD - 1))
                last.then_inc(S.ffn_done, 1)

            turn(2, 0, B, 0)
            for b in range(B):
                if b + 1 < B:
                    turn(2, b + 1, B + b + 1, (b + 1) % 2)
                pe.wait_ge(S.xT_sb, B + b + 1)
                pe.wait_ge(S.dwt_in, 64)
                if b == 0:
                    pe.wait_ge(S.x_sum, lnc(2, B - 1))
                for k in range(KD):
                    last = mm(bank[4 + b // HB][:, (b % HB) * DIM:(b % HB + 1) * DIM],
                              x2T[:, k, b * L:(b + 1) * L], dwin_sb[:, k, :], start=(k == 0), stop=(k == KD - 1))
                if b % HB == HB - 1:
                    last.then_inc(S.h0_done, 1)
            pe.wait_ge(S.h0_read, 2)
            pe.wait_ge(S.tab_done, 1)
            for l in range(DEPTH):
                for h in range(2):
                    pe.wait_ge(S.d_yn, 4 * l + h + 1)
                    for b in range(HB):
                        last = nc.tensor.transpose(bank[4 * h][:, b * L:(b + 1) * L], dyn[:, h, b, :], ident)
                    last.then_inc(S.d_tr, 1)
                for h in range(2):
                    pe.wait_ge(S.d_z, 2 * l + h + 1)
                    for b in range(HB):
                        last = mm(bank[4 * h + 1][:, b * DIM:(b + 1) * DIM], dz[:, h, b * L:(b + 1) * L], dsc[:, l, :],
                                  start=True, stop=True)
                    last.then_inc(S.d_conv, 1)
                for h in range(2):
                    pe.wait_ge(S.d_yn, 4 * l + 2 + h + 1)
                    for b in range(HB):
                        last = nc.tensor.transpose(bank[4 * h][0:DIM, b * L:(b + 1) * L], dyn[:, h, b, 0:DIM], ident)
                    last.then_inc(S.d_tr, 1)
                for h in range(2):
                    pe.wait_ge(S.d_yT, 2 * l + h + 1)
                    for k in range(2):
                        last = mm(bank[4 * h + 2 + k][:, :], dw1_sb[:, l, k * P:(k + 1) * P], dys[0:DIM, h, :],
                                  start=True, stop=True)
                    last.then_inc(S.d_f1, 1)
                for h in range(2):
                    pe.wait_ge(S.d_f, 2 * l + h + 1)
                    for b in range(HB):
                        for k in range(2):
                            last = mm(bank[4 * h + 1][:, b * DIM:(b + 1) * DIM], df[:, h, k, b * L:(b + 1) * L],
                                      dw2_sb[:, l, k, :], start=(k == 0), stop=(k == 1))
                    last.then_inc(S.d_f2, 1)
            for h in range(2):
                pe.wait_ge(S.d_yn, 4 * DEPTH + h + 1)
                for b in range(HB):
                    last = nc.tensor.transpose(bank[4 * h][0:DIM, b * L:(b + 1) * L], dyn[:, h, b, 0:DIM], ident)
                last.then_inc(S.d_tr, 1)
            for b in range(B):
                if b % HB == 0:
                    pe.wait_ge(S.d_yT, 2 * DEPTH + b // HB + 1)
                if b >= 2:
                    pe.wait_ge(S.x_sum, lnc(3, b - 2))
                mm(bank[2 + b % 2][:, :], dys[0:DIM, b // HB, (b % HB) * L:(b % HB + 1) * L], dwout_sb,
                   start=True, stop=True).then_inc(S.d_out, 1)

            pe.wait_ge(S.x_sum, lnc(3, B - 1))
            pe.wait_ge(S.ctxT_in, 16)
            n = 0
            for gi in range(NKV):
                pe.wait_ge((S.wk_in0, S.wk_in1)[gi % 2], 16 * (gi // 2 + 1))
                for h in range(2):
                    if n >= 2:
                        pe.wait_ge(S.kv_sb, n - 1)
                    for k in range(KD):
                        last = mm(bank[2 + n % 2][:, :], wk_sb[:, gi % 2, k * P:(k + 1) * P],
                                  ctxT_sb[:, k, h * HT:(h + 1) * HT], start=(k == 0), stop=(k == KD - 1))
                    last.then_inc(S.kv_ps, 1)
                    n += 1
            pe.wait_ge(S.wv_in, 16)
            for b in range(B):
                for c in range(2):
                    pe.wait_ge(S.kv_sb, n - 1)
                    for k in range(KD):
                        last = mm(bank[2 + n % 2][:, :], ctxT_sb[:, k, b * L:(b + 1) * L],
                                  wv_sb[:, k, c * 512:(c + 1) * 512], start=(k == 0), stop=(k == KD - 1))
                    last.then_inc(S.kv_ps, 1)
                    n += 1
            turn(3, 0, 2 * B, 0)
            for b in range(1, B):
                turn(3, b, 2 * B + b, b % 2)
            pe.wait_ge(S.xT_sb, 3 * B)
            pe.wait_ge(S.kv_sb, n)
            NU = 2 * NKV

            def query(v, j):
                if v >= NU:
                    return
                pe.wait_ge((S.wq_in0, S.wq_in1)[v % 2], 16 * (v // 2 + 1))
                if v * GQ + j >= 1:
                    pe.wait_ge(S.q_sb, v * GQ + j)
                for k in range(KD):
                    last = mm(bank[0][:, :], wq_sb[:, v % 2, (j * KD + k) * P:(j * KD + k + 1) * P],
                              x2T[:, k, (v // NKV) * HT:(v // NKV + 1) * HT], start=(k == 0), stop=(k == KD - 1))
                last.then_inc(S.q_ps, 1)

            for j in range(GQ):
                query(0, j)
            for s in range(NU * HB + 4):
                v, b = s // HB, s % HB
                if s < NU * HB:
                    pe.wait_ge(S.q_sb, (v + 1) * GQ)
                    if s >= 1:
                        pe.wait_ge(S.p_es, s)
                    gb = (v // NKV) * HB + b
                    for j in range(GQ):
                        last = mm(bank[1][:, j * P:(j + 1) * P], qT[:, v % 2, j, b * L:(b + 1) * L],
                                  KT[:, v % NKV, gb * L:(gb + 1) * L], start=True, stop=True)
                    last.then_inc(S.s_ps, 1)
                    query(v + 1, b)
                if 1 <= s <= NU * HB:
                    pe.wait_ge(S.p_norm, s)
                    if s >= 2:
                        pe.wait_ge(S.t_sb, s - 1)
                    for j in range(GQ):
                        last = nc.tensor.transpose(bank[2][:, j * P:(j + 1) * P], pn[:, j * P:(j + 1) * P], ident)
                    last.then_inc(S.t_ps, 1)
                if 2 <= s <= NU * HB + 1:
                    r = s - 2
                    rv, rb = r // HB, r % HB
                    pe.wait_ge(S.t_sb, r + 1)
                    if r >= 1:
                        pe.wait_ge(S.o_sb, r)
                    mm(bank[3][:, :], V[:, (rv // NKV) * HB + rb, (rv % NKV) * P:(rv % NKV + 1) * P], pT[:, r % 2, :],
                       start=True, stop=True).then_inc(S.av_ps, 1)
                if s >= 4:
                    r = s - 4
                    rv, rb = r // HB, r % HB
                    pe.wait_ge(S.o_sb, r + 1)
                    pe.wait_ge((S.wo_in0, S.wo_in1)[rv % 2], 16 * (rv // 2 + 1))
                    if rv == NKV:
                        pe.wait_ge(S.x_sum, lnc(4, rb))
                    for j in range(GQ):
                        last = mm(bank[4 + rb][:, :], oT[:, rv % 2, j, rb * L:(rb + 1) * L], wo_sb[:, rv % 2, j, :],
                                  start=(rv % NKV == 0 and j == 0), stop=(rv % NKV == NKV - 1 and j == GQ - 1))
                    last.then_inc(S.op_ps, 1)

            pe.wait_ge(S.ra_in, 32)
            turn(4, 0, 3 * B, 0)
            for b in range(B):
                if b + 1 < B:
                    turn(4, b + 1, 3 * B + b + 1, (b + 1) % 2)
                pe.wait_ge(S.xT_sb, 3 * B + b + 1)
                if b >= 1:
                    pe.wait_ge(S.r_wh, b)
                for k in range(KD):
                    last = mm(bank[2][:, 0:136], x2T[:, k, b * L:(b + 1) * L], ra_sb[:, k, :],
                              start=(k == 0), stop=(k == KD - 1))
                last.then_inc(S.r_ps, 1)
                pe.wait_ge(S.r_wh, b + 1)
                nc.tensor.transpose(bank[3][:, 0:P], wh, ident).then_inc(S.wh_ps, 1)
                pe.wait_ge(S.whT_done, b + 1)
                if b >= 2:
                    pe.wait_ge(S.x_sum, lnc(5, b - 2))
                if b == 0:
                    pe.wait_ge(S.x_sum, lnc(4, B - 1))
                mm(bank[4 + b % 2][:, :], whT, bw_sb, start=True, stop=True).then_inc(S.rf_ps, 1)

        @block.scalar
        def _(act):
            def av(o, i, f, **k):
                return nc.scalar.activation(o, i, f, **k)

            chain = [0]

            def link(ins):
                chain[0] += 1
                ins.then_inc(S.act_chain, 1)
                act.wait_ge(S.act_chain, chain[0])

            act.wait_ge(S.par_in, 16)
            av(amat[:, :], pc("alog"), ACT.Exp).then_inc(S.amat_done, 1)
            act.wait_ge(S.tab_a, 1)
            av(tsm[:, 8, :], tsm[:, 7, :], ACT.Tanh).then_inc(S.tab_b, 1)
            for h in range(2):
                def silu_u(m):
                    act.wait_ge(S.conv_done, h * MD + m + 1)
                    av(u[:, m, :], conv[:, m % 2, :], ACT.Silu).then_inc(S.u_done, 1)

                if h:
                    act.wait_ge(S.y_done, MD)
                    act.wait_ge(S.wout_done, HB)
                for m in range(16):
                    act.wait_ge(S.inproj, h * 16 + m + 1)
                    if m < MD:
                        if m >= 2:
                            act.wait_ge(S.conv_done, h * MD + m - 1)
                        av(xpad[:, m % 2, :, CV - 1:], bank[m % 2][:, :].rearrange("p (b t) -> p b t", b=HB),
                           ACT.Identity).then_inc(S.in_evac, 1)
                        if m >= 1:
                            silu_u(m - 1)
                    else:
                        if m == MD:
                            silu_u(MD - 1)
                        av(g[:, m - MD, :], bank[m % 2][:, :], ACT.Silu).then_inc(S.in_evac, 1)
                act.wait_ge(S.ssm_done, h + 1)
                av(ssmsq, bank[2][:, 0:HB * SSM], ACT.Square).then_inc(S.ssm_sq, 1)
                act.wait_ge(S.ssmT_done, h + 1)
                av(ssmT[:, :], bank[3][0:SSM, :], ACT.Identity).then_inc(S.ssmT_sb, 1)
                for m in range(MD):
                    act.wait_ge(S.dt_proj, h * MD + m + 1)
                    av(dt[:, m, :], bank[4 + m % 2][:, :], ACT.Abs, bias=pc("bdt")[:, m:m + 1]).then_inc(S.dt_abs, 1)
                    av(sp_r[:, m, :], bank[4 + m % 2][:, :], ACT.Relu, bias=pc("bdt")[:, m:m + 1]).then_inc(S.dt_relu, 1)
                    act.wait_ge(S.dt_abs, h * MD + m + 1)
                    av(dt[:, m, :], dt[:, m, :], ACT.Exp, scale=-1.0).then_inc(S.dt_exp, 1)
                for m in range(MD):
                    act.wait_ge(S.dt_w, h * MD + m + 1)
                    av(sp_w[:, m, :], sp_w[:, m, :], ACT.Ln).then_inc(S.dt_ln, 1)
                for m in range(MD):
                    for q in range(GS):
                        i = (h * MD + m) * GS + q
                        if q == 0:
                            act.wait_ge(S.dt_done, h * MD + m + 1)
                            act.wait_ge(S.dA_zero, h + 1)
                        if i >= 2:
                            act.wait_ge(S.scan_done, i - 1)
                        for n in range(NG):
                            c = m * NS + q * NG + n
                            last = av(dA[:, i % 2, n, :].rearrange("p (b t) -> p b t", b=HB)[:, :, 1:],
                                      dt[:, m, :].rearrange("p (b t) -> p b t", b=HB)[:, :, 1:],
                                      ACT.Exp, scale=amat[:, c:c + 1])
                        last.then_inc(S.dA_done, 1)

            def spectra(b):
                act.wait_ge(S.qf_done, b + 1)
                if b >= 1:
                    act.wait_ge(S.m12_done, b)
                av(qf, bank[0][:, :], ACT.Identity).then_inc(S.qf_sb, 1)

            def weights(b):
                act.wait_ge(S.es_done, b + 1)
                av(ee, es, ACT.Exp).then_inc(S.ee_done, 1)

            def products(b):
                act.wait_ge(S.vf_done, b + 1)
                if b >= 1:
                    act.wait_ge(S.m4_done, b)
                av(vri[:, 0, :], bank[5][:, :], ACT.Identity)
                av(vri[:, 1, :], bank[6][:, :], ACT.Identity).then_inc(S.vri_sb, 1)
                act.wait_ge(S.wT_done, b + 1)
                av(wT, bank[4][:, :], ACT.Identity).then_inc(S.wT_sb, 1)

            spectra(0)
            weights(0)
            for b in range(B):
                if b + 1 < B:
                    spectra(b + 1)
                products(b)
                if b + 1 < B:
                    weights(b + 1)

            def turned(b, n, bk):
                act.wait_ge(S.xTt, n + 1)
                av(x2T[:, :, b * L:(b + 1) * L], bank[bk][:, :].rearrange("p (k t) -> p k t", k=KD),
                   ACT.Identity).then_inc(S.xT_sb, 1)

            for b in range(B):
                turned(b, b, b % 2)
            for b in range(B):
                turned(b, B + b, b % 2)
            for l in range(DEPTH + 1):
                if l < DEPTH:
                    for h in range(2):
                        act.wait_ge(S.d_tr, 4 * l + h + 1)
                        av(dys[:, h, :], bank[4 * h][:, :], ACT.Silu, scale=pc("ln1w")[:, l:l + 1],
                           bias=pc("ln1b")[:, l:l + 1]).then_inc(S.d_ys, 1)
                wn_, bn_ = (pc("ln2w")[0:DIM, l:l + 1], pc("ln2b")[0:DIM, l:l + 1]) if l < DEPTH else \
                    (pc("lnlw")[0:DIM, :], pc("lnlb")[0:DIM, :])
                for h in range(2):
                    act.wait_ge(S.d_tr, 4 * l + (2 if l < DEPTH else 0) + h + 1)
                    av(dys[0:DIM, h, :], bank[4 * h][0:DIM, :], ACT.Identity, scale=wn_, bias=bn_).then_inc(S.d_yT, 1)
                if l < DEPTH:
                    for h in range(2):
                        act.wait_ge(S.d_f1, 2 * l + h + 1)
                        for k in range(2):
                            last = av(df[:, h, k, :], bank[4 * h + 2 + k][:, :], ACT.Silu,
                                      bias=pc("b1")[:, 2 * l + k:2 * l + k + 1])
                        last.then_inc(S.d_f, 1)
            n = 0
            for gi in range(NKV):
                for h in range(2):
                    act.wait_ge(S.kv_ps, n + 1)
                    av(KT[:, gi, h * HT:(h + 1) * HT], bank[2 + n % 2][:, :], ACT.Identity,
                       bias=pc("bk")[:, gi:gi + 1]).then_inc(S.kv_sb, 1)
                    n += 1
            for b in range(B):
                for c in range(2):
                    act.wait_ge(S.kv_ps, n + 1)
                    av(V[:, b, c * 512:(c + 1) * 512], bank[2 + n % 2][:, :], ACT.Identity).then_inc(S.kv_sb, 1)
                    n += 1
            for b in range(B):
                turned(b, 2 * B + b, b % 2)
            NU = 2 * NKV

            def query_out(v, j):
                if v >= NU:
                    return
                act.wait_ge(S.q_ps, v * GQ + j + 1)
                av(qT[:, v % 2, j, :], bank[0][:, :], ACT.Identity,
                   bias=pc("bq")[:, (v % NKV) * GQ + j:(v % NKV) * GQ + j + 1]).then_inc(S.q_sb, 1)

            for j in range(GQ):
                query_out(0, j)
            for s in range(NU * HB + 2):
                v, b = s // HB, s % HB
                if s < NU * HB:
                    act.wait_ge(S.p_es, s + 1)
                    av(pe_[:, s % 2, :], pe_[:, s % 2, :], ACT.Exp, scale=SQ).then_inc(S.p_exp, 1)
                    query_out(v + 1, b)
                if 1 <= s <= NU * HB:
                    r = s - 1
                    act.wait_ge(S.t_ps, r + 1)
                    if r >= 2:
                        act.wait_ge(S.av_ps, r - 1)
                    av(pT[:, r % 2, :], bank[2][:, :], ACT.Identity).then_inc(S.t_sb, 1)
                if s >= 2:
                    r = s - 2
                    rv, rb = r // HB, r % HB
                    act.wait_ge(S.av_ps, r + 1)
                    if rv >= 2:
                        act.wait_ge(S.op_ps, (rv - 2) * HB + rb + 1)
                    av(oT[:, rv % 2, :, rb * L:(rb + 1) * L], bank[3][:, :].rearrange("p (j t) -> p j t", j=GQ),
                       ACT.Identity, bias=pc("bv")[:, rv % NKV:rv % NKV + 1]).then_inc(S.o_sb, 1)
            turned(0, 3 * B, 0)
            for b in range(B):
                if b + 1 < B:
                    turned(b + 1, 3 * B + b + 1, (b + 1) % 2)
                act.wait_ge(S.wh_ps, b + 1)
                if b >= 1:
                    act.wait_ge(S.rf_ps, b)
                av(whT, bank[3][:, 0:P], ACT.Identity).then_inc(S.whT_done, 1)

        def rstd(pool, stage, b):
            pool.wait_ge(S.ln_ve, lnc(stage, b))
            nc.gpsimd.tensor_tensor(lnrs[:, b:b + 1], lnve[:, b:b + 1], halfneg[:, 0:1], ALU.pow).then_inc(S.ln_rs, 1)

        @block.gpsimd
        def _(pool):
            gp = nc.gpsimd
            chain = [0]

            def link(ins):
                chain[0] += 1
                ins.then_inc(S.pool_chain, 1)
                pool.wait_ge(S.pool_chain, chain[0])

            def pad(h):
                gp.memset(xpad[:, :, :, 0:CV - 1], 0.0).then_inc(S.pad_zero, 1)

            link(gp.memset(halfneg[:, :], -0.5))
            pad(0)
            pool.wait_ge(S.tab_c, 1)
            gp.tensor_tensor(tsm[:, 5, :], tsm[:, 4, :], halfneg[:, 0:DEPTH], ALU.pow).then_inc(S.tab_d, 1)
            for h in range(2):
                if h:
                    pool.wait_ge(S.y_done, MD)
                    pad(1)
                pool.wait_ge(S.ssm_ve, h + 1)
                gp.tensor_tensor(ssm_rs[:, 0:3 * HB], ssm_ms[:, 0:3 * HB], halfneg[:, 0:3 * HB],
                                 ALU.pow).then_inc(S.ssm_rs, 1)
                for m in range(MD):
                    pool.wait_ge(S.dtu_done, h * MD + m + 1)
                    for q in range(GS):
                        i = (h * MD + m) * GS + q
                        if m == 0:
                            pool.wait_ge((S.b_in0, S.b_in1, S.b_in2, S.b_in3)[q * NG // 4], 16 * (h + 1))
                        if i >= 2:
                            pool.wait_ge(S.scan_done, i - 1)
                        gp.tensor_tensor(bu[:, i % 2, :, :], dtu[:, m % 2, :].unsqueeze(1).to_broadcast([P, NG, HT]),
                                         Brep[:, q * NG:(q + 1) * NG, :], ALU.mult).then_inc(S.bu_done, 1)
                for b in range(h * HB, (h + 1) * HB):
                    rstd(pool, 0, b)
            pool.wait_ge(S.sz_in, 64)
            for k in range(KD):
                pool.wait_ge(S.qw_in, 16 * (k + 1))
                link(gp.tensor_copy(weff[:, k, :], qw_sb[:, 0, :]))
                link(gp.tensor_tensor(weff[:, k, :], weff[:, k, :], sz[:, 1, k, :], ALU.subtract))
                gp.tensor_tensor(weff[:, k, :], weff[:, k, :], sz[:, 0, k, :], ALU.mult).then_inc(S.deq_done, 1)
                if k < 2:
                    rstd(pool, 1, k)
            rest = [(1, b) for b in range(2, B)]
            for st, b in rest:
                rstd(pool, st, b)

            def bias(b, n, name):
                pool.wait_ge(S.xTt, n + 1)
                gp.tensor_tensor(x_tok[:, b, :], x_tok[:, b, :], rw(name), ALU.add).then_inc(S.xbias, 1)

            bias(0, 0, "fbias")
            for b in range(B):
                if b + 1 < B:
                    bias(b + 1, b + 1, "fbias")
                rstd(pool, 2, b)
            for b in range(B):
                bias(b, B + b, "bout")

            for i in range(2 * (2 * DEPTH + 1)):
                pool.wait_ge(S.d_ve, i + 1)
                h = i % 2
                gp.tensor_tensor(drs[:, h * HB:(h + 1) * HB], dve_[:, h * HB:(h + 1) * HB], halfneg[:, 0:HB],
                                 ALU.pow).then_inc(S.d_rs, 1)
            for b in range(B):
                rstd(pool, 3, b)
            for b in range(B):
                bias(b, 2 * B + b, "bo")
            for b in range(B):
                rstd(pool, 4, b)
            for b in range(B):
                rstd(pool, 5, b)

        @block.vector
        def _(dve):
            v = nc.vector
            chain = [0]

            def link(ins):
                chain[0] += 1
                ins.then_inc(S.dve_chain, 1)
                dve.wait_ge(S.dve_chain, chain[0])

            def tables():
                pr, pi = pc("pre"), pc("pim")
                T = [tsm[:, i, :] for i in range(12)]
                z, m, a, b_, ssq, rsq, one, rmod, th, ta, tb, tc = T
                link(v.scalar_tensor_tensor(out=m, in0=pr, scalar=-1.0, in1=pr, op0=ALU.mult, op1=ALU.max))
                link(v.scalar_tensor_tensor(out=ta, in0=pi, scalar=-1.0, in1=pi, op0=ALU.mult, op1=ALU.max))
                link(v.tensor_tensor(m, m, ta, ALU.max))
                link(v.tensor_scalar(z, m, 0.0, None, ALU.is_equal))
                link(v.tensor_tensor(ta, m, z, ALU.add))
                link(v.reciprocal(tb, ta))
                link(v.tensor_tensor(a, pr, tb, ALU.mult))
                link(v.tensor_tensor(a, a, z, ALU.add))
                link(v.scalar_tensor_tensor(out=b_, in0=pi, scalar=-1.0, in1=tb, op0=ALU.mult, op1=ALU.mult))
                link(v.tensor_tensor(ta, a, a, ALU.mult))
                link(v.tensor_tensor(tb, b_, b_, ALU.mult))
                v.tensor_tensor(ssq, ta, tb, ALU.add).then_inc(S.tab_c, 1)
                dve.wait_ge(S.tab_d, 1)
                link(v.tensor_tensor(ta, ssq, rsq, ALU.mult))
                v.tensor_tensor(rmod, ta, m, ALU.mult).then_inc(S.tab_a, 1)
                link(v.tensor_tensor(a, a, rsq, ALU.mult))
                link(v.tensor_tensor(b_, b_, rsq, ALU.mult))
                link(v.tensor_tensor(ta, a, a, ALU.mult))
                link(v.tensor_tensor(tb, b_, b_, ALU.mult))
                link(v.tensor_tensor(ta, ta, tb, ALU.add))
                link(v.tensor_scalar(ta, ta, -0.5, 1.5, ALU.mult, ALU.add))
                link(v.tensor_tensor(a, a, ta, ALU.mult))
                link(v.tensor_tensor(b_, b_, ta, ALU.mult))
                dve.wait_ge(S.tab_b, 1)
                link(v.tensor_tensor(ta, th, a, ALU.mult))
                link(v.scalar_tensor_tensor(out=tb, in0=th, scalar=-1.0, in1=b_, op0=ALU.mult, op1=ALU.mult))
                lo, hi = slice(0, DIM), slice(DIM, P)
                lr, li = pc("lre"), pc("lim")
                link(v.tensor_tensor(tc[lo], tb[lo], li[lo], ALU.mult))
                link(v.tensor_tensor(one[lo], ta[lo], lr[lo], ALU.mult))
                link(v.tensor_tensor(z[lo], one[lo], tc[lo], ALU.subtract))
                link(v.tensor_tensor(tc[hi], tb[hi], lr[hi], ALU.mult))
                link(v.tensor_tensor(one[hi], ta[hi], li[hi], ALU.mult))
                link(v.tensor_tensor(z[hi], one[hi], tc[hi], ALU.add))
                return z, a, b_, th

            def big_tables(a, b_, th):
                link(v.memset(ctab[:, :, 0:1], 1.0))
                link(v.memset(stab[:, :, 0:1], 0.0))
                link(v.tensor_copy(ctab[:, :, 1:2], a.unsqueeze(2)))
                link(v.tensor_copy(stab[:, :, 1:2], b_.unsqueeze(2)))
                k = 1
                while k < L:
                    sh = [P, DEPTH, k]
                    cl, sl = ctab[:, :, 1:k + 1], stab[:, :, 1:k + 1]
                    ck, sk = ctab[:, :, k:k + 1].to_broadcast(sh), stab[:, :, k:k + 1].to_broadcast(sh)
                    cn, sn, tt = ctab[:, :, k + 1:2 * k + 1], stab[:, :, k + 1:2 * k + 1], ttmp[:, :, 0:k]
                    link(v.tensor_tensor(cn, cl, ck, ALU.mult))
                    link(v.tensor_tensor(tt, sl, sk, ALU.mult))
                    link(v.tensor_tensor(cn, cn, tt, ALU.subtract))
                    link(v.tensor_tensor(sn, sl, ck, ALU.mult))
                    link(v.tensor_tensor(tt, cl, sk, ALU.mult))
                    link(v.tensor_tensor(sn, sn, tt, ALU.add))
                    k *= 2
                link(v.tensor_copy(ctab[DIM:P, :, :], stab[DIM:P, :, :]))
                link(v.memset(rtab, 1.0))
                link(v.tensor_tensor(rtab, rtab, th.unsqueeze(2).to_broadcast([P, DEPTH, HT]), ALU.mult))
                link(v.memset(rtab.rearrange("p l (b t) -> p (l b) t", b=HB)[:, :, 0:1], 0.0))
                v.tensor_tensor(dsc, rw("scl").rearrange("p (l o) -> p l o", l=DEPTH),
                                pc("twoI").unsqueeze(1).to_broadcast([P, DEPTH, DIM]), ALU.mult).then_inc(S.tab_done, 1)
                dve.wait_ge(S.tab_done, 1)

            def ln_a(stage, b, ps, ready, value):
                dve.wait_ge(ready, value)
                if stage == 0:
                    dve.wait_ge(S.xtok_in, 16)
                bias_n = {2: b + 1, 3: B + b + 1, 4: 2 * B + b + 1}.get(stage)
                if bias_n:
                    dve.wait_ge(S.xbias, bias_n)
                v.tensor_tensor(x_tok[:, b, :], x_tok[:, b, :], ps, ALU.add).then_inc(S.x_sum, 1)
                dve.wait_ge(S.x_sum, lnc(stage, b))
                link(v.bn_stats(lnst[:, b, :], x_tok[:, b, :]))
                link(v.bn_aggr(lnmv[:, b, :], lnst[:, b, :]))
                v.tensor_scalar(lnve[:, b:b + 1], lnmv[:, b, 1:2], 1e-5, None, ALU.add).then_inc(S.ln_ve, 1)

            def ln_b(stage, b):
                dve.wait_ge(S.ln_rs, lnc(stage, b))
                v.tensor_scalar(x_tok[:, b, :], x_tok[:, b, :], lnmv[:, b, 0:1], lnrs[:, b:b + 1],
                                ALU.subtract, ALU.mult).then_inc(S.x_done, 1)

            dve.wait_ge(S.par_in, 16)
            plc, a1, b1_, th1 = tables()
            dve.wait_ge(S.amat_done, 1)
            link(v.tensor_scalar(amat[:, :], amat[:, :], -1.0, None, ALU.mult))
            for h in range(2):
                dve.wait_ge(S.pad_zero, h + 1)
                for m in range(MD):
                    dve.wait_ge(S.in_evac, h * 16 + m + 1)
                    if h * MD + m >= 2:
                        dve.wait_ge(S.u_done, h * MD + m - 1)
                    acc = conv[:, m % 2, :].rearrange("p (b t) -> p b t", b=HB)
                    w = pc("convw")[:, m * CV:(m + 1) * CV]
                    link(v.tensor_scalar(acc, xpad[:, m % 2, :, 0:L], w[:, 0:1], pc("convb")[:, m:m + 1],
                                         ALU.mult, ALU.add))
                    for j in range(1, CV):
                        ins = v.scalar_tensor_tensor(out=acc, in0=xpad[:, m % 2, :, j:j + L], scalar=w[:, j:j + 1],
                                                     in1=acc, op0=ALU.mult, op1=ALU.add)
                        if j < CV - 1:
                            link(ins)
                        else:
                            ins.then_inc(S.conv_done, 1)
                dve.wait_ge(S.ssm_sq, h + 1)
                link(v.tensor_reduce(ssm_ss[:, 0:4 * HB], ssmsq.rearrange("p (a c) -> p a c", c=NS), AX.X, ALU.add))
                ss = ssm_ss[:, 0:4 * HB].rearrange("p (b c) -> p b c", b=HB)
                ms = ssm_ms[:, 0:3 * HB].rearrange("p (b c) -> p b c", b=HB)
                rs = ssm_rs[:, 0:3 * HB].rearrange("p (b c) -> p b c", b=HB)
                link(v.tensor_tensor(ms[:, :, 0:1], ss[:, :, 0:1], ss[:, :, 1:2], ALU.add))
                link(v.tensor_scalar(ms[:, :, 0:1], ms[:, :, 0:1], 1.0 / RK, 1e-6, ALU.mult, ALU.add))
                v.tensor_scalar(ms[:, :, 1:3], ss[:, :, 2:4], 1.0 / NS, 1e-6, ALU.mult, ALU.add).then_inc(S.ssm_ve, 1)
                dve.wait_ge(S.ssm_rs, h + 1)
                pb = bank[2][:, 0:HB * SSM].rearrange("p (b c) -> p b c", b=HB)
                for i, (a, b_) in enumerate(((0, RK), (RK, RK + NS), (RK + NS, SSM))):
                    ins = v.tensor_tensor(ssmn[:, :, a:b_], pb[:, :, a:b_], rs[:, :, i:i + 1].to_broadcast([P, HB, b_ - a]),
                                          ALU.mult)
                    if i < 2:
                        link(ins)
                    else:
                        ins.then_inc(S.ssm_norm, 1)
                dve.wait_ge(S.ssmT_sb, h + 1)
                v.memset(psum[:, 0:2 * NG * HT].rearrange("p (c t) -> p c t", t=L)[:, :, 0:1], 0.0).then_inc(S.dA_zero, 1)
                for m in range(MD):
                    dve.wait_ge(S.dt_exp, h * MD + m + 1)
                    v.tensor_scalar(sp_w[:, m, :], dt[:, m, :], 1.0, None, ALU.add).then_inc(S.dt_w0, 1)
                    dve.wait_ge(S.dt_w0, h * MD + m + 1)
                    v.scalar_tensor_tensor(out=dt[:, m, :], in0=sp_w[:, m, :], scalar=1.0, in1=dt[:, m, :],
                                           op0=ALU.subtract, op1=ALU.subtract).then_inc(S.dt_w, 1)

                def step_size(m):
                    dve.wait_ge(S.dt_ln, h * MD + m + 1)
                    dve.wait_ge(S.dt_relu, h * MD + m + 1)
                    link(v.tensor_tensor(sp_r[:, m, :], sp_r[:, m, :], sp_w[:, m, :], ALU.add))
                    v.tensor_tensor(dt[:, m, :], sp_r[:, m, :], dt[:, m, :], ALU.subtract).then_inc(S.dt_done, 1)

                def step_in(m):
                    if h * MD + m >= 2:
                        dve.wait_ge(S.bu_done, (h * MD + m - 1) * GS)
                    dve.wait_ge(S.dt_done, h * MD + m + 1)
                    v.tensor_tensor(dtu[:, m % 2, :], dt[:, m, :], u[:, m, :], ALU.mult).then_inc(S.dtu_done, 1)

                def c_times(i):
                    q = i % GS
                    if (i // GS) % MD == 0:
                        dve.wait_ge((S.c_in0, S.c_in1, S.c_in2, S.c_in3)[q * NG // 4], 16 * (h + 1))
                    if i >= 2:
                        dve.wait_ge(S.ysum, i - 1)
                    dve.wait_ge(S.scan_done, i + 1)
                    v.tensor_tensor(prod[:, i % 2, :, :], state.rearrange("p (n t) -> p n t", n=NG), Crep[:, q * NG:(q + 1) * NG, :],
                                    ALU.mult).then_inc(S.prod_done, 1)

                def finish_y(m):
                    dve.wait_ge(S.ysum, (h * MD + m + 1) * GS)
                    link(v.scalar_tensor_tensor(out=ytmp, in0=u[:, m, :], scalar=pc("dskip")[:, m:m + 1],
                                                in1=bank[6 + m % 2][:, :], op0=ALU.mult, op1=ALU.add))
                    v.tensor_tensor(g[:, m, :], ytmp, g[:, m, :], ALU.mult).then_inc(S.y_done, 1)

                step_size(0)
                step_in(0)
                step_size(1)
                for m in range(MD):
                    for q in range(GS):
                        i = (h * MD + m) * GS + q
                        if q == 2 and m + 1 < MD:
                            step_in(m + 1)
                        if q == 4 and m + 2 < MD:
                            step_size(m + 2)
                        dve.wait_ge(S.dA_done, i + 1)
                        dve.wait_ge(S.bu_done, i + 1)
                        if i:
                            dve.wait_ge(S.prod_done, i)
                        v.tensor_tensor_scan(state, dA[:, i % 2, :, :].rearrange("p n t -> p (n t)"),
                                             bu[:, i % 2, :, :].rearrange("p n t -> p (n t)"), 0.0,
                                             ALU.mult, ALU.add).then_inc(S.scan_done, 1)
                        if q == 5 and m >= 1:
                            finish_y(m - 1)
                        c_times(i)
                finish_y(MD - 1)
                for b in range(h * HB, (h + 1) * HB):
                    ln_a(0, b, bank[b % 2][:, :], S.wout_done, b + 1)
                    if b > h * HB:
                        ln_b(0, b - 1)
                ln_b(0, (h + 1) * HB - 1)

            link(v.memset(m9, -BIG))

            def spectra(b):
                dve.wait_ge(S.qf_sb, b + 1)
                dve.wait_ge(S.kf_done, b + 1)
                if b >= 1:
                    dve.wait_ge(S.corr, b)
                v.tensor_tensor(m12[:, 0, :], qf, bank[1][:, :], ALU.mult)
                v.tensor_tensor(m12[:, 1, :], qf, bank[2][:, :], ALU.mult).then_inc(S.m12_done, 1)

            def topk(b):
                dve.wait_ge(S.corr, b + 1)
                cor = bank[3][:, :]
                for t in range(KD):
                    o = slice(t * P, (t + 1) * P)
                    last = v.max(mx8[:, t * 8:t * 8 + 8], cor[:, o])
                link(last)
                v.tensor_tensor(es.rearrange("p (t n) -> p t n", t=KD), cor.rearrange("p (t n) -> p t n", t=KD),
                                mx8.rearrange("p (t n) -> p t n", t=KD)[:, :, 0:1].to_broadcast([P, KD, P]),
                                ALU.subtract).then_inc(S.es_done, 1)
                for t in range(KD):
                    o = slice(t * P, (t + 1) * P)
                    last = v.match_replace(rep1[:, o], mx8[:, t * 8:t * 8 + 8], cor[:, o], -BIG)
                last.then_inc(S.corr_read, 1)
                dve.wait_ge(S.corr_read, b + 1)
                for t in range(KD):
                    last = v.max(nx8[:, t * 8:t * 8 + 8], rep1[:, t * P:(t + 1) * P])
                link(last)
                link(v.tensor_copy(m9.rearrange("p (t n) -> p t n", t=KD)[:, :, 0:TOPK - 8],
                                   nx8.rearrange("p (t n) -> p t n", t=KD)[:, :, 0:TOPK - 8]))
                for t in range(KD):
                    o = slice(t * P, (t + 1) * P)
                    last = v.match_replace(rep2[:, o], m9[:, t * 8:t * 8 + 8], rep1[:, o], -BIG)
                link(last)
                dve.wait_ge(S.ee_done, b + 1)
                link(v.scalar_tensor_tensor(out=rep2, in0=rep2, scalar=-BIG, in1=ee, op0=ALU.is_equal, op1=ALU.mult))
                link(v.tensor_reduce(wsum[:, 0:KD], rep2.rearrange("p (t n) -> p t n", t=KD), AX.X, ALU.add))
                link(v.reciprocal(winv[:, 0:KD], wsum[:, 0:KD]))
                if b >= 2:
                    dve.wait_ge(S.wT_done, b - 1)
                v.tensor_tensor(wn[:, b % 2, :].rearrange("p (t n) -> p t n", t=KD),
                                rep2.rearrange("p (t n) -> p t n", t=KD),
                                winv[:, 0:KD].unsqueeze(2).to_broadcast([P, KD, P]), ALU.mult).then_inc(S.wn_done, 1)

            def products(b):
                dve.wait_ge(S.wf_done, b + 1)
                dve.wait_ge(S.vri_sb, b + 1)
                if b >= 1:
                    dve.wait_ge(S.xat_done, b)
                v.tensor_tensor(m4[:, 0, :], vri[:, 0, :], bank[5][:, :], ALU.mult)
                v.tensor_tensor(m4[:, 2, :], vri[:, 1, :], bank[5][:, :], ALU.mult)
                v.tensor_tensor(m4[:, 1, :], vri[:, 1, :], bank[6][:, :], ALU.mult)
                v.tensor_tensor(m4[:, 3, :], vri[:, 0, :], bank[6][:, :], ALU.mult).then_inc(S.m4_done, 1)

            spectra(0)
            topk(0)
            for b in range(B):
                if b + 1 < B:
                    spectra(b + 1)
                products(b)
                if b + 1 < B:
                    topk(b + 1)
                ln_a(1, b, bank[7][:, :], S.xat_done, b + 1)
                if b >= 1:
                    ln_b(1, b - 1)
            ln_b(1, B - 1)
            for k in range(KD):
                dve.wait_ge(S.lora_done, k + 1)
                dve.wait_ge(S.deq_done, k + 1)
                v.scalar_tensor_tensor(out=weff[:, k, :], in0=bank[4][:, :], scalar=1.0 / 16, in1=weff[:, k, :],
                                       op0=ALU.mult, op1=ALU.add).then_inc(S.weff_done, 1)
            for b in range(B):
                ln_a(2, b, bank[2 + b % 2][:, :], S.ffn_done, b + 1)
                if b >= 1:
                    ln_b(2, b - 1)
            ln_b(2, B - 1)
            big_tables(a1, b1_, th1)
            for h in range(2):
                dve.wait_ge(S.h0_done, h + 1)
                hs = slice(h * HB, (h + 1) * HB)
                v.tensor_tensor(dh[:, hs, :], bank[4 + h][:, 0:HB * DIM].rearrange("p (b c) -> p b c", b=HB),
                                rw("bin").unsqueeze(1).to_broadcast([P, HB, DIM]), ALU.add).then_inc(S.h0_read, 1)
            dve.wait_ge(S.h0_read, 2)

            def stats(h):
                for b in range(h * HB, (h + 1) * HB):
                    last = v.bn_stats(dst[:, b, :], dh[:, b, :])
                link(last)
                for b in range(h * HB, (h + 1) * HB):
                    last = v.bn_aggr(dmv[:, b, :], dst[:, b, :])
                link(last)
                hs = slice(h * HB, (h + 1) * HB)
                v.tensor_scalar(dve_[:, hs], dmv[:, hs, 1:2].rearrange("p b o -> p (b o)"), 1e-5, None,
                                ALU.add).then_inc(S.d_ve, 1)
                link(v.tensor_tensor(dhc[:, hs, :], dh[:, hs, :], dmv[:, hs, 0:1].to_broadcast([P, HB, DIM]),
                                     ALU.subtract))

            def norm(n, h, copies, free):
                dve.wait_ge(S.d_rs, n)
                if free:
                    dve.wait_ge(S.d_tr, free)
                hs = slice(h * HB, (h + 1) * HB)
                for c in range(copies):
                    last = v.tensor_tensor(dyn[:, h, :, c * DIM:(c + 1) * DIM], dhc[:, hs, :],
                                           drs[:, hs].unsqueeze(2).to_broadcast([P, HB, DIM]), ALU.mult)
                last.then_inc(S.d_yn, 1)

            for l in range(DEPTH):
                for h in range(2):
                    stats(h)
                for h in range(2):
                    norm(4 * l + h + 1, h, 2, 4 * l)
                for h in range(2):
                    dve.wait_ge(S.d_ys, 2 * l + h + 1)
                    if l:
                        dve.wait_ge(S.d_conv, 2 * l)
                    z3 = dz[:, h, :].rearrange("p (b t) -> p b t", b=HB)
                    tab = ctab[:, l, 0:L].unsqueeze(1).to_broadcast([P, HB, L])
                    link(v.tensor_tensor(z3, dys[:, h, :].rearrange("p (b t) -> p b t", b=HB), tab, ALU.mult))
                    link(v.tensor_scalar(z3[:, :, 0:1], z3[:, :, 0:1], plc[:, l:l + 1], None, ALU.add))
                    link(v.tensor_tensor_scan(dz[:, h, :], rtab[:, l, :], dz[:, h, :], 0.0, ALU.mult, ALU.add))
                    v.tensor_tensor(z3, z3, tab, ALU.mult).then_inc(S.d_z, 1)
                for h in range(2):
                    hs = slice(h * HB, (h + 1) * HB)
                    dve.wait_ge(S.d_conv, 2 * l + h + 1)
                    v.tensor_tensor(dh[:, hs, :], dh[:, hs, :],
                                    bank[4 * h + 1][:, 0:HB * DIM].rearrange("p (b c) -> p b c", b=HB),
                                    ALU.add).then_inc(S.d_hread, 1)
                    dve.wait_ge(S.d_hread, 2 * l + h + 1)
                    stats(h)
                for h in range(2):
                    norm(4 * l + 2 + h + 1, h, 1, 4 * l + 2)
                for h in range(2):
                    hs = slice(h * HB, (h + 1) * HB)
                    link(v.tensor_tensor(dh[:, hs, :], dh[:, hs, :],
                                         rw("b2")[:, l * DIM:(l + 1) * DIM].unsqueeze(1).to_broadcast([P, HB, DIM]),
                                         ALU.add))
                    dve.wait_ge(S.d_f2, 2 * l + h + 1)
                    v.tensor_tensor(dh[:, hs, :], dh[:, hs, :],
                                    bank[4 * h + 1][:, 0:HB * DIM].rearrange("p (b c) -> p b c", b=HB),
                                    ALU.add).then_inc(S.d_f2read, 1)
                    dve.wait_ge(S.d_f2read, 2 * l + h + 1)
            for h in range(2):
                stats(h)
            for h in range(2):
                norm(4 * DEPTH + h + 1, h, 1, 4 * DEPTH)
            for b in range(B):
                ln_a(3, b, bank[2 + b % 2][:, :], S.d_out, b + 1)
                if b >= 1:
                    ln_b(3, b - 1)
            ln_b(3, B - 1)
            NU = 2 * NKV
            sh = [P, GQ, P]

            def soft_a(s):
                dve.wait_ge(S.s_ps, s + 1)
                ps = bank[1][:, :].rearrange("p (j m) -> p j m", j=GQ)
                link(v.tensor_reduce(amax[:, :], ps, AX.X, ALU.max))
                if s >= 2:
                    dve.wait_ge(S.p_norm, s - 1)
                v.tensor_tensor(pe_[:, s % 2, :].rearrange("p (j m) -> p j m", j=GQ), ps,
                                amax[:, :].unsqueeze(2).to_broadcast(sh), ALU.subtract).then_inc(S.p_es, 1)

            def soft_b(s):
                dve.wait_ge(S.p_exp, s + 1)
                pr = pe_[:, s % 2, :].rearrange("p (j m) -> p j m", j=GQ)
                link(v.tensor_reduce(asum[:, 0, :], pr, AX.X, ALU.add))
                link(v.reciprocal(ainv[:, :], asum[:, 0, :]))
                if s >= 1:
                    dve.wait_ge(S.t_ps, s)
                v.tensor_tensor(pn.rearrange("p (j m) -> p j m", j=GQ), pr, ainv[:, :].unsqueeze(2).to_broadcast(sh),
                                ALU.mult).then_inc(S.p_norm, 1)

            def attn_ln(rb):
                pass

            def soft_read(s):
                pass

            for s in range(NU * HB + 4):
                if s < NU * HB:
                    soft_a(s)
                    soft_b(s)
                if s >= 4:
                    r = s - 4
                    rv, rb = r // HB, r % HB
                    if rv % NKV == NKV - 1:
                        b = (rv // NKV) * HB + rb
                        ln_a(4, b, bank[4 + rb][:, :], S.op_ps, r + 1)
                        ln_b(4, b)
            for b in range(B):
                dve.wait_ge(S.r_ps, b + 1)
                link(v.tensor_copy(logits, bank[2][:, P:P + 8]))
                link(v.max(rt8, logits))
                link(v.max_index(ri8[:, :], rt8, logits))
                link(v.tensor_copy(rif, ri8[:, :]))
                link(v.tensor_scalar(rwt, pc("iota8"), rif[:, 0:1], rt8[:, 0:1], ALU.is_equal, ALU.mult))
                if b >= 1:
                    dve.wait_ge(S.wh_ps, b)
                v.tensor_tensor(wh.rearrange("p (e r) -> p e r", e=8), bank[2][:, 0:P].rearrange("p (e r) -> p e r", e=8),
                                rwt.unsqueeze(2).to_broadcast([P, 8, 16]), ALU.mult).then_inc(S.r_wh, 1)
                if b >= 1:
                    ln_a(5, b - 1, bank[4 + (b - 1) % 2][:, :], S.rf_ps, b)
                    ln_b(5, b - 1)
            ln_a(5, B - 1, bank[4 + (B - 1) % 2][:, :], S.rf_ps, B)
            ln_b(5, B - 1)


def kernel(**inp):
    import concourse.bacc as bacc
    from concourse.bass_utils import run_bass_kernel_spmd

    a = {k: np.asarray(v) for k, v in inp.items()}
    cat = np.concatenate

    def cols(v):
        return v.reshape(-1, P).T

    def twice(v):
        return cat([v.T, v.T], 0)

    x, ctx = a["x"], a["ctx_4096"]
    xT = x.reshape(2, HT, KD, P).transpose(0, 3, 2, 1)
    bkv = a["L1_xattn_bkv"]
    vals = {
        "convw": a["L0_attn_conv_w"].reshape(MD, P, CV).transpose(1, 0, 2).reshape(P, MD * CV),
        "convb": cols(a["L0_attn_conv_b"]), "bdt": cols(a["L0_attn_b_dt"]),
        "alog": a["L0_attn_A_log"].reshape(MD, P, NS).transpose(1, 0, 2).reshape(P, MD * NS),
        "dskip": cols(a["L0_attn_D"]), "bq": cols(a["L1_xattn_bq"]),
        "bk": cols(bkv[:1024]), "bv": cols(bkv[1024:]),
        "ln1w": twice(a["L1_attn_ln1_w"]), "ln1b": twice(a["L1_attn_ln1_b"]),
        "ln2w": twice(a["L1_attn_ln2_w"]), "ln2b": twice(a["L1_attn_ln2_b"]),
        "lnlw": twice(a["L1_attn_lnl_w"][None]), "lnlb": twice(a["L1_attn_lnl_b"][None]),
        "b1": cols(a["L1_attn_b1"].reshape(-1)),
        "pre": twice(a["L1_attn_phz_re"]), "pim": twice(a["L1_attn_phz_im"]),
        "lre": twice(a["L1_attn_lc_re"]), "lim": twice(a["L1_attn_lc_im"]),
        "ident": np.eye(P, dtype=np.float32), "twoI": cat([np.eye(DIM, dtype=np.float32)] * 2, 0),
        "iota8": np.tile(np.arange(8, dtype=np.float32), (P, 1)),
    }
    par = cat([vals[n] for n, _ in _COLS], 1)
    rvals = {"fbias": a["L0_ffn_bias"], "bout": a["L1_attn_bout"], "bo": a["L1_xattn_bo"], "bin": a["L1_attn_bin"],
             "b2": a["L1_attn_b2"].reshape(-1), "scl": a["L1_attn_sc_lin"].reshape(-1)}
    wkv = a["L1_xattn_Wkv"]

    def groups(s):
        return s.T.reshape(KD, 2, D).transpose(1, 0, 2)

    arrays = {
        "xT": xT, "xtok": x.transpose(1, 0, 2),
        "ctxT": ctx.reshape(B * L, KD, P).transpose(2, 1, 0), "ctxtok": ctx.transpose(1, 0, 2),
        "par": par, "rows": cat([rvals[n] for n, _ in _ROWS]), "four": fourier(),
        "win": a["L0_attn_W_in"].reshape(16, P, KD, P).transpose(0, 3, 2, 1).reshape(16, P, 512),
        "wx": a["L0_attn_W_x"].reshape(SSM, MD, P).transpose(2, 1, 0),
        "wdt": a["L0_attn_W_dt"].T, "wout": a["L0_attn_W_out"].T.reshape(MD, P, D),
        "qw": a["L0_ffn_qweight"].T.reshape(KD, P, D), "sc": groups(a["L0_ffn_scales"]),
        "ze": groups(a["L0_ffn_zeros"]), "loraA": a["L0_ffn_lora_A"], "loraBT": a["L0_ffn_lora_B"].T,
        "dwin": a["L1_attn_Win"].reshape(DIM, KD, P).transpose(2, 1, 0),
        "dw1": a["L1_attn_W1"].transpose(2, 0, 1),
        "dw2": a["L1_attn_W2"].reshape(DEPTH, DIM, 2, P).transpose(3, 0, 2, 1),
        "dwout": a["L1_attn_Wout"].T,
        "wq": a["L1_xattn_Wq"].reshape(KD, P, NKV, GQ, P).transpose(2, 1, 3, 0, 4).reshape(NKV, P, GQ * 512),
        "wk": wkv[:, :1024].reshape(KD, P, NKV, P).transpose(2, 1, 0, 3).reshape(NKV, P, 512),
        "wv": wkv[:, 1024:].reshape(KD, P, 1024).transpose(1, 0, 2),
        "wo": a["L1_xattn_Wo"].reshape(NKV, GQ, P, D).transpose(0, 2, 1, 3),
        "ra": cat([a["L1_ffn_A"].reshape(P, D), a["L1_ffn_route_w"]], 0).T.reshape(KD, P, P + 8).transpose(1, 0, 2),
        "bwT": a["L1_ffn_Bw"].transpose(0, 2, 1).reshape(P, D),
    }
    arrays = {k: np.ascontiguousarray(v) for k, v in arrays.items()}
    nc = bacc.Bacc("TRN2", target_bir_lowering=False, num_devices=1)
    args = [nc.dram_tensor(n, v.shape, mybir.dt.from_np(v.dtype), kind="ExternalInput").ap() for n, v in arrays.items()]
    args.append(nc.dram_tensor("out", (B, L, D), F32, kind="ExternalOutput").ap())
    decoder_kernel(nc, *args)
    r = run_bass_kernel_spmd(nc, [arrays], core_ids=[0])
    return r.results[0]["out"]
```

```python
from contextlib import ExitStack

import numpy as np

import concourse.bass as bass
from concourse import mybir

F32 = mybir.dt.float32
F32R = mybir.dt.float32r
I32 = mybir.dt.int32
U32 = mybir.dt.uint32
ALU = mybir.AluOpType
ACT = mybir.ActivationFunctionType
AX = mybir.AxisListType

P = 128
B = 8
L = 128
D = 512
KD = D // P
HB = B // 2
HT = HB * L
DI = 1024
MD = DI // P
NS = 16
NG = 2
GS = NS // NG
RK = 32
SSM = RK + 2 * NS
CV = 4
DEPTH, DIM, DFF = 4, 64, 256
EARLY = 2
KVL = 8
NKV, GQ = 8, 4
TOPK = int(2 * np.log(L))
BIG = 3.0e38
SQ = float(1.0 / np.sqrt(128.0))

_COLS = [("convw", MD * CV), ("convb", MD), ("bdt", MD), ("alog", MD * NS), ("dskip", MD),
         ("bq", NKV * GQ), ("bk", NKV), ("bv", NKV), ("ln1w", DEPTH), ("ln1b", DEPTH),
         ("ln2w", DEPTH), ("ln2b", DEPTH), ("lnlw", 1), ("lnlb", 1), ("b1", DEPTH * 2),
         ("pre", DEPTH), ("pim", DEPTH), ("lre", DEPTH), ("lim", DEPTH), ("ident", P),
         ("twoI", DIM), ("iota8", 8)]
COL = {}
_at = 0
for _n, _w in _COLS:
    COL[_n] = (_at, _at + _w)
    _at += _w
NPAR = _at
_ROWS = [("fbias", D), ("bout", D), ("bo", D), ("bin", DIM), ("b2", DEPTH * DIM), ("scl", DEPTH * DIM)]
ROW = {}
_at = 0
for _n, _w in _ROWS:
    ROW[_n] = (_at, _at + _w)
    _at += _w
NROW = _at
FOUR = ["q", "k_swap", "c_re", "c_im", "w_re", "w_im", "v_re", "v_im", "o_rr", "o_ii", "o_ri", "o_ir"]


def fourier():
    n = np.arange(L)[:, None].astype(np.float64)
    m = {}
    f = np.arange(64)[None, :]
    re, im = np.cos(2 * np.pi * n * f / L), -np.sin(2 * np.pi * n * f / L)
    im[:, 0] = np.cos(np.pi * n[:, 0])
    m["q"] = np.concatenate([re, im], 1)
    m["k_swap"] = np.concatenate([im, re], 1)
    t = np.arange(L)[None, :]
    fc = np.arange(64)[:, None]
    w = np.where(fc == 0, 1.0, 2.0) / L
    cos, sin = w * np.cos(2 * np.pi * fc * t / L), w * np.sin(2 * np.pi * fc * t / L)
    lower = cos.copy()
    lower[0] = np.cos(np.pi * t[0]) / L
    m["c_re"] = np.concatenate([cos, lower], 0)
    m["c_im"] = np.concatenate([sin * (fc > 0), -sin * (fc > 0)], 0)
    f = np.arange(128)[None, :]
    re, im = np.cos(np.pi * n * f / L), -np.sin(np.pi * n * f / L)
    im[:, 0] = np.cos(np.pi * n[:, 0])
    m["w_re"], m["w_im"] = re, im
    s = np.arange(2 * L)[:, None].astype(np.float64)
    re, im = np.cos(np.pi * s * f / L), -np.sin(np.pi * s * f / L)
    im[:, 0] = np.cos(np.pi * s[:, 0])
    for name, full in (("v_re", re), ("v_im", im)):
        fold = full[:L].copy()
        fold[L - 1] += full[L:].sum(0)
        m[name] = fold
    fc = np.arange(128)[:, None]
    w = np.where(fc == 0, 1.0, 2.0) / (2 * L)
    cos, sin = w * np.cos(np.pi * fc * t / L), w * np.sin(np.pi * fc * t / L)
    ii = cos.copy()
    ii[0] = np.cos(np.pi * t[0]) / (2 * L)
    m["o_rr"], m["o_ii"] = cos, ii
    m["o_ri"], m["o_ir"] = -sin * (fc > 0), sin * (fc > 0)
    return np.ascontiguousarray(np.stack([m[k] for k in FOUR], 1).astype(np.float32))


def decoder_kernel(nc, xT, xtok, ctxT, ctxtok, par, rows, four, win, wx, wdt, wout, qw, sc, ze,
                   loraA, loraBT, dwin, dw1, dw2, dwout, wq, wk, wv, wo, ra, bwT, out):
    scratch = nc.dram_tensor("bc_scratch", [2, 2 * NS, HT], F32, kind="Internal").ap()
    with ExitStack() as ctx:
        def sb(name, shape, dt=F32):
            return ctx.enter_context(nc.sbuf_tensor(name, shape, dt))

        names = {}

        def sem(name):
            names[name] = ctx.enter_context(nc.semaphore(name))
            return names[name]

        KB = 256
        with nc.sbuf_tensor("arena", [P, 172 * KB], F32) as arena:
            pass
        with nc.sbuf_tensor("gap0", [P, 64 * KB], F32), nc.sbuf_tensor("x_split", [P, 16 * KB], F32R) as x_split, \
                nc.sbuf_tensor("gap1", [P, 16 * KB], F32), nc.sbuf_tensor("o_split", [P, 12 * KB], F32R) as o_split, \
                nc.sbuf_tensor("gap2", [P, 20 * KB], F32), nc.sbuf_tensor("w_split", [P, 44 * KB], F32R) as w_split:
            pass
        sb("arena_space", [P, 172 * KB])

        def part(at, size, parts=P):
            return arena[0:parts, int(at * KB):int(at * KB) + size]

        x_tok = sb("x_tok", [P, B, D])
        prm = sb("prm", [P, NPAR])
        row = sb("row", [P, NROW])
        amat = sb("amat", [P, MD * NS])
        lnst = sb("lnst", [P, B, 6])
        lnmv = sb("lnmv", [P, B, 2])
        lnve = sb("lnve", [P, B])
        lnrs = sb("lnrs", [P, B])
        halfneg = sb("halfneg", [P, 16])

        def pc(name):
            a, b = COL[name]
            return prm[:, a:b]

        def rw(name):
            a, b = ROW[name]
            return row[:, a:b]

        ident = pc("ident")
        psum = ctx.enter_context(nc.psum_tensor("psum", [P, 8 * 512], F32))
        bank = [psum[:, i * 512:(i + 1) * 512] for i in range(8)]

        xs = x_split[:, :].rearrange("p (i k n) -> p i k n", i=2, k=KD)
        osp = o_split[:, :].rearrange("p (i s n) -> p i s n", i=2, s=3)
        wqs = w_split[:, 0:12 * KB].rearrange("p (i s n) -> p i s n", i=2, s=3)
        wos = w_split[:, 12 * KB:44 * KB].rearrange("p (i s n) -> p i s n", i=2, s=8)
        xTh = part(0, KD * HT).rearrange("p (k n) -> p k n", k=KD)
        wring = part(8, 4 * 512).rearrange("p (s n) -> p s n", s=4)
        xpad = part(16, 2 * HB * (L + CV - 1)).rearrange("p (s b n) -> p s b n", s=2, b=HB)
        conv = part(21, 2 * HT).rearrange("p (s n) -> p s n", s=2)
        ssmsq = part(26, HB * SSM)
        ssmn = part(27, HB * SSM).rearrange("p (b c) -> p b c", b=HB)
        ssm_ss = part(28, 64)
        ssm_ms = part(28.5, 16)
        ssm_rs = part(28.75, 16)
        Brep = part(0, NS * HT).rearrange("p (n t) -> p n t", n=NS)
        Crep = part(32, NS * HT).rearrange("p (n t) -> p n t", n=NS)
        dA = psum[:, 0:3 * NG * HT].rearrange("p (s n t) -> p s n t", s=3, n=NG)
        skip = sb("skip", [P, 2, P])
        zeros = sb("zeros", [P, NG * HB])
        bu = part(80, 2 * NG * HT).rearrange("p (s n t) -> p s n t", s=2, n=NG)
        prod = part(88, 2 * NG * HT).rearrange("p (s n t) -> p s n t", s=2, n=NG)
        sp_w = part(64, MD * HT).rearrange("p (m t) -> p m t", m=MD)
        sp_r = part(96, MD * HT).rearrange("p (m t) -> p m t", m=MD)
        u = part(112, MD * HT).rearrange("p (m t) -> p m t", m=MD)
        dt = part(128, MD * HT).rearrange("p (m t) -> p m t", m=MD)
        g = part(144, MD * HT).rearrange("p (m t) -> p m t", m=MD)
        wout_sb = dt
        wx_sb = part(160, MD * SSM).rearrange("p (k o) -> p k o", k=MD)
        wdt_sb = part(162, DI, RK)
        dtu = part(166, 2 * HT).rearrange("p (s n) -> p s n", s=2)
        ytmp = part(170, HT)
        ssmT = sb("ssmT", [SSM, HT])
        ctx_sb = part(0, B * D).rearrange("p (b d) -> p b d", b=B)
        four_sb = part(16, len(FOUR) * P).rearrange("p (i n) -> p i n", i=len(FOUR))
        fm = {k: four_sb[:, i, :] for i, k in enumerate(FOUR)}
        qf = part(22, D)
        m12 = part(24, 2 * D).rearrange("p (i n) -> p i n", i=2)
        es = part(28, D)
        ee = part(30, D)
        rep1 = part(32, D)
        rep2 = part(34, D)
        wn = part(36, 2 * D).rearrange("p (s n) -> p s n", s=2)
        wT = part(40, D)
        vri = part(42, 2 * D).rearrange("p (i n) -> p i n", i=2)
        m4 = part(46, 4 * D).rearrange("p (i n) -> p i n", i=4)
        mx8 = part(54, 4 * 8)
        nx8 = part(54.25, 4 * 8)
        m9 = part(54.5, 4 * 8)
        wsum = part(54.75, 8)
        winv = part(55, 8)
        ctxT_sb = part(64, KD * B * L).rearrange("p (k n) -> p k n", k=KD)
        sz = part(80, 2 * KD * D).rearrange("p (i k n) -> p i k n", i=2, k=KD)
        weff = part(96, KD * D).rearrange("p (k n) -> p k n", k=KD)
        qw_sb = sb("qw_sb", [P, 1, D], I32)
        lora = part(104, 2 * D, 16).rearrange("p (i n) -> p i n", i=2)
        x2T = part(112, KD * B * L).rearrange("p (k n) -> p k n", k=KD)
        rtab = part(128, DEPTH * HT).rearrange("p (l t) -> p l t", l=DEPTH)
        ctab = part(136, DEPTH * (L + 1)).rearrange("p (l t) -> p l t", l=DEPTH)
        stab = part(138.25, DEPTH * (L + 1)).rearrange("p (l t) -> p l t", l=DEPTH)
        ttmp = part(140.5, DEPTH * P).rearrange("p (l t) -> p l t", l=DEPTH)
        tsm = sb("tsm", [P, 12, DEPTH])
        dh = part(144, B * DIM).rearrange("p (b c) -> p b c", b=B)
        dhc = part(146, B * DIM).rearrange("p (b c) -> p b c", b=B)
        dyn = part(148, 2 * HB * P).rearrange("p (h b c) -> p h b c", h=2, b=HB)
        dys = part(152, 2 * HT).rearrange("p (h t) -> p h t", h=2)
        dz = part(156, 2 * HT).rearrange("p (h t) -> p h t", h=2)
        df = part(160, 2 * 2 * HT).rearrange("p (h k t) -> p h k t", h=2, k=2)
        dw1_sb = part(168, DEPTH * DFF, DIM).rearrange("p (l f) -> p l f", l=DEPTH)
        dw2_sb = part(104, DEPTH * 2 * DIM).rearrange("p (l k o) -> p l k o", l=DEPTH, k=2)
        dwin_sb = part(106, KD * DIM).rearrange("p (k o) -> p k o", k=KD)
        dwout_sb = part(107, D, DIM)
        dsc = part(109, DEPTH * DIM).rearrange("p (l o) -> p l o", l=DEPTH)
        dst = sb("dst", [P, B, 6])
        dmv = sb("dmv", [P, B, 2])
        dve_ = sb("dve_", [P, B])
        drs = sb("drs", [P, B])
        KT = part(0, NKV * B * L).rearrange("p (g n) -> p g n", g=NKV)
        V = part(32, B * NKV * P).rearrange("p (b n) -> p b n", b=B)
        wk_sb = part(32, 2 * 512).rearrange("p (s n) -> p s n", s=2)
        wv_sb = part(80, KD * 1024).rearrange("p (k n) -> p k n", k=KD)
        qT = part(80, 2 * GQ * HT).rearrange("p (s j n) -> p s j n", s=2, j=GQ)
        pe_ = part(112, 2 * 512).rearrange("p (s n) -> p s n", s=2)
        pn = part(116, 512)
        pT = part(118, 2 * 512).rearrange("p (s n) -> p s n", s=2)
        wq_sb = part(108, 2 * 512).rearrange("p (s n) -> p s n", s=2)
        wo_sb = part(122, 3 * 512).rearrange("p (s n) -> p s n", s=3)
        amax = sb("amax", [P, 4])
        asum = sb("asum", [P, 2, 4])
        ainv = sb("ainv", [P, 4])
        ra_sb = part(0, KD * 136).rearrange("p (k n) -> p k n", k=KD)
        bw_sb = part(3, D)
        logits = part(6, 8)
        rt8 = part(6.25, 8)
        ri8 = sb("ri8", [P, 8], U32)
        rif = part(6.5, 8)
        rwt = part(6.75, 8)
        wh = part(7, P)
        whT = part(8, P)

        ls = {n: sem(n) for n in (
            "par_in", "row_in", "xtok_in", "wx_in", "xT_in", "w_in0", "w_in1", "w_in2", "w_in3",
            "bc_out", "b_in0", "b_in1", "b_in2", "b_in3", "c_in0", "c_in1", "c_in2", "c_in3", "wout_in",
            "ctxtok_in", "four_in", "ctxT_in", "sz_in", "qw_in", "lora_in", "dwt_in", "wk_in0", "wk_in1",
            "wv_in", "wq_in0", "wq_in1", "wo_in0", "wo_in1", "wo_in2", "ra_in", "stored",
            "dve_chain", "act_chain", "pool_chain",
            "pad_zero", "zero_done", "amat_done", "deq_done",
            "xs_hi", "xs_lo", "wi_hi", "wi_lo", "wq_hi", "wq_lo", "wo_hi", "wo_lo", "o_hi", "x4_hi", "x4_lo",
            "inproj", "in_evac", "conv_done", "u_done", "ssm_done", "ssm_sq", "ssm_ve", "ssm_rs", "ssm_norm",
            "ssmT_done", "ssmT_sb", "dt_proj", "dt_abs", "dt_exp", "dt_relu", "dt_w0", "dt_w", "dt_base", "dt_ln", "skip_done",
            "dt_done", "dtu_done", "dA_done", "bu_done", "scan_done", "prod_done", "ysum", "y_done",
            "wout_done",
            "x_sum", "ln_ve", "ln_rs", "x_done",
            "kf_done", "qf_done", "qf_sb", "m12_done", "corr", "es_done", "corr_read", "ee_done", "wn_done",
            "vf_done", "vri_sb", "wT_done", "wT_sb", "wf_done", "m4_done", "xat_done",
            "lora_done", "weff_done", "xTt", "xT_sb", "xbias", "ffn_done",
            "tab_a", "tab_b", "tab_c", "tab_d", "tab_done",
            "h0_done", "h0_read", "d_ve", "d_rs", "d_yn", "d_tr", "d_ys", "d_z", "d_conv", "d_hread", "d_yT",
            "d_f1", "d_f", "d_f2", "d_f2read", "d_out",
            "kv_ps", "kv_sb", "q_ps", "q_sb", "s_ps", "p_es", "p_exp", "p_norm", "t_ps", "t_sb",
            "av_ps", "o_sb", "op_ps",
            "r_ps", "r_wh", "wh_ps", "whT_done", "rf_ps",
        )}
        S = type("S", (), ls)

        block = ctx.enter_context(nc.Block())

        def lnc(stage, b):
            return stage * B + b + 1

        @block.sync
        def _(sp):
            def load(dst, src, s):
                sp.dma_start(dst, src).then_inc(s, 16)

            load(prm[:, :], par, S.par_in)
            for h in range(2):
                if h:
                    sp.wait_ge(S.y_done, MD)
                load(xTh, xT[h], S.xT_in)
                for m in range(16):
                    i = h * 16 + m
                    if m >= 4:
                        sp.wait_ge(S.wi_lo, i - 3)
                    load(wring[:, i % 4, :], win[m], (S.w_in0, S.w_in1, S.w_in2, S.w_in3)[i % 4])
                    if i == 1:
                        load(wx_sb, wx, S.wx_in)
                        load(wdt_sb, wdt, S.wx_in)
                        load(row[:, :], rows.partition_broadcast(P), S.row_in)
                        load(x_tok[:, :, :], xtok, S.xtok_in)
                sp.wait_ge(S.ssmT_sb, h + 1)
                sp.dma_start(scratch[h], ssmT[RK:SSM, :]).then_inc(S.bc_out, 16)
                sp.wait_ge(S.bc_out, 16 * (h + 1))
                for q in range(4):
                    for c, (dst, s) in enumerate(((Brep, (S.b_in0, S.b_in1, S.b_in2, S.b_in3)),
                                                  (Crep, (S.c_in0, S.c_in1, S.c_in2, S.c_in3)))):
                        src = scratch[h, c * NS + q * 4:c * NS + (q + 1) * 4, :]
                        load(dst[:, q * 4:(q + 1) * 4, :].rearrange("p n t -> p (n t)"),
                             src.rearrange("n t -> (n t)").partition_broadcast(P), s[q])
                for m in range(MD):
                    sp.wait_ge(S.y_done, h * MD + m + 1)
                    load(wout_sb[:, m, :], wout[m], S.wout_in)
            load(ctx_sb, ctxtok, S.ctxtok_in)
            load(four_sb, four, S.four_in)
            for i, t in enumerate((sc, ze)):
                for half in range(2):
                    load(sz[64 * half:64 * half + 64, i, :, :], t[half].partition_broadcast(64), S.sz_in)
            load(lora[:, 0, :], loraA, S.lora_in)
            load(lora[:, 1, :], loraBT, S.lora_in)
            load(ctxT_sb, ctxT, S.ctxT_in)
            for k in range(KD):
                if k:
                    sp.wait_ge(S.deq_done, k)
                load(qw_sb[:, 0, :], qw[k], S.qw_in)
            sp.wait_ge(S.weff_done, KD)
            load(dw2_sb, dw2, S.dwt_in)
            load(dwin_sb, dwin, S.dwt_in)
            load(dwout_sb, dwout, S.dwt_in)
            load(dw1_sb, dw1, S.dwt_in)
            load(wv_sb, wv, S.wv_in)
            for i in range(NKV):
                if i >= 2:
                    sp.wait_ge(S.kv_ps, 2 * (i - 1))
                load(wk_sb[:, i % 2, :], wk[i], (S.wk_in0, S.wk_in1)[i % 2])
            sp.wait_ge(S.d_out, 2 * HB)
            NT = 2 * NKV * GQ
            AHEAD = 6
            for i in range(NT + AHEAD):
                if i < NT:
                    if i >= 2:
                        sp.wait_ge(S.wq_lo, i - 1)
                    load(wq_sb[:, i % 2, :], wq[i // GQ % NKV, :, (i % GQ) * 512:(i % GQ + 1) * 512],
                         (S.wq_in0, S.wq_in1)[i % 2])
                o = i - AHEAD
                if o >= 0:
                    if o >= 3:
                        sp.wait_ge(S.wo_lo, o - 2)
                    load(wo_sb[:, o % 3, :], wo[o // GQ % NKV, :, o % GQ, :], (S.wo_in0, S.wo_in1, S.wo_in2)[o % 3])
            sp.wait_ge(S.s_ps, 2 * NKV * HB)
            load(ra_sb, ra, S.ra_in)
            load(bw_sb, bwT, S.ra_in)
            for b in range(B):
                sp.wait_ge(S.x_done, lnc(5, b))
                sp.dma_start(out[b], x_tok[:, b, :]).then_inc(S.stored, 16)
            sp.wait_ge(S.stored, 16 * B)

        @block.tensor
        def _(pe):
            mm = nc.tensor.matmul

            def mm3(o, l, r, start, stop):
                mm(o, l[0], r[0], start=start, stop=False)
                mm(o, l[0], r[1], start=False, stop=False)
                return mm(o, l[1], r[0], start=False, stop=stop)

            for h in range(2):
                for m in range(16):
                    i = h * 16 + m
                    pe.wait_ge(S.wi_lo, i + 1)
                    if i >= 2:
                        pe.wait_ge(S.in_evac, i - 1)
                    if h and m == 0:
                        pe.wait_ge(S.x_sum, lnc(0, HB - 1))
                    for k in range(KD):
                        if m == 0:
                            pe.wait_ge(S.xs_lo, h * KD + k + 1)
                        last = mm3(bank[m % 2][:, :], [osp[:, e, i % 3, k * P:(k + 1) * P] for e in range(2)],
                                   [xs[:, e, k, :] for e in range(2)], start=(k == 0), stop=(k == KD - 1))
                    last.then_inc(S.inproj, 1)
                pe.wait_ge(S.u_done, MD * (h + 1))
                pe.wait_ge(S.wx_in, 32)
                for b in range(HB):
                    for k in range(MD):
                        last = mm(bank[2][:, b * SSM:(b + 1) * SSM], u[:, k, b * L:(b + 1) * L], wx_sb[:, k, :],
                                  start=(k == 0), stop=(k == MD - 1))
                last.then_inc(S.ssm_done, 1)
                pe.wait_ge(S.ssm_norm, h + 1)
                for b in range(HB):
                    last = nc.tensor.transpose(bank[3][0:SSM, b * L:(b + 1) * L], ssmn[:, b, :], ident)
                last.then_inc(S.ssmT_done, 1)
                pe.wait_ge(S.ssmT_sb, h + 1)
                for m in range(MD):
                    i = h * MD + m
                    if m >= 4:
                        pe.wait_ge(S.dt_relu, i - 3)
                    last = mm(bank[4 + m % 4][:, :], wdt_sb[:, m * P:(m + 1) * P], ssmT[0:RK, :],
                              start=True, stop=True)
                    last.then_inc(S.dt_proj, 1)
                pe.wait_ge(S.dt_relu, MD * (h + 1))
                for m in range(MD):
                    if h * MD + m >= 2:
                        pe.wait_ge(S.y_done, h * MD + m - 1)
                    pe.wait_ge(S.skip_done, h * MD + m + 1)
                    mm(bank[6 + m % 2][:, :], skip[:, m % 2, :], u[:, m, :], start=True, stop=False)
                    for q in range(GS):
                        i = (h * MD + m) * GS + q
                        pe.wait_ge(S.prod_done, i + 1)
                        for n in range(NG):
                            last = mm(bank[6 + m % 2][:, :], ident, prod[:, i % 2, n, :],
                                      start=False, stop=(q == GS - 1 and n == NG - 1))
                        last.then_inc(S.ysum, 1)
                pe.wait_ge(S.y_done, MD * (h + 1))
                pe.wait_ge(S.wout_in, 16 * MD * (h + 1))
                for b in range(HB):
                    if b >= 2:
                        pe.wait_ge(S.x_sum, lnc(0, h * HB + b - 2))
                    for k in range(MD):
                        last = mm(bank[b % 2][:, :], g[:, k, b * L:(b + 1) * L], wout_sb[:, k, :],
                                  start=(k == 0), stop=(k == MD - 1))
                    last.then_inc(S.wout_done, 1)

            def spectra(b):
                if b == 0:
                    pe.wait_ge(S.ctxtok_in, 16)
                    pe.wait_ge(S.four_in, 16)
                    pe.wait_ge(S.x_sum, lnc(0, B - 1))
                    pe.wait_ge(S.y_done, 2 * MD)
                if b >= 1:
                    pe.wait_ge(S.m12_done, b)
                mm(bank[1][:, :], fm["q"], ctx_sb[:, b, :], start=True, stop=True)
                mm(bank[2][:, :], fm["k_swap"], ctx_sb[:, b, :], start=True, stop=True).then_inc(S.kf_done, 1)
                pe.wait_ge(S.x_done, lnc(0, b))
                mm(bank[0][:, :], fm["q"], x_tok[:, b, :], start=True, stop=True).then_inc(S.qf_done, 1)

            def correlate(b):
                pe.wait_ge(S.m12_done, b + 1)
                if b >= 1:
                    pe.wait_ge(S.corr_read, b)
                for t in range(KD):
                    o = bank[3][:, t * P:(t + 1) * P]
                    mm(o, m12[:, 0, t * P:(t + 1) * P], fm["c_re"], start=True, stop=False)
                    last = mm(o, m12[:, 1, t * P:(t + 1) * P], fm["c_im"], start=False, stop=True)
                last.then_inc(S.corr, 1)

            def weights(b):
                if b >= 1:
                    pe.wait_ge(S.m4_done, b)
                mm(bank[5][:, :], fm["v_re"], ctx_sb[:, b, :], start=True, stop=True)
                mm(bank[6][:, :], fm["v_im"], ctx_sb[:, b, :], start=True, stop=True).then_inc(S.vf_done, 1)
                pe.wait_ge(S.wn_done, b + 1)
                for t in range(KD):
                    last = nc.tensor.transpose(bank[4][:, t * P:(t + 1) * P], wn[:, b % 2, t * P:(t + 1) * P], ident)
                last.then_inc(S.wT_done, 1)
                pe.wait_ge(S.vri_sb, b + 1)
                pe.wait_ge(S.wT_sb, b + 1)
                mm(bank[5][:, :], fm["w_re"], wT, start=True, stop=True)
                mm(bank[6][:, :], fm["w_im"], wT, start=True, stop=True).then_inc(S.wf_done, 1)

            def aggregate(b):
                pe.wait_ge(S.m4_done, b + 1)
                if b >= 1:
                    pe.wait_ge(S.x_sum, lnc(1, b - 1))
                for i, k in enumerate(("o_rr", "o_ii", "o_ri", "o_ir")):
                    last = mm(bank[7][:, :], fm[k], m4[:, i, :], start=(i == 0), stop=(i == 3))
                last.then_inc(S.xat_done, 1)

            spectra(0)
            correlate(0)
            for b in range(B):
                if b + 1 < B:
                    spectra(b + 1)
                weights(b)
                if b + 1 < B:
                    correlate(b + 1)
                aggregate(b)

            def turn(stage, b, n, bk):
                pe.wait_ge(S.x_done, lnc(stage, b))
                if n >= 2:
                    pe.wait_ge(S.xT_sb, n - 1)
                for k in range(KD):
                    last = nc.tensor.transpose(bank[bk][:, k * P:(k + 1) * P], x_tok[:, b, k * P:(k + 1) * P], ident)
                last.then_inc(S.xTt, 1)

            pe.wait_ge(S.lora_in, 32)
            for k in range(KD):
                if k >= 1:
                    pe.wait_ge(S.weff_done, k)
                mm(bank[4][:, :], lora[:, 0, k * P:(k + 1) * P], lora[:, 1, :], start=True, stop=True).then_inc(S.lora_done, 1)
            turn(1, 0, 0, 0)
            for b in range(B):
                if b + 1 < B:
                    turn(1, b + 1, b + 1, (b + 1) % 2)
                pe.wait_ge(S.xT_sb, b + 1)
                pe.wait_ge(S.weff_done, KD)
                if b >= 2:
                    pe.wait_ge(S.x_sum, lnc(2, b - 2))
                for k in range(KD):
                    last = mm(bank[2 + b % 2][:, :], x2T[:, k, b * L:(b + 1) * L], weff[:, k, :],
                              start=(k == 0), stop=(k == KD - 1))
                last.then_inc(S.ffn_done, 1)

            turn(2, 0, B, 0)
            for b in range(B):
                if b + 1 < B:
                    turn(2, b + 1, B + b + 1, (b + 1) % 2)
                pe.wait_ge(S.xT_sb, B + b + 1)
                pe.wait_ge(S.dwt_in, 64)
                if b == 0:
                    pe.wait_ge(S.x_sum, lnc(2, B - 1))
                for k in range(KD):
                    last = mm(bank[4 + b // HB][:, (b % HB) * DIM:(b % HB + 1) * DIM],
                              x2T[:, k, b * L:(b + 1) * L], dwin_sb[:, k, :], start=(k == 0), stop=(k == KD - 1))
                if b % HB == HB - 1:
                    last.then_inc(S.h0_done, 1)
            pe.wait_ge(S.h0_read, 2)
            pe.wait_ge(S.tab_done, 1)
            pe.wait_ge(S.ctxT_in, 16)

            def keys_values(n):
                if n >= 4 * NKV:
                    return
                if n >= 2:
                    pe.wait_ge(S.kv_sb, n - 1)
                o = bank[3 + 4 * (n % 2)][:, :]
                if n < 2 * NKV:
                    gi, h = n // 2, n % 2
                    if h == 0:
                        pe.wait_ge((S.wk_in0, S.wk_in1)[gi % 2], 16 * (gi // 2 + 1))
                    for k in range(KD):
                        last = mm(o, wk_sb[:, gi % 2, k * P:(k + 1) * P], ctxT_sb[:, k, h * HT:(h + 1) * HT],
                                  start=(k == 0), stop=(k == KD - 1))
                else:
                    b, c = (n - 2 * NKV) // 2, n % 2
                    pe.wait_ge(S.wv_in, 16)
                    for k in range(KD):
                        last = mm(o, ctxT_sb[:, k, b * L:(b + 1) * L], wv_sb[:, k, c * 512:(c + 1) * 512],
                                  start=(k == 0), stop=(k == KD - 1))
                last.then_inc(S.kv_ps, 1)

            for l in range(DEPTH):
                for h in range(2):
                    pe.wait_ge(S.d_yn, 4 * l + h + 1)
                    for b in range(HB):
                        last = nc.tensor.transpose(bank[4 * h][:, b * L:(b + 1) * L], dyn[:, h, b, :], ident)
                    last.then_inc(S.d_tr, 1)
                    keys_values(KVL * l + h)
                for h in range(2):
                    pe.wait_ge(S.d_z, 2 * l + h + 1)
                    for b in range(HB):
                        last = mm(bank[4 * h + 1][:, b * DIM:(b + 1) * DIM], dz[:, h, b * L:(b + 1) * L], dsc[:, l, :],
                                  start=True, stop=True)
                    last.then_inc(S.d_conv, 1)
                    keys_values(KVL * l + 2 + h)
                for h in range(2):
                    pe.wait_ge(S.d_yn, 4 * l + 2 + h + 1)
                    for b in range(HB):
                        last = nc.tensor.transpose(bank[4 * h][0:DIM, b * L:(b + 1) * L], dyn[:, h, b, 0:DIM], ident)
                    last.then_inc(S.d_tr, 1)
                    keys_values(KVL * l + 4 + h)
                for h in range(2):
                    pe.wait_ge(S.d_yT, 2 * l + h + 1)
                    for k in range(2):
                        last = mm(bank[4 * h + 2 * k][:, :], dw1_sb[:, l, k * P:(k + 1) * P], dys[0:DIM, h, :],
                                  start=True, stop=True)
                    last.then_inc(S.d_f1, 1)
                for h in range(2):
                    pe.wait_ge(S.d_f, 2 * l + h + 1)
                    for b in range(HB):
                        for k in range(2):
                            last = mm(bank[4 * h + 1][:, b * DIM:(b + 1) * DIM], df[:, h, k, b * L:(b + 1) * L],
                                      dw2_sb[:, l, k, :], start=(k == 0), stop=(k == 1))
                    last.then_inc(S.d_f2, 1)
                    keys_values(KVL * l + 6 + h)
            for h in range(2):
                pe.wait_ge(S.d_yn, 4 * DEPTH + h + 1)
                for b in range(HB):
                    last = nc.tensor.transpose(bank[4 * h][0:DIM, b * L:(b + 1) * L], dyn[:, h, b, 0:DIM], ident)
                last.then_inc(S.d_tr, 1)
            for b in range(B):
                if b % HB == 0:
                    pe.wait_ge(S.d_yT, 2 * DEPTH + b // HB + 1)
                if b >= 2:
                    pe.wait_ge(S.x_sum, lnc(3, b - 2))
                mm(bank[2 + 4 * (b % 2)][:, :], dys[0:DIM, b // HB, (b % HB) * L:(b % HB + 1) * L], dwout_sb,
                   start=True, stop=True).then_inc(S.d_out, 1)

            pe.wait_ge(S.x_sum, lnc(3, B - 1))
            pe.wait_ge(S.kv_sb, 4 * NKV)
            NU = 2 * NKV

            def turn_half(h, b, bk):
                gb = h * HB + b
                pe.wait_ge(S.x_done, lnc(3, gb))
                if b >= 2:
                    pe.wait_ge(S.x4_lo, gb - 1)
                for k in range(KD):
                    last = nc.tensor.transpose(bank[bk][:, k * P:(k + 1) * P], x_tok[:, gb, k * P:(k + 1) * P], ident)
                last.then_inc(S.xTt, 1)

            for b in range(HB):
                turn_half(0, b, b % 2)

            def query(v, j):
                if v >= NU:
                    return
                n = v * GQ + j
                if v % NKV == 0 and j == 0:
                    pe.wait_ge(S.x4_lo, (v // NKV + 1) * HB)
                pe.wait_ge(S.wq_lo, n + 1)
                if n >= 1:
                    pe.wait_ge(S.q_sb, n)
                for k in range(KD):
                    last = mm3(bank[0][:, :], [wqs[:, e, n % 3, k * P:(k + 1) * P] for e in range(2)],
                               [xs[:, e, k, :] for e in range(2)], start=(k == 0), stop=(k == KD - 1))
                last.then_inc(S.q_ps, 1)

            for j in range(GQ):
                query(0, j)
            for s in range(NU * HB + 4):
                v, b = s // HB, s % HB
                if s < NU * HB:
                    pe.wait_ge(S.q_sb, (v + 1) * GQ)
                    if s >= 1:
                        pe.wait_ge(S.p_es, s)
                    gb = (v // NKV) * HB + b
                    for j in range(GQ):
                        last = mm(bank[1][:, j * P:(j + 1) * P], qT[:, v % 2, j, b * L:(b + 1) * L],
                                  KT[:, v % NKV, gb * L:(gb + 1) * L], start=True, stop=True)
                    last.then_inc(S.s_ps, 1)
                    if s == (NKV - 1) * HB:
                        for i in range(HB):
                            if i == 0:
                                pe.wait_ge(S.t_sb, s - 1)
                            turn_half(1, i, (2, 0)[i % 2])
                    query(v + 1, b)
                if 1 <= s <= NU * HB:
                    pe.wait_ge(S.p_norm, s)
                    if s >= 2:
                        pe.wait_ge(S.t_sb, s - 1)
                    for j in range(GQ):
                        last = nc.tensor.transpose(bank[2][:, j * P:(j + 1) * P], pn[:, j * P:(j + 1) * P], ident)
                    last.then_inc(S.t_ps, 1)
                if 2 <= s <= NU * HB + 1:
                    r = s - 2
                    rv, rb = r // HB, r % HB
                    pe.wait_ge(S.t_sb, r + 1)
                    if r >= 1:
                        pe.wait_ge(S.o_sb, r)
                    mm(bank[3][:, :], V[:, (rv // NKV) * HB + rb, (rv % NKV) * P:(rv % NKV + 1) * P], pT[:, r % 2, :],
                       start=True, stop=True).then_inc(S.av_ps, 1)
                if s >= 4:
                    r = s - 4
                    rv, rb = r // HB, r % HB
                    pe.wait_ge(S.o_sb, r + 1)
                    if rv == NKV:
                        pe.wait_ge(S.x_sum, lnc(4, rb))
                    for j in range(GQ):
                        pe.wait_ge(S.wo_lo, rv * GQ + j + 1)
                        last = mm3(bank[4 + rb][:, :], [osp[:, e, r % 3, j * P:(j + 1) * P] for e in range(2)],
                                   [wos[:, e, (rv * GQ + j) % 8, :] for e in range(2)],
                                   start=(rv % NKV == 0 and j == 0), stop=(rv % NKV == NKV - 1 and j == GQ - 1))
                    last.then_inc(S.op_ps, 1)

            pe.wait_ge(S.ra_in, 32)
            turn(4, 0, 2 * B, 0)
            for b in range(B):
                if b + 1 < B:
                    turn(4, b + 1, 2 * B + b + 1, (b + 1) % 2)
                pe.wait_ge(S.xT_sb, 2 * B + b + 1)
                if b >= 1:
                    pe.wait_ge(S.r_wh, b)
                for k in range(KD):
                    last = mm(bank[2][:, 0:136], x2T[:, k, b * L:(b + 1) * L], ra_sb[:, k, :],
                              start=(k == 0), stop=(k == KD - 1))
                last.then_inc(S.r_ps, 1)
                pe.wait_ge(S.r_wh, b + 1)
                nc.tensor.transpose(bank[3][:, 0:P], wh, ident).then_inc(S.wh_ps, 1)
                pe.wait_ge(S.whT_done, b + 1)
                if b >= 2:
                    pe.wait_ge(S.x_sum, lnc(5, b - 2))
                if b == 0:
                    pe.wait_ge(S.x_sum, lnc(4, B - 1))
                mm(bank[4 + b % 2][:, :], whT, bw_sb, start=True, stop=True).then_inc(S.rf_ps, 1)

        @block.scalar
        def _(act):
            def av(o, i, f, **k):
                return nc.scalar.activation(o, i, f, **k)

            chain = [0]

            def link(ins):
                chain[0] += 1
                ins.then_inc(S.act_chain, 1)
                act.wait_ge(S.act_chain, chain[0])

            act.wait_ge(S.par_in, 16)
            av(amat[:, :], pc("alog"), ACT.Exp).then_inc(S.amat_done, 1)
            act.wait_ge(S.tab_a, 1)
            av(tsm[:, 8, :], tsm[:, 7, :], ACT.Tanh).then_inc(S.tab_b, 1)
            def split_in(i):
                if i >= 32:
                    return
                act.wait_ge((S.w_in0, S.w_in1, S.w_in2, S.w_in3)[i % 4], 16 * (i // 4 + 1))
                if i >= 3:
                    act.wait_ge(S.inproj, i - 2)
                av(osp[:, 0, i % 3, :], wring[:, i % 4, :], ACT.Identity).then_inc(S.wi_hi, 1)

            for h in range(2):
                def silu_u(m):
                    act.wait_ge(S.conv_done, h * MD + m + 1)
                    av(u[:, m, :], conv[:, m % 2, :], ACT.Silu).then_inc(S.u_done, 1)

                if h:
                    act.wait_ge(S.y_done, MD)
                act.wait_ge(S.xT_in, 16 * (h + 1))
                for k in range(KD):
                    if k == 1:
                        split_in(h * 16)
                    av(xs[:, 0, k, :], xTh[:, k, :], ACT.Identity).then_inc(S.xs_hi, 1)
                split_in(h * 16 + 1)
                for m in range(16):
                    if m + 2 < 16:
                        split_in(h * 16 + m + 2)
                    act.wait_ge(S.inproj, h * 16 + m + 1)
                    if m < MD:
                        if m >= 2:
                            act.wait_ge(S.conv_done, h * MD + m - 1)
                        av(xpad[:, m % 2, :, CV - 1:], bank[m % 2][:, :].rearrange("p (b t) -> p b t", b=HB),
                           ACT.Identity).then_inc(S.in_evac, 1)
                        if m >= 1:
                            silu_u(m - 1)
                    else:
                        if m == MD:
                            silu_u(MD - 1)
                        av(g[:, m - MD, :], bank[m % 2][:, :], ACT.Silu).then_inc(S.in_evac, 1)
                act.wait_ge(S.ssm_done, h + 1)
                av(ssmsq, bank[2][:, 0:HB * SSM], ACT.Square).then_inc(S.ssm_sq, 1)
                act.wait_ge(S.ssmT_done, h + 1)
                av(ssmT[:, :], bank[3][0:SSM, :], ACT.Identity).then_inc(S.ssmT_sb, 1)
                def exp_dt(m):
                    act.wait_ge(S.dt_abs, h * MD + m + 1)
                    av(dt[:, m, :], dt[:, m, :], ACT.Exp, scale=-1.0).then_inc(S.dt_exp, 1)

                def ln_dt(m):
                    act.wait_ge(S.dt_w, h * MD + m + 1)
                    av(sp_w[:, m, :], sp_w[:, m, :], ACT.Ln).then_inc(S.dt_ln, 1)

                for m in range(MD):
                    act.wait_ge(S.dt_proj, h * MD + m + 1)
                    av(dt[:, m, :], bank[4 + m % 4][:, :], ACT.Abs, bias=pc("bdt")[:, m:m + 1]).then_inc(S.dt_abs, 1)
                    if 1 <= m <= EARLY:
                        exp_dt(m - 1)
                for m in range(EARLY):
                    ln_dt(m)
                act.wait_ge(S.dt_relu, MD * (h + 1))
                act.wait_ge(S.zero_done, 1)
                for m in range(MD):
                    if m >= 2:
                        act.wait_ge(S.ysum, (h * MD + m - 1) * GS)
                    av(skip[:, m % 2, :], ident, ACT.Identity, scale=pc("dskip")[:, m:m + 1]).then_inc(S.skip_done, 1)
                    for q in range(GS):
                        i = (h * MD + m) * GS + q
                        if q == 0:
                            act.wait_ge(S.dt_done, h * MD + m + 1)
                        if i >= 3:
                            act.wait_ge(S.prod_done, i - 2)
                        av(dA[:, i % 3, :, :].rearrange("p n (b t) -> p (n b) t", b=HB)[:, :, 0:1],
                           zeros[:, :].unsqueeze(2), ACT.Identity)
                        for n in range(NG):
                            c = m * NS + q * NG + n
                            last = av(dA[:, i % 3, n, :].rearrange("p (b t) -> p b t", b=HB)[:, :, 1:],
                                      dt[:, m, :].rearrange("p (b t) -> p b t", b=HB)[:, :, 1:],
                                      ACT.Exp, scale=amat[:, c:c + 1])
                        last.then_inc(S.dA_done, 1)
                        if m == 0 and q + EARLY < MD:
                            exp_dt(q + EARLY)
                    if m == 0:
                        for k in range(EARLY, MD):
                            ln_dt(k)

            def spectra(b):
                act.wait_ge(S.qf_done, b + 1)
                if b >= 1:
                    act.wait_ge(S.m12_done, b)
                av(qf, bank[0][:, :], ACT.Identity).then_inc(S.qf_sb, 1)

            def weights(b):
                act.wait_ge(S.es_done, b + 1)
                av(ee, es, ACT.Exp).then_inc(S.ee_done, 1)

            def products(b):
                act.wait_ge(S.vf_done, b + 1)
                if b >= 1:
                    act.wait_ge(S.m4_done, b)
                av(vri[:, 0, :], bank[5][:, :], ACT.Identity)
                av(vri[:, 1, :], bank[6][:, :], ACT.Identity).then_inc(S.vri_sb, 1)
                act.wait_ge(S.wT_done, b + 1)
                av(wT, bank[4][:, :], ACT.Identity).then_inc(S.wT_sb, 1)

            spectra(0)
            weights(0)
            for b in range(B):
                if b + 1 < B:
                    spectra(b + 1)
                products(b)
                if b + 1 < B:
                    weights(b + 1)

            def turned(b, n, bk):
                act.wait_ge(S.xTt, n + 1 if n < 2 * B else n + B + 1)
                av(x2T[:, :, b * L:(b + 1) * L], bank[bk][:, :].rearrange("p (k t) -> p k t", k=KD),
                   ACT.Identity).then_inc(S.xT_sb, 1)

            for b in range(B):
                turned(b, b, b % 2)
            for b in range(B):
                turned(b, B + b, b % 2)
            def keys_values(n):
                if n >= 4 * NKV:
                    return
                act.wait_ge(S.kv_ps, n + 1)
                o = bank[3 + 4 * (n % 2)][:, :]
                if n < 2 * NKV:
                    av(KT[:, n // 2, (n % 2) * HT:(n % 2 + 1) * HT], o, ACT.Identity,
                       bias=pc("bk")[:, n // 2:n // 2 + 1]).then_inc(S.kv_sb, 1)
                else:
                    b, c = (n - 2 * NKV) // 2, n % 2
                    av(V[:, b, c * 512:(c + 1) * 512], o, ACT.Identity).then_inc(S.kv_sb, 1)

            for l in range(DEPTH + 1):
                if l < DEPTH:
                    for h in range(2):
                        act.wait_ge(S.d_tr, 4 * l + h + 1)
                        av(dys[:, h, :], bank[4 * h][:, :], ACT.Silu, scale=pc("ln1w")[:, l:l + 1],
                           bias=pc("ln1b")[:, l:l + 1]).then_inc(S.d_ys, 1)
                        keys_values(KVL * l + h)
                    for h in range(2):
                        keys_values(KVL * l + 2 + h)
                wn_, bn_ = (pc("ln2w")[0:DIM, l:l + 1], pc("ln2b")[0:DIM, l:l + 1]) if l < DEPTH else \
                    (pc("lnlw")[0:DIM, :], pc("lnlb")[0:DIM, :])
                for h in range(2):
                    act.wait_ge(S.d_tr, 4 * l + (2 if l < DEPTH else 0) + h + 1)
                    av(dys[0:DIM, h, :], bank[4 * h][0:DIM, :], ACT.Identity, scale=wn_, bias=bn_).then_inc(S.d_yT, 1)
                    if l < DEPTH:
                        keys_values(KVL * l + 4 + h)
                if l < DEPTH:
                    for h in range(2):
                        act.wait_ge(S.d_f1, 2 * l + h + 1)
                        for k in range(2):
                            last = av(df[:, h, k, :], bank[4 * h + 2 * k][:, :], ACT.Silu,
                                      bias=pc("b1")[:, 2 * l + k:2 * l + k + 1])
                        last.then_inc(S.d_f, 1)
                    for h in range(2):
                        keys_values(KVL * l + 6 + h)
            NU = 2 * NKV

            def split_q(n):
                if n < NU * GQ:
                    act.wait_ge((S.wq_in0, S.wq_in1)[n % 2], 16 * (n // 2 + 1))
                    if n >= 3:
                        act.wait_ge(S.q_ps, n - 2)
                    av(wqs[:, 0, n % 3, :], wq_sb[:, n % 2, :], ACT.Identity).then_inc(S.wq_hi, 1)

            def split_o(n):
                act.wait_ge((S.wo_in0, S.wo_in1, S.wo_in2)[n % 3], 16 * (n // 3 + 1))
                if n >= 8:
                    act.wait_ge(S.op_ps, (n // GQ - 1) * HB)
                av(wos[:, 0, n % 8, :], wo_sb[:, n % 3, :], ACT.Identity).then_inc(S.wo_hi, 1)

            def turned_half(h, b, bk):
                gb = h * HB + b
                act.wait_ge(S.xTt, 2 * B + gb + 1)
                if h and b == 0:
                    act.wait_ge(S.q_ps, NKV * GQ)
                av(xs[:, 0, :, b * L:(b + 1) * L], bank[bk][:, :].rearrange("p (k t) -> p k t", k=KD),
                   ACT.Identity).then_inc(S.x4_hi, 1)

            for j in range(3):
                split_q(j)
            for b in range(HB):
                turned_half(0, b, b % 2)

            def query_out(v, j):
                if v >= NU:
                    return
                act.wait_ge(S.q_ps, v * GQ + j + 1)
                av(qT[:, v % 2, j, :], bank[0][:, :], ACT.Identity,
                   bias=pc("bq")[:, (v % NKV) * GQ + j:(v % NKV) * GQ + j + 1]).then_inc(S.q_sb, 1)

            for j in range(GQ):
                query_out(0, j)
                split_q(j + 3)
            for s in range(NU * HB + 2):
                v, b = s // HB, s % HB
                if s < NU * HB:
                    act.wait_ge(S.p_es, s + 1)
                    av(pe_[:, s % 2, :], pe_[:, s % 2, :], ACT.Exp, scale=SQ).then_inc(S.p_exp, 1)
                    if s == (NKV - 1) * HB:
                        for i in range(HB):
                            turned_half(1, i, (2, 0)[i % 2])
                    query_out(v + 1, b)
                    split_q((v + 1) * GQ + b + 3)
                    split_o(s)
                if 1 <= s <= NU * HB:
                    r = s - 1
                    act.wait_ge(S.t_ps, r + 1)
                    if r >= 2:
                        act.wait_ge(S.av_ps, r - 1)
                    av(pT[:, r % 2, :], bank[2][:, :], ACT.Identity).then_inc(S.t_sb, 1)
                if s >= 2:
                    r = s - 2
                    rv, rb = r // HB, r % HB
                    act.wait_ge(S.av_ps, r + 1)
                    if r >= 3:
                        act.wait_ge(S.op_ps, r - 2)
                    av(osp[:, 0, r % 3, :], bank[3][:, :], ACT.Identity,
                       bias=pc("bv")[:, rv % NKV:rv % NKV + 1]).then_inc(S.o_hi, 1)
            turned(0, 2 * B, 0)
            for b in range(B):
                if b + 1 < B:
                    turned(b + 1, 2 * B + b + 1, (b + 1) % 2)
                act.wait_ge(S.wh_ps, b + 1)
                if b >= 1:
                    act.wait_ge(S.rf_ps, b)
                av(whT, bank[3][:, 0:P], ACT.Identity).then_inc(S.whT_done, 1)

        def rstd(pool, stage, b):
            pool.wait_ge(S.ln_ve, lnc(stage, b))
            nc.gpsimd.tensor_tensor(lnrs[:, b:b + 1], lnve[:, b:b + 1], halfneg[:, 0:1], ALU.pow).then_inc(S.ln_rs, 1)

        @block.gpsimd
        def _(pool):
            gp = nc.gpsimd
            chain = [0]

            def link(ins):
                chain[0] += 1
                ins.then_inc(S.pool_chain, 1)
                pool.wait_ge(S.pool_chain, chain[0])

            def pad(h):
                gp.memset(xpad[:, :, :, 0:CV - 1], 0.0).then_inc(S.pad_zero, 1)

            link(gp.memset(halfneg[:, :], -0.5))
            pad(0)
            pool.wait_ge(S.tab_c, 1)
            gp.tensor_tensor(tsm[:, 5, :], tsm[:, 4, :], halfneg[:, 0:DEPTH], ALU.pow).then_inc(S.tab_d, 1)
            def rest_of(out_, whole, hi, ready, value, done):
                pool.wait_ge(ready, value)
                gp.tensor_tensor(out_, whole, hi.bitcast(F32), ALU.subtract).then_inc(done, 1)

            for h in range(2):
                if h:
                    pool.wait_ge(S.y_done, MD)
                    pad(1)
                for m in range(16):
                    i = h * 16 + m
                    rest_of(osp[:, 1, i % 3, :], wring[:, i % 4, :], osp[:, 0, i % 3, :], S.wi_hi, i + 1, S.wi_lo)
                pool.wait_ge(S.ssm_ve, h + 1)
                gp.tensor_tensor(ssm_rs[:, 0:3 * HB], ssm_ms[:, 0:3 * HB], halfneg[:, 0:3 * HB],
                                 ALU.pow).then_inc(S.ssm_rs, 1)

                def base(m):
                    pool.wait_ge(S.dt_relu, h * MD + m + 1)
                    pool.wait_ge(S.dt_w, h * MD + m + 1)
                    gp.tensor_tensor(sp_r[:, m, :], sp_r[:, m, :], dt[:, m, :], ALU.subtract).then_inc(S.dt_base, 1)

                for m in range(EARLY):
                    base(m)
                for m in range(MD):
                    pool.wait_ge(S.dtu_done, h * MD + m + 1)
                    for q in range(GS):
                        i = (h * MD + m) * GS + q
                        if m == 0 and q >= GS - (MD - EARLY):
                            base(q - GS + MD)
                        if m == 0:
                            pool.wait_ge((S.b_in0, S.b_in1, S.b_in2, S.b_in3)[q * NG // 4], 16 * (h + 1))
                        if i >= 2:
                            pool.wait_ge(S.scan_done, i - 1)
                        gp.tensor_tensor(bu[:, i % 2, :, :], dtu[:, m % 2, :].unsqueeze(1).to_broadcast([P, NG, HT]),
                                         Brep[:, q * NG:(q + 1) * NG, :], ALU.mult).then_inc(S.bu_done, 1)
                for b in range(h * HB, (h + 1) * HB):
                    rstd(pool, 0, b)
            pool.wait_ge(S.sz_in, 64)
            for k in range(KD):
                pool.wait_ge(S.qw_in, 16 * (k + 1))
                link(gp.tensor_copy(weff[:, k, :], qw_sb[:, 0, :]))
                link(gp.tensor_tensor(weff[:, k, :], weff[:, k, :], sz[:, 1, k, :], ALU.subtract))
                gp.tensor_tensor(weff[:, k, :], weff[:, k, :], sz[:, 0, k, :], ALU.mult).then_inc(S.deq_done, 1)
                if k < 2:
                    rstd(pool, 1, k)
            rest = [(1, b) for b in range(2, B)]
            for st, b in rest:
                rstd(pool, st, b)

            def bias(b, n, name):
                pool.wait_ge(S.xTt, n + 1)
                gp.tensor_tensor(x_tok[:, b, :], x_tok[:, b, :], rw(name), ALU.add).then_inc(S.xbias, 1)

            bias(0, 0, "fbias")
            for b in range(B):
                if b + 1 < B:
                    bias(b + 1, b + 1, "fbias")
                rstd(pool, 2, b)
            for b in range(B):
                bias(b, B + b, "bout")

            for i in range(2 * (2 * DEPTH + 1)):
                pool.wait_ge(S.d_ve, i + 1)
                h = i % 2
                gp.tensor_tensor(drs[:, h * HB:(h + 1) * HB], dve_[:, h * HB:(h + 1) * HB], halfneg[:, 0:HB],
                                 ALU.pow).then_inc(S.d_rs, 1)
            for b in range(B):
                rstd(pool, 3, b)
            def rest_q(n):
                if n < 2 * NKV * GQ:
                    rest_of(wqs[:, 1, n % 3, :], wq_sb[:, n % 2, :], wqs[:, 0, n % 3, :], S.wq_hi, n + 1, S.wq_lo)

            for n in range(3):
                rest_q(n)
            for b in range(HB):
                bias(b, 2 * B + b, "bo")
            for n in range(3, 7):
                rest_q(n)
            for s in range(2 * NKV * HB + 4):
                if s < 2 * NKV * HB:
                    rest_q(s + 7)
                    rest_of(wos[:, 1, s % 8, :], wo_sb[:, s % 3, :], wos[:, 0, s % 8, :], S.wo_hi, s + 1, S.wo_lo)
                if s == (NKV - 1) * HB:
                    for b in range(HB, B):
                        bias(b, 2 * B + b, "bo")
                u, b = (s - 4) // HB, (s - 4) % HB
                if u % NKV == NKV - 1 and s >= 4:
                    rstd(pool, 4, (u // NKV) * HB + b)
            for b in range(B):
                rstd(pool, 5, b)

        @block.vector
        def _(dve):
            v = nc.vector
            chain = [0]

            def link(ins):
                chain[0] += 1
                ins.then_inc(S.dve_chain, 1)
                dve.wait_ge(S.dve_chain, chain[0])

            def tables():
                pr, pi = pc("pre"), pc("pim")
                T = [tsm[:, i, :] for i in range(12)]
                z, m, a, b_, ssq, rsq, one, rmod, th, ta, tb, tc = T
                link(v.scalar_tensor_tensor(out=m, in0=pr, scalar=-1.0, in1=pr, op0=ALU.mult, op1=ALU.max))
                link(v.scalar_tensor_tensor(out=ta, in0=pi, scalar=-1.0, in1=pi, op0=ALU.mult, op1=ALU.max))
                link(v.tensor_tensor(m, m, ta, ALU.max))
                link(v.tensor_scalar(z, m, 0.0, None, ALU.is_equal))
                link(v.tensor_tensor(ta, m, z, ALU.add))
                link(v.reciprocal(tb, ta))
                link(v.tensor_tensor(a, pr, tb, ALU.mult))
                link(v.tensor_tensor(a, a, z, ALU.add))
                link(v.scalar_tensor_tensor(out=b_, in0=pi, scalar=-1.0, in1=tb, op0=ALU.mult, op1=ALU.mult))
                link(v.tensor_tensor(ta, a, a, ALU.mult))
                link(v.tensor_tensor(tb, b_, b_, ALU.mult))
                v.tensor_tensor(ssq, ta, tb, ALU.add).then_inc(S.tab_c, 1)
                dve.wait_ge(S.tab_d, 1)
                link(v.tensor_tensor(ta, ssq, rsq, ALU.mult))
                v.tensor_tensor(rmod, ta, m, ALU.mult).then_inc(S.tab_a, 1)
                link(v.tensor_tensor(a, a, rsq, ALU.mult))
                link(v.tensor_tensor(b_, b_, rsq, ALU.mult))
                link(v.tensor_tensor(ta, a, a, ALU.mult))
                link(v.tensor_tensor(tb, b_, b_, ALU.mult))
                link(v.tensor_tensor(ta, ta, tb, ALU.add))
                link(v.tensor_scalar(ta, ta, -0.5, 1.5, ALU.mult, ALU.add))
                link(v.tensor_tensor(a, a, ta, ALU.mult))
                link(v.tensor_tensor(b_, b_, ta, ALU.mult))
                dve.wait_ge(S.tab_b, 1)
                link(v.tensor_tensor(ta, th, a, ALU.mult))
                link(v.scalar_tensor_tensor(out=tb, in0=th, scalar=-1.0, in1=b_, op0=ALU.mult, op1=ALU.mult))
                lo, hi = slice(0, DIM), slice(DIM, P)
                lr, li = pc("lre"), pc("lim")
                link(v.tensor_tensor(tc[lo], tb[lo], li[lo], ALU.mult))
                link(v.tensor_tensor(one[lo], ta[lo], lr[lo], ALU.mult))
                link(v.tensor_tensor(z[lo], one[lo], tc[lo], ALU.subtract))
                link(v.tensor_tensor(tc[hi], tb[hi], lr[hi], ALU.mult))
                link(v.tensor_tensor(one[hi], ta[hi], li[hi], ALU.mult))
                link(v.tensor_tensor(z[hi], one[hi], tc[hi], ALU.add))
                return z, a, b_, th

            def big_tables(a, b_, th):
                link(v.memset(ctab[:, :, 0:1], 1.0))
                link(v.memset(stab[:, :, 0:1], 0.0))
                link(v.tensor_copy(ctab[:, :, 1:2], a.unsqueeze(2)))
                link(v.tensor_copy(stab[:, :, 1:2], b_.unsqueeze(2)))
                k = 1
                while k < L:
                    sh = [P, DEPTH, k]
                    cl, sl = ctab[:, :, 1:k + 1], stab[:, :, 1:k + 1]
                    ck, sk = ctab[:, :, k:k + 1].to_broadcast(sh), stab[:, :, k:k + 1].to_broadcast(sh)
                    cn, sn, tt = ctab[:, :, k + 1:2 * k + 1], stab[:, :, k + 1:2 * k + 1], ttmp[:, :, 0:k]
                    link(v.tensor_tensor(cn, cl, ck, ALU.mult))
                    link(v.tensor_tensor(tt, sl, sk, ALU.mult))
                    link(v.tensor_tensor(cn, cn, tt, ALU.subtract))
                    link(v.tensor_tensor(sn, sl, ck, ALU.mult))
                    link(v.tensor_tensor(tt, cl, sk, ALU.mult))
                    link(v.tensor_tensor(sn, sn, tt, ALU.add))
                    k *= 2
                link(v.tensor_copy(ctab[DIM:P, :, :], stab[DIM:P, :, :]))
                link(v.memset(rtab, 1.0))
                link(v.tensor_tensor(rtab, rtab, th.unsqueeze(2).to_broadcast([P, DEPTH, HT]), ALU.mult))
                link(v.memset(rtab.rearrange("p l (b t) -> p (l b) t", b=HB)[:, :, 0:1], 0.0))
                v.tensor_tensor(dsc, rw("scl").rearrange("p (l o) -> p l o", l=DEPTH),
                                pc("twoI").unsqueeze(1).to_broadcast([P, DEPTH, DIM]), ALU.mult).then_inc(S.tab_done, 1)
                dve.wait_ge(S.tab_done, 1)

            def ln_a(stage, b, ps, ready, value):
                dve.wait_ge(ready, value)
                if stage == 0:
                    dve.wait_ge(S.xtok_in, 16)
                bias_n = {2: b + 1, 3: B + b + 1, 4: 2 * B + b + 1}.get(stage)
                if bias_n:
                    dve.wait_ge(S.xbias, bias_n)
                v.tensor_tensor(x_tok[:, b, :], x_tok[:, b, :], ps, ALU.add).then_inc(S.x_sum, 1)
                dve.wait_ge(S.x_sum, lnc(stage, b))
                link(v.bn_stats(lnst[:, b, :], x_tok[:, b, :]))
                link(v.bn_aggr(lnmv[:, b, :], lnst[:, b, :]))
                v.tensor_scalar(lnve[:, b:b + 1], lnmv[:, b, 1:2], 1e-5, None, ALU.add).then_inc(S.ln_ve, 1)

            def ln_b(stage, b):
                dve.wait_ge(S.ln_rs, lnc(stage, b))
                v.tensor_scalar(x_tok[:, b, :], x_tok[:, b, :], lnmv[:, b, 0:1], lnrs[:, b:b + 1],
                                ALU.subtract, ALU.mult).then_inc(S.x_done, 1)

            v.memset(zeros[:, :], 0.0).then_inc(S.zero_done, 1)
            dve.wait_ge(S.par_in, 16)
            plc, a1, b1_, th1 = tables()
            dve.wait_ge(S.amat_done, 1)
            link(v.tensor_scalar(amat[:, :], amat[:, :], -1.0, None, ALU.mult))
            for h in range(2):
                for k in range(KD):
                    dve.wait_ge(S.xs_hi, h * KD + k + 1)
                    v.tensor_tensor(xs[:, 1, k, :], xTh[:, k, :], xs[:, 0, k, :].bitcast(F32),
                                    ALU.subtract).then_inc(S.xs_lo, 1)
                dve.wait_ge(S.pad_zero, h + 1)
                for m in range(MD):
                    dve.wait_ge(S.in_evac, h * 16 + m + 1)
                    if h * MD + m >= 2:
                        dve.wait_ge(S.u_done, h * MD + m - 1)
                    acc = conv[:, m % 2, :].rearrange("p (b t) -> p b t", b=HB)
                    w = pc("convw")[:, m * CV:(m + 1) * CV]
                    link(v.tensor_scalar(acc, xpad[:, m % 2, :, 0:L], w[:, 0:1], pc("convb")[:, m:m + 1],
                                         ALU.mult, ALU.add))
                    for j in range(1, CV):
                        ins = v.scalar_tensor_tensor(out=acc, in0=xpad[:, m % 2, :, j:j + L], scalar=w[:, j:j + 1],
                                                     in1=acc, op0=ALU.mult, op1=ALU.add)
                        if j < CV - 1:
                            link(ins)
                        else:
                            ins.then_inc(S.conv_done, 1)
                dve.wait_ge(S.ssm_sq, h + 1)
                link(v.tensor_reduce(ssm_ss[:, 0:4 * HB], ssmsq.rearrange("p (a c) -> p a c", c=NS), AX.X, ALU.add))
                ss = ssm_ss[:, 0:4 * HB].rearrange("p (b c) -> p b c", b=HB)
                ms = ssm_ms[:, 0:3 * HB].rearrange("p (b c) -> p b c", b=HB)
                rs = ssm_rs[:, 0:3 * HB].rearrange("p (b c) -> p b c", b=HB)
                link(v.tensor_tensor(ms[:, :, 0:1], ss[:, :, 0:1], ss[:, :, 1:2], ALU.add))
                link(v.tensor_scalar(ms[:, :, 0:1], ms[:, :, 0:1], 1.0 / RK, 1e-6, ALU.mult, ALU.add))
                v.tensor_scalar(ms[:, :, 1:3], ss[:, :, 2:4], 1.0 / NS, 1e-6, ALU.mult, ALU.add).then_inc(S.ssm_ve, 1)
                dve.wait_ge(S.ssm_rs, h + 1)
                pb = bank[2][:, 0:HB * SSM].rearrange("p (b c) -> p b c", b=HB)
                for i, (a, b_) in enumerate(((0, RK), (RK, RK + NS), (RK + NS, SSM))):
                    ins = v.tensor_tensor(ssmn[:, :, a:b_], pb[:, :, a:b_], rs[:, :, i:i + 1].to_broadcast([P, HB, b_ - a]),
                                          ALU.mult)
                    if i < 2:
                        link(ins)
                    else:
                        ins.then_inc(S.ssm_norm, 1)
                for m in range(MD):
                    dve.wait_ge(S.dt_abs, h * MD + m + 1)
                    v.tensor_scalar(sp_r[:, m, :], bank[4 + m % 4][:, :], pc("bdt")[:, m:m + 1], 0.0,
                                    ALU.add, ALU.max).then_inc(S.dt_relu, 1)

                def one_plus(m):
                    dve.wait_ge(S.dt_exp, h * MD + m + 1)
                    v.tensor_scalar(sp_w[:, m, :], dt[:, m, :], 1.0, None, ALU.add).then_inc(S.dt_w0, 1)
                    dve.wait_ge(S.dt_w0, h * MD + m + 1)
                    v.scalar_tensor_tensor(out=dt[:, m, :], in0=sp_w[:, m, :], scalar=1.0, in1=dt[:, m, :],
                                           op0=ALU.subtract, op1=ALU.subtract).then_inc(S.dt_w, 1)

                def step_size(m):
                    dve.wait_ge(S.dt_ln, h * MD + m + 1)
                    dve.wait_ge(S.dt_base, h * MD + m + 1)
                    v.tensor_tensor(dt[:, m, :], sp_r[:, m, :], sp_w[:, m, :], ALU.add).then_inc(S.dt_done, 1)

                def step_in(m):
                    if h * MD + m >= 2:
                        dve.wait_ge(S.bu_done, (h * MD + m - 1) * GS)
                    dve.wait_ge(S.dt_done, h * MD + m + 1)
                    v.tensor_tensor(dtu[:, m % 2, :], dt[:, m, :], u[:, m, :], ALU.mult).then_inc(S.dtu_done, 1)

                def c_times(i):
                    q = i % GS
                    if (i // GS) % MD == 0:
                        dve.wait_ge((S.c_in0, S.c_in1, S.c_in2, S.c_in3)[q * NG // 4], 16 * (h + 1))
                    if i >= 2:
                        dve.wait_ge(S.ysum, i - 1)
                    dve.wait_ge(S.scan_done, i + 1)
                    v.tensor_tensor(prod[:, i % 2, :, :], dA[:, i % 3, :, :], Crep[:, q * NG:(q + 1) * NG, :],
                                    ALU.mult).then_inc(S.prod_done, 1)

                def scan(i):
                    dve.wait_ge(S.dA_done, i + 1)
                    dve.wait_ge(S.bu_done, i + 1)
                    d = dA[:, i % 3, :, :].rearrange("p n t -> p (n t)")
                    v.tensor_tensor_scan(d, d, bu[:, i % 2, :, :].rearrange("p n t -> p (n t)"), 0.0,
                                         ALU.mult, ALU.add).then_inc(S.scan_done, 1)

                def finish_y(m):
                    dve.wait_ge(S.ysum, (h * MD + m + 1) * GS)
                    v.tensor_tensor(g[:, m, :], bank[6 + m % 2][:, :], g[:, m, :], ALU.mult).then_inc(S.y_done, 1)

                for m in range(EARLY):
                    one_plus(m)
                step_size(0)
                step_in(0)
                step_size(1)
                scan(h * MD * GS)
                for m in range(MD):
                    for q in range(GS):
                        i = (h * MD + m) * GS + q
                        if i + 1 < (h + 1) * MD * GS:
                            scan(i + 1)
                        if m == 0 and q + EARLY < MD:
                            one_plus(q + EARLY)
                        if q == 1 and 1 <= m < MD - 1:
                            step_size(m + 1)
                        if q == 3 and m + 1 < MD:
                            step_in(m + 1)
                        if q == 5 and m >= 1:
                            finish_y(m - 1)
                        c_times(i)
                finish_y(MD - 1)
                for b in range(h * HB, (h + 1) * HB):
                    ln_a(0, b, bank[b % 2][:, :], S.wout_done, b + 1)
                    if b > h * HB:
                        ln_b(0, b - 1)
                ln_b(0, (h + 1) * HB - 1)

            link(v.memset(m9, -BIG))

            def spectra(b):
                dve.wait_ge(S.qf_sb, b + 1)
                dve.wait_ge(S.kf_done, b + 1)
                if b >= 1:
                    dve.wait_ge(S.corr, b)
                v.tensor_tensor(m12[:, 0, :], qf, bank[1][:, :], ALU.mult)
                v.tensor_tensor(m12[:, 1, :], qf, bank[2][:, :], ALU.mult).then_inc(S.m12_done, 1)

            def topk(b):
                dve.wait_ge(S.corr, b + 1)
                cor = bank[3][:, :]
                for t in range(KD):
                    o = slice(t * P, (t + 1) * P)
                    last = v.max(mx8[:, t * 8:t * 8 + 8], cor[:, o])
                link(last)
                v.tensor_tensor(es.rearrange("p (t n) -> p t n", t=KD), cor.rearrange("p (t n) -> p t n", t=KD),
                                mx8.rearrange("p (t n) -> p t n", t=KD)[:, :, 0:1].to_broadcast([P, KD, P]),
                                ALU.subtract).then_inc(S.es_done, 1)
                for t in range(KD):
                    o = slice(t * P, (t + 1) * P)
                    last = v.match_replace(rep1[:, o], mx8[:, t * 8:t * 8 + 8], cor[:, o], -BIG)
                last.then_inc(S.corr_read, 1)
                dve.wait_ge(S.corr_read, b + 1)
                for t in range(KD):
                    last = v.max(nx8[:, t * 8:t * 8 + 8], rep1[:, t * P:(t + 1) * P])
                link(last)
                link(v.tensor_copy(m9.rearrange("p (t n) -> p t n", t=KD)[:, :, 0:TOPK - 8],
                                   nx8.rearrange("p (t n) -> p t n", t=KD)[:, :, 0:TOPK - 8]))
                for t in range(KD):
                    o = slice(t * P, (t + 1) * P)
                    last = v.match_replace(rep2[:, o], m9[:, t * 8:t * 8 + 8], rep1[:, o], -BIG)
                link(last)
                dve.wait_ge(S.ee_done, b + 1)
                link(v.scalar_tensor_tensor(out=rep2, in0=rep2, scalar=-BIG, in1=ee, op0=ALU.is_equal, op1=ALU.mult))
                link(v.tensor_reduce(wsum[:, 0:KD], rep2.rearrange("p (t n) -> p t n", t=KD), AX.X, ALU.add))
                link(v.reciprocal(winv[:, 0:KD], wsum[:, 0:KD]))
                if b >= 2:
                    dve.wait_ge(S.wT_done, b - 1)
                v.tensor_tensor(wn[:, b % 2, :].rearrange("p (t n) -> p t n", t=KD),
                                rep2.rearrange("p (t n) -> p t n", t=KD),
                                winv[:, 0:KD].unsqueeze(2).to_broadcast([P, KD, P]), ALU.mult).then_inc(S.wn_done, 1)

            def products(b):
                dve.wait_ge(S.wf_done, b + 1)
                dve.wait_ge(S.vri_sb, b + 1)
                if b >= 1:
                    dve.wait_ge(S.xat_done, b)
                v.tensor_tensor(m4[:, 0, :], vri[:, 0, :], bank[5][:, :], ALU.mult)
                v.tensor_tensor(m4[:, 2, :], vri[:, 1, :], bank[5][:, :], ALU.mult)
                v.tensor_tensor(m4[:, 1, :], vri[:, 1, :], bank[6][:, :], ALU.mult)
                v.tensor_tensor(m4[:, 3, :], vri[:, 0, :], bank[6][:, :], ALU.mult).then_inc(S.m4_done, 1)

            spectra(0)
            topk(0)
            for b in range(B):
                if b + 1 < B:
                    spectra(b + 1)
                if b >= 1:
                    ln_a(1, b - 1, bank[7][:, :], S.xat_done, b)
                products(b)
                if b >= 1:
                    ln_b(1, b - 1)
                if b + 1 < B:
                    topk(b + 1)
            ln_a(1, B - 1, bank[7][:, :], S.xat_done, B)
            ln_b(1, B - 1)
            for k in range(KD):
                dve.wait_ge(S.lora_done, k + 1)
                dve.wait_ge(S.deq_done, k + 1)
                v.scalar_tensor_tensor(out=weff[:, k, :], in0=bank[4][:, :], scalar=1.0 / 16, in1=weff[:, k, :],
                                       op0=ALU.mult, op1=ALU.add).then_inc(S.weff_done, 1)
            for b in range(B):
                ln_a(2, b, bank[2 + b % 2][:, :], S.ffn_done, b + 1)
                if b >= 1:
                    ln_b(2, b - 1)
            ln_b(2, B - 1)
            big_tables(a1, b1_, th1)
            for h in range(2):
                dve.wait_ge(S.h0_done, h + 1)
                hs = slice(h * HB, (h + 1) * HB)
                v.tensor_tensor(dh[:, hs, :], bank[4 + h][:, 0:HB * DIM].rearrange("p (b c) -> p b c", b=HB),
                                rw("bin").unsqueeze(1).to_broadcast([P, HB, DIM]), ALU.add).then_inc(S.h0_read, 1)
            dve.wait_ge(S.h0_read, 2)

            def stats(h):
                for b in range(h * HB, (h + 1) * HB):
                    last = v.bn_stats(dst[:, b, :], dh[:, b, :])
                link(last)
                for b in range(h * HB, (h + 1) * HB):
                    last = v.bn_aggr(dmv[:, b, :], dst[:, b, :])
                link(last)
                hs = slice(h * HB, (h + 1) * HB)
                v.tensor_scalar(dve_[:, hs], dmv[:, hs, 1:2].rearrange("p b o -> p (b o)"), 1e-5, None,
                                ALU.add).then_inc(S.d_ve, 1)
                link(v.tensor_tensor(dhc[:, hs, :], dh[:, hs, :], dmv[:, hs, 0:1].to_broadcast([P, HB, DIM]),
                                     ALU.subtract))

            def norm(n, h, copies, free):
                dve.wait_ge(S.d_rs, n)
                if free:
                    dve.wait_ge(S.d_tr, free)
                hs = slice(h * HB, (h + 1) * HB)
                for c in range(copies):
                    last = v.tensor_tensor(dyn[:, h, :, c * DIM:(c + 1) * DIM], dhc[:, hs, :],
                                           drs[:, hs].unsqueeze(2).to_broadcast([P, HB, DIM]), ALU.mult)
                last.then_inc(S.d_yn, 1)

            for l in range(DEPTH):
                for h in range(2):
                    stats(h)
                for h in range(2):
                    norm(4 * l + h + 1, h, 2, 4 * l)
                for h in range(2):
                    dve.wait_ge(S.d_ys, 2 * l + h + 1)
                    if l:
                        dve.wait_ge(S.d_conv, 2 * l)
                    z3 = dz[:, h, :].rearrange("p (b t) -> p b t", b=HB)
                    tab = ctab[:, l, 0:L].unsqueeze(1).to_broadcast([P, HB, L])
                    link(v.tensor_tensor(z3, dys[:, h, :].rearrange("p (b t) -> p b t", b=HB), tab, ALU.mult))
                    link(v.tensor_scalar(z3[:, :, 0:1], z3[:, :, 0:1], plc[:, l:l + 1], None, ALU.add))
                    link(v.tensor_tensor_scan(dz[:, h, :], rtab[:, l, :], dz[:, h, :], 0.0, ALU.mult, ALU.add))
                    v.tensor_tensor(z3, z3, tab, ALU.mult).then_inc(S.d_z, 1)
                for h in range(2):
                    hs = slice(h * HB, (h + 1) * HB)
                    dve.wait_ge(S.d_conv, 2 * l + h + 1)
                    v.tensor_tensor(dh[:, hs, :], dh[:, hs, :],
                                    bank[4 * h + 1][:, 0:HB * DIM].rearrange("p (b c) -> p b c", b=HB),
                                    ALU.add).then_inc(S.d_hread, 1)
                    dve.wait_ge(S.d_hread, 2 * l + h + 1)
                    stats(h)
                for h in range(2):
                    norm(4 * l + 2 + h + 1, h, 1, 4 * l + 2)
                for h in range(2):
                    hs = slice(h * HB, (h + 1) * HB)
                    link(v.tensor_tensor(dh[:, hs, :], dh[:, hs, :],
                                         rw("b2")[:, l * DIM:(l + 1) * DIM].unsqueeze(1).to_broadcast([P, HB, DIM]),
                                         ALU.add))
                    dve.wait_ge(S.d_f2, 2 * l + h + 1)
                    v.tensor_tensor(dh[:, hs, :], dh[:, hs, :],
                                    bank[4 * h + 1][:, 0:HB * DIM].rearrange("p (b c) -> p b c", b=HB),
                                    ALU.add).then_inc(S.d_f2read, 1)
                    dve.wait_ge(S.d_f2read, 2 * l + h + 1)
            for h in range(2):
                stats(h)
            for h in range(2):
                norm(4 * DEPTH + h + 1, h, 1, 4 * DEPTH)
            for b in range(B):
                ln_a(3, b, bank[2 + 4 * (b % 2)][:, :], S.d_out, b + 1)
                if b >= 1:
                    ln_b(3, b - 1)
            ln_b(3, B - 1)
            NU = 2 * NKV
            sh = [P, GQ, P]

            def soft_a(s):
                dve.wait_ge(S.s_ps, s + 1)
                ps = bank[1][:, :].rearrange("p (j m) -> p j m", j=GQ)
                link(v.tensor_reduce(amax[:, :], ps, AX.X, ALU.max))
                if s >= 2:
                    dve.wait_ge(S.p_norm, s - 1)
                v.tensor_tensor(pe_[:, s % 2, :].rearrange("p (j m) -> p j m", j=GQ), ps,
                                amax[:, :].unsqueeze(2).to_broadcast(sh), ALU.subtract).then_inc(S.p_es, 1)

            def soft_b(s):
                dve.wait_ge(S.p_exp, s + 1)
                pr = pe_[:, s % 2, :].rearrange("p (j m) -> p j m", j=GQ)
                link(v.tensor_reduce(asum[:, 0, :], pr, AX.X, ALU.add))
                link(v.reciprocal(ainv[:, :], asum[:, 0, :]))
                if s >= 1:
                    dve.wait_ge(S.t_ps, s)
                v.tensor_tensor(pn.rearrange("p (j m) -> p j m", j=GQ), pr, ainv[:, :].unsqueeze(2).to_broadcast(sh),
                                ALU.mult).then_inc(S.p_norm, 1)

            def x_rest(h, b, bk):
                dve.wait_ge(S.x4_hi, h * HB + b + 1)
                o = slice(b * L, (b + 1) * L)
                v.tensor_tensor(xs[:, 1, :, o], bank[bk][:, :].rearrange("p (k t) -> p k t", k=KD),
                                xs[:, 0, :, o].bitcast(F32), ALU.subtract).then_inc(S.x4_lo, 1)

            def o_rest(r):
                dve.wait_ge(S.o_hi, r + 1)
                u = r // HB % NKV
                v.scalar_tensor_tensor(out=osp[:, 1, r % 3, :], in0=bank[3][:, :], scalar=pc("bv")[:, u:u + 1],
                                       in1=osp[:, 0, r % 3, :].bitcast(F32), op0=ALU.add,
                                       op1=ALU.subtract).then_inc(S.o_sb, 1)

            for b in range(HB):
                x_rest(0, b, b % 2)
            for s in range(NU * HB + 4):
                if s < NU * HB:
                    soft_a(s)
                    if s == (NKV - 1) * HB:
                        for b in range(HB):
                            x_rest(1, b, (2, 0)[b % 2])
                    soft_b(s)
                if 2 <= s <= NU * HB + 1:
                    o_rest(s - 2)
                if s >= 4:
                    r = s - 4
                    rv, rb = r // HB, r % HB
                    if rv % NKV == NKV - 1:
                        b = (rv // NKV) * HB + rb
                        ln_a(4, b, bank[4 + rb][:, :], S.op_ps, r + 1)
                        ln_b(4, b)
            for b in range(B):
                dve.wait_ge(S.r_ps, b + 1)
                link(v.tensor_copy(logits, bank[2][:, P:P + 8]))
                link(v.max(rt8, logits))
                link(v.max_index(ri8[:, :], rt8, logits))
                link(v.tensor_copy(rif, ri8[:, :]))
                link(v.tensor_scalar(rwt, pc("iota8"), rif[:, 0:1], rt8[:, 0:1], ALU.is_equal, ALU.mult))
                if b >= 1:
                    dve.wait_ge(S.wh_ps, b)
                v.tensor_tensor(wh.rearrange("p (e r) -> p e r", e=8), bank[2][:, 0:P].rearrange("p (e r) -> p e r", e=8),
                                rwt.unsqueeze(2).to_broadcast([P, 8, 16]), ALU.mult).then_inc(S.r_wh, 1)
                if b >= 1:
                    ln_a(5, b - 1, bank[4 + (b - 1) % 2][:, :], S.rf_ps, b)
                    ln_b(5, b - 1)
            ln_a(5, B - 1, bank[4 + (B - 1) % 2][:, :], S.rf_ps, B)
            ln_b(5, B - 1)


def kernel(**inp):
    import concourse.bacc as bacc
    from concourse.bass_utils import run_bass_kernel_spmd

    a = {k: np.asarray(v) for k, v in inp.items()}
    cat = np.concatenate

    def cols(v):
        return v.reshape(-1, P).T

    def twice(v):
        return cat([v.T, v.T], 0)

    x, ctx = a["x"], a["ctx_4096"]
    xT = x.reshape(2, HT, KD, P).transpose(0, 3, 2, 1)
    bkv = a["L1_xattn_bkv"]
    vals = {
        "convw": a["L0_attn_conv_w"].reshape(MD, P, CV).transpose(1, 0, 2).reshape(P, MD * CV),
        "convb": cols(a["L0_attn_conv_b"]), "bdt": cols(a["L0_attn_b_dt"]),
        "alog": a["L0_attn_A_log"].reshape(MD, P, NS).transpose(1, 0, 2).reshape(P, MD * NS),
        "dskip": cols(a["L0_attn_D"]), "bq": cols(a["L1_xattn_bq"]),
        "bk": cols(bkv[:1024]), "bv": cols(bkv[1024:]),
        "ln1w": twice(a["L1_attn_ln1_w"]), "ln1b": twice(a["L1_attn_ln1_b"]),
        "ln2w": twice(a["L1_attn_ln2_w"]), "ln2b": twice(a["L1_attn_ln2_b"]),
        "lnlw": twice(a["L1_attn_lnl_w"][None]), "lnlb": twice(a["L1_attn_lnl_b"][None]),
        "b1": cols(a["L1_attn_b1"].reshape(-1)),
        "pre": twice(a["L1_attn_phz_re"]), "pim": twice(a["L1_attn_phz_im"]),
        "lre": twice(a["L1_attn_lc_re"]), "lim": twice(a["L1_attn_lc_im"]),
        "ident": np.eye(P, dtype=np.float32), "twoI": cat([np.eye(DIM, dtype=np.float32)] * 2, 0),
        "iota8": np.tile(np.arange(8, dtype=np.float32), (P, 1)),
    }
    par = cat([vals[n] for n, _ in _COLS], 1)
    rvals = {"fbias": a["L0_ffn_bias"], "bout": a["L1_attn_bout"], "bo": a["L1_xattn_bo"], "bin": a["L1_attn_bin"],
             "b2": a["L1_attn_b2"].reshape(-1), "scl": a["L1_attn_sc_lin"].reshape(-1)}
    wkv = a["L1_xattn_Wkv"]

    def groups(s):
        return s.T.reshape(KD, 2, D).transpose(1, 0, 2)

    arrays = {
        "xT": xT, "xtok": x.transpose(1, 0, 2),
        "ctxT": ctx.reshape(B * L, KD, P).transpose(2, 1, 0), "ctxtok": ctx.transpose(1, 0, 2),
        "par": par, "rows": cat([rvals[n] for n, _ in _ROWS]), "four": fourier(),
        "win": a["L0_attn_W_in"].reshape(16, P, KD, P).transpose(0, 3, 2, 1).reshape(16, P, 512),
        "wx": a["L0_attn_W_x"].reshape(SSM, MD, P).transpose(2, 1, 0),
        "wdt": a["L0_attn_W_dt"].T, "wout": a["L0_attn_W_out"].T.reshape(MD, P, D),
        "qw": a["L0_ffn_qweight"].T.reshape(KD, P, D), "sc": groups(a["L0_ffn_scales"]),
        "ze": groups(a["L0_ffn_zeros"]), "loraA": a["L0_ffn_lora_A"], "loraBT": a["L0_ffn_lora_B"].T,
        "dwin": a["L1_attn_Win"].reshape(DIM, KD, P).transpose(2, 1, 0),
        "dw1": a["L1_attn_W1"].transpose(2, 0, 1),
        "dw2": a["L1_attn_W2"].reshape(DEPTH, DIM, 2, P).transpose(3, 0, 2, 1),
        "dwout": a["L1_attn_Wout"].T,
        "wq": a["L1_xattn_Wq"].reshape(KD, P, NKV, GQ, P).transpose(2, 1, 3, 0, 4).reshape(NKV, P, GQ * 512),
        "wk": wkv[:, :1024].reshape(KD, P, NKV, P).transpose(2, 1, 0, 3).reshape(NKV, P, 512),
        "wv": wkv[:, 1024:].reshape(KD, P, 1024).transpose(1, 0, 2),
        "wo": a["L1_xattn_Wo"].reshape(NKV, GQ, P, D).transpose(0, 2, 1, 3),
        "ra": cat([a["L1_ffn_A"].reshape(P, D), a["L1_ffn_route_w"]], 0).T.reshape(KD, P, P + 8).transpose(1, 0, 2),
        "bwT": a["L1_ffn_Bw"].transpose(0, 2, 1).reshape(P, D),
    }
    arrays = {k: np.ascontiguousarray(v) for k, v in arrays.items()}
    nc = bacc.Bacc("TRN2", target_bir_lowering=False, num_devices=1)
    args = [nc.dram_tensor(n, v.shape, mybir.dt.from_np(v.dtype), kind="ExternalInput").ap() for n, v in arrays.items()]
    args.append(nc.dram_tensor("out", (B, L, D), F32, kind="ExternalOutput").ap())
    decoder_kernel(nc, *args)
    r = run_bass_kernel_spmd(nc, [arrays], core_ids=[0])
    return r.results[0]["out"]
```

```python
from contextlib import ExitStack

import numpy as np

import concourse.bass as bass
from concourse import mybir

F32 = mybir.dt.float32
F32R = mybir.dt.float32r
I32 = mybir.dt.int32
U32 = mybir.dt.uint32
ALU = mybir.AluOpType
ACT = mybir.ActivationFunctionType
AX = mybir.AxisListType

P = 128
B = 8
L = 128
D = 512
KD = D // P
HB = B // 2
HT = HB * L
DI = 1024
MD = DI // P
NS = 16
NG = 2
GS = NS // NG
RK = 32
SSM = RK + 2 * NS
CV = 4
DEPTH, DIM, DFF = 4, 64, 256
XP_AT, BACK_AT, TR_AT, DT_AT = 10, 11, 13, 14
ROUTED_FROM = 40
EARLY = 2
KVL = 8
KV_EMPTY = (1 + 1 * KVL + 5, 1 + 2 * KVL + 5)
NKV, GQ = 8, 4
TOPK = int(2 * np.log(L))
BIG = 3.0e38
SQ = float(1.0 / np.sqrt(128.0))

_COLS = [("convw", MD * CV), ("convb", MD), ("bdt", MD), ("alog", MD * NS), ("dskip", MD),
         ("bq", NKV * GQ), ("bk", NKV), ("bv", NKV), ("ln1w", DEPTH), ("ln1b", DEPTH),
         ("ln2w", DEPTH), ("ln2b", DEPTH), ("lnlw", 1), ("lnlb", 1), ("b1", DEPTH * 2),
         ("pre", DEPTH), ("pim", DEPTH), ("lre", DEPTH), ("lim", DEPTH), ("ident", P),
         ("twoI", DIM), ("iota8", 8)]
COL = {}
_at = 0
for _n, _w in _COLS:
    COL[_n] = (_at, _at + _w)
    _at += _w
NPAR = _at
_ROWS = [("fbias", D), ("bout", D), ("bo", D), ("bin", DIM), ("b2", DEPTH * DIM), ("scl", DEPTH * DIM)]
ROW = {}
_at = 0
for _n, _w in _ROWS:
    ROW[_n] = (_at, _at + _w)
    _at += _w
NROW = _at
FOUR = ["q", "k_swap", "c_re", "c_im", "w_re", "w_im", "v_re", "v_im", "o_rr", "o_ii", "o_ri", "o_ir"]


def fourier():
    n = np.arange(L)[:, None].astype(np.float64)
    m = {}
    f = np.arange(64)[None, :]
    re, im = np.cos(2 * np.pi * n * f / L), -np.sin(2 * np.pi * n * f / L)
    im[:, 0] = np.cos(np.pi * n[:, 0])
    m["q"] = np.concatenate([re, im], 1)
    m["k_swap"] = np.concatenate([im, re], 1)
    t = np.arange(L)[None, :]
    fc = np.arange(64)[:, None]
    w = np.where(fc == 0, 1.0, 2.0) / L
    cos, sin = w * np.cos(2 * np.pi * fc * t / L), w * np.sin(2 * np.pi * fc * t / L)
    lower = cos.copy()
    lower[0] = np.cos(np.pi * t[0]) / L
    m["c_re"] = np.concatenate([cos, lower], 0)
    m["c_im"] = np.concatenate([sin * (fc > 0), -sin * (fc > 0)], 0)
    f = np.arange(128)[None, :]
    re, im = np.cos(np.pi * n * f / L), -np.sin(np.pi * n * f / L)
    im[:, 0] = np.cos(np.pi * n[:, 0])
    m["w_re"], m["w_im"] = re, im
    s = np.arange(2 * L)[:, None].astype(np.float64)
    re, im = np.cos(np.pi * s * f / L), -np.sin(np.pi * s * f / L)
    im[:, 0] = np.cos(np.pi * s[:, 0])
    for name, full in (("v_re", re), ("v_im", im)):
        fold = full[:L].copy()
        fold[L - 1] += full[L:].sum(0)
        m[name] = fold
    fc = np.arange(128)[:, None]
    w = np.where(fc == 0, 1.0, 2.0) / (2 * L)
    cos, sin = w * np.cos(np.pi * fc * t / L), w * np.sin(np.pi * fc * t / L)
    ii = cos.copy()
    ii[0] = np.cos(np.pi * t[0]) / (2 * L)
    m["o_rr"], m["o_ii"] = cos, ii
    m["o_ri"], m["o_ir"] = -sin * (fc > 0), sin * (fc > 0)
    return np.ascontiguousarray(np.stack([m[k] for k in FOUR], 1).astype(np.float32))


def decoder_kernel(nc, xT, xtok, ctxT, ctxtok, par, rows, four, win, wx, wdt, wout, qw, sc, ze,
                   loraA, loraBT, dwin, dw1, dw2, dwout, wq, wk, wv, wo, ra, bwT, out):
    scratch = nc.dram_tensor("bc_scratch", [2, 2 * NS, HT], F32, kind="Internal").ap()
    with ExitStack() as ctx:
        def sb(name, shape, dt=F32):
            return ctx.enter_context(nc.sbuf_tensor(name, shape, dt))

        names = {}

        def sem(name):
            names[name] = ctx.enter_context(nc.semaphore(name))
            return names[name]

        KB = 256
        with nc.sbuf_tensor("arena", [P, 172 * KB], F32) as arena:
            pass
        with nc.sbuf_tensor("gap0", [P, 64 * KB], F32), nc.sbuf_tensor("x_split", [P, 16 * KB], F32R) as x_split, \
                nc.sbuf_tensor("gap1", [P, 16 * KB], F32), nc.sbuf_tensor("o_split", [P, 12 * KB], F32R) as o_split, \
                nc.sbuf_tensor("gap2", [P, 20 * KB], F32), nc.sbuf_tensor("w_split", [P, 44 * KB], F32R) as w_split:
            pass
        with nc.sbuf_tensor("gap3", [P, 32 * KB], F32), nc.sbuf_tensor("in_split", [P, 28 * KB], F32R) as in_split:
            pass
        sb("arena_space", [P, 172 * KB])

        def part(at, size, parts=P):
            return arena[0:parts, int(at * KB):int(at * KB) + size]

        x_tok = sb("x_tok", [P, B, D])
        prm = sb("prm", [P, NPAR])
        row = sb("row", [P, NROW])
        amat = sb("amat", [P, MD * NS])
        lnst = sb("lnst", [P, B, 6])
        lnmv = sb("lnmv", [P, B, 2])
        lnve = sb("lnve", [P, B])
        lnrs = sb("lnrs", [P, B])
        halfneg = sb("halfneg", [P, 16])

        def pc(name):
            a, b = COL[name]
            return prm[:, a:b]

        def rw(name):
            a, b = ROW[name]
            return row[:, a:b]

        ident = pc("ident")
        psum = ctx.enter_context(nc.psum_tensor("psum", [P, 8 * 512], F32))
        bank = [psum[:, i * 512:(i + 1) * 512] for i in range(8)]

        xs = x_split[:, :].rearrange("p (i k n) -> p i k n", i=2, k=KD)
        osp = o_split[:, :].rearrange("p (i s n) -> p i s n", i=2, s=3)
        xin = in_split[:, 0:16 * KB].rearrange("p (i k n) -> p i k n", i=2, k=KD)
        win_s = in_split[:, 16 * KB:28 * KB].rearrange("p (i s n) -> p i s n", i=2, s=3)
        wqs = w_split[:, 0:12 * KB].rearrange("p (i s n) -> p i s n", i=2, s=3)
        wos = w_split[:, 12 * KB:44 * KB].rearrange("p (i s n) -> p i s n", i=2, s=8)
        xTh = part(0, KD * HT).rearrange("p (k n) -> p k n", k=KD)
        wring = part(8, 4 * 512).rearrange("p (s n) -> p s n", s=4)
        xpad = part(16, 2 * HB * (L + CV - 1)).rearrange("p (s b n) -> p s b n", s=2, b=HB)
        conv = part(21, 2 * HT).rearrange("p (s n) -> p s n", s=2)
        ssmsq = part(26, HB * SSM)
        ssmn = part(27, HB * SSM).rearrange("p (b c) -> p b c", b=HB)
        ssmc = part(29, HT, SSM)
        ssm_ss = part(28, 64)
        ssm_ms = part(28.5, 16)
        ssm_rs = part(28.75, 16)
        Brep = part(0, NS * HT).rearrange("p (n t) -> p n t", n=NS)
        Crep = part(32, NS * HT).rearrange("p (n t) -> p n t", n=NS)
        dA = psum[:, 0:3 * NG * HT].rearrange("p (s n t) -> p s n t", s=3, n=NG)
        skip = sb("skip", [P, 2, P])
        zeros = sb("zeros", [P, NG * HB])
        bu = part(80, 2 * NG * HT).rearrange("p (s n t) -> p s n t", s=2, n=NG)
        prod = part(88, 2 * NG * HT).rearrange("p (s n t) -> p s n t", s=2, n=NG)
        sp_w = part(64, MD * HT).rearrange("p (m t) -> p m t", m=MD)
        sp_r = part(96, MD * HT).rearrange("p (m t) -> p m t", m=MD)
        u = part(112, MD * HT).rearrange("p (m t) -> p m t", m=MD)
        dt = part(128, MD * HT).rearrange("p (m t) -> p m t", m=MD)
        g = part(144, MD * HT).rearrange("p (m t) -> p m t", m=MD)
        wout_sb = dt
        wx_sb = part(160, MD * SSM).rearrange("p (k o) -> p k o", k=MD)
        wdt_sb = part(162, DI, RK)
        dtu = part(166, 2 * HT).rearrange("p (s n) -> p s n", s=2)
        ssmT = sb("ssmT", [SSM, HT])
        ctx_sb = part(0, B * D).rearrange("p (b d) -> p b d", b=B)
        four_sb = part(16, len(FOUR) * P).rearrange("p (i n) -> p i n", i=len(FOUR))
        fm = {k: four_sb[:, i, :] for i, k in enumerate(FOUR)}
        qf = part(22, D)
        m12 = part(24, 2 * D).rearrange("p (i n) -> p i n", i=2)
        negmax = part(28, KD)
        ee = part(30, D)
        rep1 = part(32, D)
        rep2 = part(34, D)
        wn = part(36, 2 * D).rearrange("p (s n) -> p s n", s=2)
        wT = part(40, D)
        vri = part(42, 2 * D).rearrange("p (i n) -> p i n", i=2)
        m4 = part(46, 4 * D).rearrange("p (i n) -> p i n", i=4)
        mx8 = part(54, 4 * 8)
        nx8 = part(54.25, 4 * 8)
        m9 = part(54.5, 4 * 8)
        wsum = part(54.75, 8)
        winv = part(55, 8)
        ctxT_sb = part(64, KD * B * L).rearrange("p (k n) -> p k n", k=KD)
        sz = part(80, 2 * KD * D).rearrange("p (i k n) -> p i k n", i=2, k=KD)
        weff = part(96, KD * D).rearrange("p (k n) -> p k n", k=KD)
        qw_sb = sb("qw_sb", [P, 1, D], I32)
        lora = part(104, 2 * D, 16).rearrange("p (i n) -> p i n", i=2)
        x2T = part(112, KD * B * L).rearrange("p (k n) -> p k n", k=KD)
        rtab = part(128, DEPTH * HT).rearrange("p (l t) -> p l t", l=DEPTH)
        ctab = part(136, DEPTH * (L + 1)).rearrange("p (l t) -> p l t", l=DEPTH)
        stab = part(138.25, DEPTH * (L + 1)).rearrange("p (l t) -> p l t", l=DEPTH)
        ttmp = part(140.5, 2 * DEPTH * 64).rearrange("p (i l t) -> p i l t", i=2, l=DEPTH)
        tsm = sb("tsm", [P, 12, DEPTH])
        dh = part(144, B * DIM).rearrange("p (b c) -> p b c", b=B)
        dhc = part(146, B * DIM).rearrange("p (b c) -> p b c", b=B)
        dyn = part(148, 2 * HB * P).rearrange("p (h b c) -> p h b c", h=2, b=HB)
        dys = part(152, 2 * HT).rearrange("p (h t) -> p h t", h=2)
        dz = part(156, 2 * HT).rearrange("p (h t) -> p h t", h=2)
        df = part(160, 2 * 2 * HT).rearrange("p (h k t) -> p h k t", h=2, k=2)
        dw1_sb = part(168, DEPTH * DFF, DIM).rearrange("p (l f) -> p l f", l=DEPTH)
        dw2_sb = part(104, DEPTH * 2 * DIM).rearrange("p (l k o) -> p l k o", l=DEPTH, k=2)
        dwin_sb = part(106, KD * DIM).rearrange("p (k o) -> p k o", k=KD)
        dwout_sb = sb("dwout_sb", [DIM, D])[:, :]
        dsc = part(109, DEPTH * DIM).rearrange("p (l o) -> p l o", l=DEPTH)
        dst = sb("dst", [P, B, 6])
        dmv = sb("dmv", [P, B, 2])
        dve_ = sb("dve_", [P, B])
        drs = sb("drs", [P, B])
        KT = part(0, NKV * B * L).rearrange("p (g n) -> p g n", g=NKV)
        V = part(32, B * NKV * P).rearrange("p (b n) -> p b n", b=B)
        wk_sb = part(32, 2 * 512).rearrange("p (s n) -> p s n", s=2)
        wv_sb = part(80, KD * 1024).rearrange("p (k n) -> p k n", k=KD)
        qT = part(80, 2 * GQ * HT).rearrange("p (s j n) -> p s j n", s=2, j=GQ)
        pe_ = part(112, 2 * 512).rearrange("p (s n) -> p s n", s=2)
        pn = part(116, 512)
        pT = part(118, 2 * 512).rearrange("p (s n) -> p s n", s=2)
        wq_sb = part(108, 2 * 512).rearrange("p (s n) -> p s n", s=2)
        wo_sb = part(122, 3 * 512).rearrange("p (s n) -> p s n", s=3)
        amax = sb("amax", [P, 4])
        asum = sb("asum", [P, 2, 4])
        ainv = sb("ainv", [P, 4])
        ra_sb = part(32, KD * 136).rearrange("p (k n) -> p k n", k=KD)
        bw_sb = part(35, D)
        logits = part(38, 8)
        rt8 = part(38.25, 8)
        ri8 = sb("ri8", [P, 8], U32)
        rif = part(38.5, 8)
        rwt = part(38.75, 8)
        wh = part(39, P)
        whT = part(40, P)
        x5T = part(42, 2 * D).rearrange("p (s k t) -> p s k t", s=2, k=KD)

        ls = {n: sem(n) for n in (
            "par_in", "row_in", "xtok_in", "wx_in", "xT_in0", "xT_in1", "xT_in2", "xT_in3", "w_in0", "w_in1", "w_in2", "w_in3",
            "bc_out", "b_in0", "b_in1", "b_in2", "b_in3", "c_in0", "c_in1", "c_in2", "c_in3", "wout_in",
            "ctxtok_in", "four_in", "ctxT_in", "sz_in", "qw_in", "lora_in", "dwt_in", "wk_in0", "wk_in1",
            "wv_in", "wq_in0", "wq_in1", "wo_in0", "wo_in1", "wo_in2", "ra_in", "stored",
            "dve_chain", "act_chain", "pool_chain",
            "pad_zero", "zero_done", "amat_done", "deq_done",
            "xs_hi", "xs_lo", "wi_hi", "wi_lo", "wq_hi", "wq_lo", "wo_hi", "wo_lo", "o_hi", "x4_hi", "x4_lo",
            "inproj", "in_evac", "conv_done", "u_done", "xp_done", "xp_sb", "ssm_done", "ssm_sq", "ssm_ve", "ssm_rs", "ssm_norm",
            "ssmT_done", "ssmT_sb", "dt_proj", "dt_abs", "dt_exp", "dt_relu", "dt_w0", "dt_w", "dt_base", "dt_ln", "skip_done",
            "dt_done", "dtu_done", "dA_done", "bu_done", "scan_done", "prod_done", "ysum", "y_done",
            "wout_done",
            "x_sum", "ln_ve", "ln_rs", "x_done",
            "kf_done", "qf_done", "qf_sb", "m12_done", "corr", "rep_done", "ee_done", "wn_done",
            "vf_done", "vri_sb", "wT_done", "wT_sb", "wf_done", "m4_done", "xat_done",
            "lora_done", "weff_done", "xTt", "xT_sb", "xbias", "ffn_done",
            "tab_a", "tab_b", "tab_c", "tab_d", "tab_e", "tab_done",
            "h0_done", "h0_read", "d_ve", "d_rs", "d_yn", "d_tr", "d_ys", "d_z", "d_conv", "d_hread", "d_yT",
            "d_f1", "d_f", "d_f2", "d_f2read", "d_out",
            "kv_ps", "kv_sb", "q_ps", "q_sb", "s_ps", "p_es", "p_exp", "p_norm", "t_ps", "t_sb",
            "av_ps", "o_sb", "op_ps",
            "r_ps", "r_wh", "wh_ps", "whT_done", "rf_ps",
        )}
        S = type("S", (), ls)

        block = ctx.enter_context(nc.Block())

        def lnc(stage, b):
            if stage == 4 and b >= HB:
                return stage * B + HB + b + 1
            if stage == 5 and b < HB:
                return stage * B - HB + b + 1
            return stage * B + b + 1

        def routed_at(s):
            at = s - ROUTED_FROM
            if 0 <= at < 4 * HB:
                return [(at // 4, at % 4, 2)]
            at = s - (2 * NKV * HB + 1)
            return [(HB + at - k, k, ((at % 2), 2, 3, 4 + at - k)[k]) for k in (3, 2, 1, 0) if 0 <= at - k < HB]

        SLOTS = 2 * NKV * HB + 8

        @block.sync
        def _(sp):
            def load(dst, src, s):
                sp.dma_start(dst, src).then_inc(s, 16)

            load(prm[:, :], par, S.par_in)
            for h in range(2):
                if h:
                    sp.wait_ge(S.y_done, MD)
                for k in range(KD):
                    load(xTh[:, k, :], xT[h, :, k, :], (S.xT_in0, S.xT_in1, S.xT_in2, S.xT_in3)[k])
                    if k == 0:
                        load(wring[:, 0, :], win[0], S.w_in0)
                for m in range(1, 16):
                    i = h * 16 + m
                    if m >= 4:
                        sp.wait_ge(S.wi_lo, i - 3)
                    load(wring[:, i % 4, :], win[m], (S.w_in0, S.w_in1, S.w_in2, S.w_in3)[i % 4])
                    if i == 5:
                        load(wx_sb, wx, S.wx_in)
                        load(wdt_sb, wdt, S.wx_in)
                        load(row[:, :], rows.partition_broadcast(P), S.row_in)
                    if i == 10:
                        load(x_tok[:, :, :], xtok, S.xtok_in)
                sp.wait_ge(S.ssmT_sb, h + 1)
                sp.dma_start(scratch[h], ssmT[RK:SSM, :]).then_inc(S.bc_out, 16)
                sp.wait_ge(S.bc_out, 16 * (h + 1))
                for c, (dst, s) in enumerate(((Brep, (S.b_in0, S.b_in1, S.b_in2, S.b_in3)),
                                              (Crep, (S.c_in0, S.c_in1, S.c_in2, S.c_in3)))):
                    for q in range(4):
                        if c == 0 and q == 1:
                            sp.wait_ge(S.wi_lo, 16 * (h + 1))
                        if c == 1 and q == 0:
                            sp.wait_ge(S.inproj, 16 * (h + 1))
                        src = scratch[h, c * NS + q * 4:c * NS + (q + 1) * 4, :]
                        load(dst[:, q * 4:(q + 1) * 4, :].rearrange("p n t -> p (n t)"),
                             src.rearrange("n t -> (n t)").partition_broadcast(P), s[q])
                for m in range(MD):
                    sp.wait_ge(S.y_done, h * MD + m + 1)
                    load(wout_sb[:, m, :], wout[m], S.wout_in)
            load(ctx_sb, ctxtok, S.ctxtok_in)
            load(four_sb, four, S.four_in)
            for i, t in enumerate((sc, ze)):
                for half in range(2):
                    load(sz[64 * half:64 * half + 64, i, :, :], t[half].partition_broadcast(64), S.sz_in)
            load(lora[:, 0, :], loraA, S.lora_in)
            load(lora[:, 1, :], loraBT, S.lora_in)
            load(ctxT_sb, ctxT, S.ctxT_in)
            for k in range(KD):
                if k:
                    sp.wait_ge(S.deq_done, k)
                load(qw_sb[:, 0, :], qw[k], S.qw_in)
            sp.wait_ge(S.weff_done, KD)
            load(dw2_sb, dw2, S.dwt_in)
            load(dwin_sb, dwin, S.dwt_in)
            load(dwout_sb, dwout, S.dwt_in)
            load(dw1_sb, dw1, S.dwt_in)
            load(wv_sb, wv, S.wv_in)
            for i in range(NKV):
                if i >= 2:
                    sp.wait_ge(S.kv_ps, 2 * (i - 1))
                load(wk_sb[:, i % 2, :], wk[i], (S.wk_in0, S.wk_in1)[i % 2])
            sp.wait_ge(S.d_conv, 2 * DEPTH)
            NT = 2 * NKV * GQ
            AHEAD = 6
            for i in range(NT + AHEAD):
                if i < NT:
                    if i >= 2:
                        sp.wait_ge(S.wq_lo, i - 1)
                    load(wq_sb[:, i % 2, :], wq[i // GQ % NKV, :, (i % GQ) * 512:(i % GQ + 1) * 512],
                         (S.wq_in0, S.wq_in1)[i % 2])
                o = i - AHEAD
                if o >= 0:
                    if o >= 3:
                        sp.wait_ge(S.wo_lo, o - 2)
                    if o == ROUTED_FROM - 5:
                        sp.wait_ge(S.av_ps, NKV * HB)
                        load(ra_sb, ra, S.ra_in)
                        load(bw_sb, bwT, S.ra_in)
                    load(wo_sb[:, o % 3, :], wo[o // GQ % NKV, :, o % GQ, :], (S.wo_in0, S.wo_in1, S.wo_in2)[o % 3])
            for b in range(B):
                sp.wait_ge(S.x_done, lnc(5, b))
                sp.dma_start(out[b], x_tok[:, b, :]).then_inc(S.stored, 16)
            sp.wait_ge(S.stored, 16 * B)

        @block.tensor
        def _(pe):
            mm = nc.tensor.matmul

            def mm3(o, l, r, start, stop):
                mm(o, l[0], r[0], start=start, stop=False)
                mm(o, l[0], r[1], start=False, stop=False)
                return mm(o, l[1], r[0], start=False, stop=stop)

            def in_proj(h, m):
                i = h * 16 + m
                pe.wait_ge(S.wi_lo, i + 1)
                if i >= 2:
                    pe.wait_ge(S.in_evac, i - 1)
                if h and m == 0:
                    pe.wait_ge(S.x_sum, lnc(0, HB - 1))
                for k in range(KD):
                    if m == 0:
                        pe.wait_ge(S.xs_lo, h * KD + k + 1)
                    last = mm3(bank[m % 2][:, :], [win_s[:, e, i % 3, k * P:(k + 1) * P] for e in range(2)],
                               [xin[:, e, k, :] for e in range(2)], start=(k == 0), stop=(k == KD - 1))
                last.then_inc(S.inproj, 1)

            for h in range(2):
                for m in range(XP_AT):
                    in_proj(h, m)
                pe.wait_ge(S.u_done, MD * (h + 1))
                pe.wait_ge(S.wx_in, 32)
                for k in range(MD):
                    last = mm(bank[3][0:SSM, :], wx_sb[:, k, :], u[:, k, :], start=(k == 0), stop=(k == MD - 1))
                last.then_inc(S.xp_done, 1)
                for m in range(XP_AT, BACK_AT):
                    in_proj(h, m)
                pe.wait_ge(S.xp_sb, h + 1)
                for b in range(HB):
                    last = nc.tensor.transpose(bank[2][:, b * SSM:(b + 1) * SSM], ssmc[:, b * L:(b + 1) * L],
                                               ident[0:SSM, 0:SSM])
                last.then_inc(S.ssm_done, 1)
                for m in range(BACK_AT, TR_AT):
                    in_proj(h, m)
                pe.wait_ge(S.ssm_norm, h + 1)
                for b in range(HB):
                    last = nc.tensor.transpose(bank[3][0:SSM, b * L:(b + 1) * L], ssmn[:, b, :], ident)
                last.then_inc(S.ssmT_done, 1)
                for m in range(TR_AT, DT_AT):
                    in_proj(h, m)
                pe.wait_ge(S.ssmT_sb, h + 1)
                for m in range(MD):
                    i = h * MD + m
                    if m >= 4:
                        pe.wait_ge(S.dt_relu, i - 3)
                    last = mm(bank[4 + m % 4][:, :], wdt_sb[:, m * P:(m + 1) * P], ssmT[0:RK, :],
                              start=True, stop=True)
                    last.then_inc(S.dt_proj, 1)
                for m in range(DT_AT, 16):
                    in_proj(h, m)
                pe.wait_ge(S.dt_relu, MD * (h + 1))
                for m in range(MD):
                    if h * MD + m >= 2:
                        pe.wait_ge(S.y_done, h * MD + m - 1)
                    pe.wait_ge(S.skip_done, h * MD + m + 1)
                    mm(bank[6 + m % 2][:, :], skip[:, m % 2, :], u[:, m, :], start=True, stop=False)
                    for q in range(GS):
                        i = (h * MD + m) * GS + q
                        pe.wait_ge(S.prod_done, i + 1)
                        for n in range(NG):
                            last = mm(bank[6 + m % 2][:, :], ident, prod[:, i % 2, n, :],
                                      start=False, stop=(q == GS - 1 and n == NG - 1))
                        last.then_inc(S.ysum, 1)
                pe.wait_ge(S.y_done, MD * (h + 1))
                pe.wait_ge(S.wout_in, 16 * MD * (h + 1))
                for b in range(HB):
                    if b >= 2:
                        pe.wait_ge(S.x_sum, lnc(0, h * HB + b - 2))
                    for k in range(MD):
                        last = mm(bank[b % 2][:, :], g[:, k, b * L:(b + 1) * L], wout_sb[:, k, :],
                                  start=(k == 0), stop=(k == MD - 1))
                    last.then_inc(S.wout_done, 1)

            def spectra(b):
                if b == 0:
                    pe.wait_ge(S.ctxtok_in, 16)
                    pe.wait_ge(S.four_in, 16)
                    pe.wait_ge(S.x_sum, lnc(0, B - 1))
                    pe.wait_ge(S.y_done, 2 * MD)
                if b >= 1:
                    pe.wait_ge(S.m12_done, b)
                mm(bank[1][:, :], fm["q"], ctx_sb[:, b, :], start=True, stop=True)
                mm(bank[2][:, :], fm["k_swap"], ctx_sb[:, b, :], start=True, stop=True).then_inc(S.kf_done, 1)
                pe.wait_ge(S.x_done, lnc(0, b))
                mm(bank[0][:, :], fm["q"], x_tok[:, b, :], start=True, stop=True).then_inc(S.qf_done, 1)

            def correlate(b):
                pe.wait_ge(S.m12_done, b + 1)
                if b >= 1:
                    pe.wait_ge(S.ee_done, b)
                for t in range(KD):
                    o = bank[3][:, t * P:(t + 1) * P]
                    mm(o, m12[:, 0, t * P:(t + 1) * P], fm["c_re"], start=True, stop=False)
                    last = mm(o, m12[:, 1, t * P:(t + 1) * P], fm["c_im"], start=False, stop=True)
                last.then_inc(S.corr, 1)

            def weights(b):
                if b >= 1:
                    pe.wait_ge(S.m4_done, b)
                mm(bank[5][:, :], fm["v_re"], ctx_sb[:, b, :], start=True, stop=True)
                mm(bank[6][:, :], fm["v_im"], ctx_sb[:, b, :], start=True, stop=True).then_inc(S.vf_done, 1)
                pe.wait_ge(S.wn_done, b + 1)
                for t in range(KD):
                    last = nc.tensor.transpose(bank[4][:, t * P:(t + 1) * P], wn[:, b % 2, t * P:(t + 1) * P], ident)
                last.then_inc(S.wT_done, 1)
                pe.wait_ge(S.vri_sb, b + 1)
                pe.wait_ge(S.wT_sb, b + 1)
                mm(bank[5][:, :], fm["w_re"], wT, start=True, stop=True)
                mm(bank[6][:, :], fm["w_im"], wT, start=True, stop=True).then_inc(S.wf_done, 1)

            def aggregate(b):
                pe.wait_ge(S.m4_done, b + 1)
                if b >= 1:
                    pe.wait_ge(S.x_sum, lnc(1, b - 1))
                for i, k in enumerate(("o_rr", "o_ri", "o_ir", "o_ii")):
                    last = mm(bank[7][:, :], fm[k], m4[:, i, :], start=(i == 0), stop=(i == 3))
                last.then_inc(S.xat_done, 1)

            spectra(0)
            correlate(0)
            for b in range(B):
                if b + 1 < B:
                    spectra(b + 1)
                weights(b)
                if b + 1 < B:
                    correlate(b + 1)
                else:
                    pe.wait_ge(S.lora_in, 32)
                    pe.wait_ge(S.m12_done, B)
                    pe.wait_ge(S.ee_done, B)
                    pe.wait_ge(S.wT_sb, B)
                    for k in range(KD):
                        mm(bank[1 + k][:, :], lora[:, 0, k * P:(k + 1) * P], lora[:, 1, :],
                           start=True, stop=True).then_inc(S.lora_done, 1)
                aggregate(b)

            def turn(stage, b, n, bk):
                pe.wait_ge(S.x_done, lnc(stage, b))
                if n >= 2:
                    pe.wait_ge(S.xT_sb, n - 1)
                for k in range(KD):
                    last = nc.tensor.transpose(bank[bk][:, k * P:(k + 1) * P], x_tok[:, b, k * P:(k + 1) * P], ident)
                last.then_inc(S.xTt, 1)

            turn(1, 0, 0, 0)
            pe.wait_ge(S.weff_done, KD)
            for b in range(B):
                if b + 1 < B:
                    turn(1, b + 1, b + 1, (b + 1) % 2)
                pe.wait_ge(S.xT_sb, b + 1)
                if b >= 2:
                    pe.wait_ge(S.x_sum, lnc(2, b - 2))
                for k in range(KD):
                    last = mm(bank[2 + b % 2][:, :], x2T[:, k, b * L:(b + 1) * L], weff[:, k, :],
                              start=(k == 0), stop=(k == KD - 1))
                last.then_inc(S.ffn_done, 1)

            turn(2, 0, B, 0)
            for b in range(B):
                if b + 1 < B:
                    turn(2, b + 1, B + b + 1, (b + 1) % 2)
                pe.wait_ge(S.xT_sb, B + b + 1)
                pe.wait_ge(S.dwt_in, 64)
                if b == 0:
                    pe.wait_ge(S.x_sum, lnc(2, B - 1))
                for k in range(KD):
                    last = mm(bank[4 + b // HB][:, (b % HB) * DIM:(b % HB + 1) * DIM],
                              x2T[:, k, b * L:(b + 1) * L], dwin_sb[:, k, :], start=(k == 0), stop=(k == KD - 1))
                if b % HB == HB - 1:
                    last.then_inc(S.h0_done, 1)
            pe.wait_ge(S.h0_read, 2)
            pe.wait_ge(S.tab_done, 1)
            pe.wait_ge(S.ctxT_in, 16)

            def keys_values(at):
                if at in KV_EMPTY:
                    return
                n = at - sum(at > e for e in KV_EMPTY)
                if n >= 2:
                    pe.wait_ge(S.kv_sb, n - 1)
                o = bank[3 + 4 * (n % 2)][:, :]
                if n < 2 * NKV:
                    gi, h = n // 2, n % 2
                    if h == 0:
                        pe.wait_ge((S.wk_in0, S.wk_in1)[gi % 2], 16 * (gi // 2 + 1))
                    for k in range(KD):
                        last = mm(o, wk_sb[:, gi % 2, k * P:(k + 1) * P], ctxT_sb[:, k, h * HT:(h + 1) * HT],
                                  start=(k == 0), stop=(k == KD - 1))
                else:
                    b, c = (n - 2 * NKV) // 2, n % 2
                    pe.wait_ge(S.wv_in, 16)
                    for k in range(KD):
                        last = mm(o, ctxT_sb[:, k, b * L:(b + 1) * L], wv_sb[:, k, c * 512:(c + 1) * 512],
                                  start=(k == 0), stop=(k == KD - 1))
                last.then_inc(S.kv_ps, 1)

            keys_values(0)
            for l in range(DEPTH):
                for h in range(2):
                    pe.wait_ge(S.d_yn, 4 * l + h + 1)
                    for b in range(HB):
                        last = nc.tensor.transpose(bank[4 * h][:, b * L:(b + 1) * L], dyn[:, h, b, :], ident)
                    last.then_inc(S.d_tr, 1)
                    keys_values(1 + KVL * l + h)
                for h in range(2):
                    pe.wait_ge(S.d_z, 2 * l + h + 1)
                    for b in range(HB):
                        last = mm(bank[4 * h + 1][:, b * DIM:(b + 1) * DIM], dz[:, h, b * L:(b + 1) * L], dsc[:, l, :],
                                  start=True, stop=True)
                    last.then_inc(S.d_conv, 1)
                    keys_values(1 + KVL * l + 2 + h)
                for h in range(2):
                    pe.wait_ge(S.d_yn, 4 * l + 2 + h + 1)
                    for b in range(HB):
                        last = nc.tensor.transpose(bank[4 * h][0:DIM, b * L:(b + 1) * L], dyn[:, h, b, 0:DIM], ident)
                    last.then_inc(S.d_tr, 1)
                    keys_values(1 + KVL * l + 4 + h)
                for h in range(2):
                    pe.wait_ge(S.d_yT, 2 * l + h + 1)
                    for k in range(2):
                        last = mm(bank[4 * h + 2 * k][:, :], dw1_sb[:, l, k * P:(k + 1) * P], dys[0:DIM, h, :],
                                  start=True, stop=True)
                    last.then_inc(S.d_f1, 1)
                for h in range(2):
                    pe.wait_ge(S.d_f, 2 * l + h + 1)
                    for b in range(HB):
                        for k in range(2):
                            last = mm(bank[4 * h + 1][:, b * DIM:(b + 1) * DIM], df[:, h, k, b * L:(b + 1) * L],
                                      dw2_sb[:, l, k, :], start=(k == 0), stop=(k == 1))
                    last.then_inc(S.d_f2, 1)
                    keys_values(1 + KVL * l + 6 + h)
            keys_values(1 + KVL * DEPTH)
            for h in range(2):
                pe.wait_ge(S.d_yn, 4 * DEPTH + h + 1)
                for b in range(HB):
                    last = nc.tensor.transpose(bank[4 * h][0:DIM, b * L:(b + 1) * L], dyn[:, h, b, 0:DIM], ident)
                last.then_inc(S.d_tr, 1)

            def network_out(b):
                if b % HB == 0:
                    pe.wait_ge(S.d_yT, 2 * DEPTH + b // HB + 1)
                if b >= 2:
                    pe.wait_ge(S.x_sum, lnc(3, b - 2))
                mm(bank[2 + 4 * (b % 2)][:, :], dys[0:DIM, b // HB, (b % HB) * L:(b % HB + 1) * L], dwout_sb,
                   start=True, stop=True).then_inc(S.d_out, 1)

            for b in range(HB):
                network_out(b)

            pe.wait_ge(S.kv_sb, 4 * NKV)
            NU = 2 * NKV

            def turn_half(h, b, bk):
                gb = h * HB + b
                pe.wait_ge(S.x_done, lnc(3, gb))
                if b >= 2:
                    pe.wait_ge(S.x4_lo, gb - 1)
                for k in range(KD):
                    last = nc.tensor.transpose(bank[bk][:, k * P:(k + 1) * P], x_tok[:, gb, k * P:(k + 1) * P], ident)
                last.then_inc(S.xTt, 1)

            for b in range(HB):
                turn_half(0, b, b % 2)

            def query(v, j):
                if v >= NU:
                    return
                n = v * GQ + j
                if v % NKV == 0 and j == 0:
                    pe.wait_ge(S.x4_lo, (v // NKV + 1) * HB)
                pe.wait_ge(S.wq_lo, n + 1)
                if n >= 1:
                    pe.wait_ge(S.q_sb, n)
                for k in range(KD):
                    last = mm3(bank[0][:, :], [wqs[:, e, n % 3, k * P:(k + 1) * P] for e in range(2)],
                               [xs[:, e, k, :] for e in range(2)], start=(k == 0), stop=(k == KD - 1))
                last.then_inc(S.q_ps, 1)

            def routed(b, step, bk):
                if step == 0:
                    pe.wait_ge(S.x_done, lnc(4, b))
                    if b >= 2:
                        pe.wait_ge(S.xT_sb, 2 * B + b - 1)
                    for k in range(KD):
                        last = nc.tensor.transpose(bank[bk][:, k * P:(k + 1) * P], x_tok[:, b, k * P:(k + 1) * P],
                                                   ident)
                    last.then_inc(S.xTt, 1)
                elif step == 1:
                    pe.wait_ge(S.ra_in, 32)
                    pe.wait_ge(S.xT_sb, 2 * B + b + 1)
                    if b >= 1:
                        pe.wait_ge(S.r_wh, b)
                    for k in range(KD):
                        last = mm(bank[bk][:, 0:136], x5T[:, b % 2, k, :], ra_sb[:, k, :],
                                  start=(k == 0), stop=(k == KD - 1))
                    last.then_inc(S.r_ps, 1)
                elif step == 2:
                    pe.wait_ge(S.r_wh, b + 1)
                    nc.tensor.transpose(bank[bk][:, 0:P], wh, ident).then_inc(S.wh_ps, 1)
                else:
                    pe.wait_ge(S.whT_done, b + 1)
                    mm(bank[bk][:, :], whT, bw_sb, start=True, stop=True).then_inc(S.rf_ps, 1)

            network_out(HB)
            for j in range(GQ):
                if HB + j + 1 < B:
                    network_out(HB + j + 1)
                query(0, j)
            pe.wait_ge(S.x_sum, lnc(3, B - 1))
            for s in range(SLOTS):
                v, b = s // HB, s % HB
                if s < NU * HB:
                    pe.wait_ge(S.q_sb, (v + 1) * GQ)
                    if s >= 1:
                        pe.wait_ge(S.p_es, s)
                    gb = (v // NKV) * HB + b
                    for j in range(GQ):
                        last = mm(bank[1][:, j * P:(j + 1) * P], qT[:, v % 2, j, b * L:(b + 1) * L],
                                  KT[:, v % NKV, gb * L:(gb + 1) * L], start=True, stop=True)
                    last.then_inc(S.s_ps, 1)
                    if s == (NKV - 1) * HB:
                        for i in range(HB):
                            if i == 0:
                                pe.wait_ge(S.t_sb, s - 1)
                            turn_half(1, i, (2, 0)[i % 2])
                    query(v + 1, b)
                if 1 <= s <= NU * HB:
                    pe.wait_ge(S.p_norm, s)
                    if s >= 2:
                        pe.wait_ge(S.t_sb, s - 1)
                    for rb, step, bk in routed_at(s - 1):
                        pe.wait_ge((S.xT_sb, S.r_wh, S.whT_done, S.x_sum)[step],
                                   (2 * B + rb + 1, rb + 1, rb + 1, lnc(5, rb))[step])
                    for j in range(GQ):
                        last = nc.tensor.transpose(bank[2][:, j * P:(j + 1) * P], pn[:, j * P:(j + 1) * P], ident)
                    last.then_inc(S.t_ps, 1)
                if 2 <= s <= NU * HB + 1:
                    r = s - 2
                    rv, rb = r // HB, r % HB
                    pe.wait_ge(S.t_sb, r + 1)
                    if r >= 1:
                        pe.wait_ge(S.o_sb, r)
                    mm(bank[3][:, :], V[:, (rv // NKV) * HB + rb, (rv % NKV) * P:(rv % NKV + 1) * P], pT[:, r % 2, :],
                       start=True, stop=True).then_inc(S.av_ps, 1)
                if 4 <= s < NU * HB + 4:
                    r = s - 4
                    rv, rb = r // HB, r % HB
                    pe.wait_ge(S.o_sb, r + 1)
                    if rv == NKV:
                        pe.wait_ge(S.x_sum, lnc(4, rb))
                    for j in range(GQ):
                        pe.wait_ge(S.wo_lo, rv * GQ + j + 1)
                        last = mm3(bank[4 + rb][:, :], [osp[:, e, r % 3, j * P:(j + 1) * P] for e in range(2)],
                                   [wos[:, e, (rv * GQ + j) % 8, :] for e in range(2)],
                                   start=(rv % NKV == 0 and j == 0), stop=(rv % NKV == NKV - 1 and j == GQ - 1))
                    last.then_inc(S.op_ps, 1)
                for rb, step, bk in routed_at(s):
                    if rb < HB:
                        pe.wait_ge(S.t_sb, s)
                    elif rb == HB and step == 0:
                        pe.wait_ge(S.t_sb, NU * HB)
                        pe.wait_ge(S.o_sb, NU * HB)
                    routed(rb, step, bk)

        @block.scalar
        def _(act):
            def av(o, i, f, **k):
                return nc.scalar.activation(o, i, f, **k)

            chain = [0]

            def link(ins):
                chain[0] += 1
                ins.then_inc(S.act_chain, 1)
                act.wait_ge(S.act_chain, chain[0])

            act.wait_ge(S.par_in, 16)
            av(amat[:, :], pc("alog"), ACT.Exp).then_inc(S.amat_done, 1)
            def split_in(i):
                if i >= 32:
                    return
                act.wait_ge((S.w_in0, S.w_in1, S.w_in2, S.w_in3)[i % 4], 16 * (i // 4 + 1))
                if i >= 3:
                    act.wait_ge(S.inproj, i - 2)
                av(win_s[:, 0, i % 3, :], wring[:, i % 4, :], ACT.Identity).then_inc(S.wi_hi, 1)

            for h in range(2):
                def silu_u(m):
                    act.wait_ge(S.conv_done, h * MD + m + 1)
                    av(u[:, m, :], conv[:, m % 2, :], ACT.Silu).then_inc(S.u_done, 1)

                if h:
                    act.wait_ge(S.y_done, MD)
                for k in range(KD):
                    if k == 1:
                        split_in(h * 16)
                    act.wait_ge((S.xT_in0, S.xT_in1, S.xT_in2, S.xT_in3)[k], 16 * (h + 1))
                    av(xin[:, 0, k, :], xTh[:, k, :], ACT.Identity).then_inc(S.xs_hi, 1)
                split_in(h * 16 + 1)
                def in_out(m):
                    if m + 2 < 16:
                        split_in(h * 16 + m + 2)
                    act.wait_ge(S.inproj, h * 16 + m + 1)
                    if m < MD:
                        if m >= 2:
                            act.wait_ge(S.conv_done, h * MD + m - 1)
                        av(xpad[:, m % 2, :, CV - 1:], bank[m % 2][:, :].rearrange("p (b t) -> p b t", b=HB),
                           ACT.Identity).then_inc(S.in_evac, 1)
                        if m >= 1:
                            silu_u(m - 1)
                    else:
                        if m == MD:
                            silu_u(MD - 1)
                        av(g[:, m - MD, :], bank[m % 2][:, :], ACT.Silu).then_inc(S.in_evac, 1)

                for m in range(XP_AT):
                    in_out(m)
                act.wait_ge(S.xp_done, h + 1)
                av(ssmc, bank[3][0:SSM, :], ACT.Identity).then_inc(S.xp_sb, 1)
                for m in range(XP_AT, BACK_AT):
                    in_out(m)
                act.wait_ge(S.ssm_done, h + 1)
                av(ssmsq, bank[2][:, 0:HB * SSM], ACT.Square).then_inc(S.ssm_sq, 1)
                for m in range(BACK_AT, TR_AT):
                    in_out(m)
                act.wait_ge(S.ssmT_done, h + 1)
                av(ssmT[:, :], bank[3][0:SSM, :], ACT.Identity).then_inc(S.ssmT_sb, 1)
                for m in range(TR_AT, DT_AT):
                    in_out(m)
                def exp_dt(m):
                    act.wait_ge(S.dt_abs, h * MD + m + 1)
                    av(dt[:, m, :], dt[:, m, :], ACT.Exp, scale=-1.0).then_inc(S.dt_exp, 1)

                def ln_dt(m):
                    act.wait_ge(S.dt_w, h * MD + m + 1)
                    av(sp_w[:, m, :], sp_w[:, m, :], ACT.Ln).then_inc(S.dt_ln, 1)

                for m in range(MD):
                    act.wait_ge(S.dt_proj, h * MD + m + 1)
                    av(dt[:, m, :], bank[4 + m % 4][:, :], ACT.Abs, bias=pc("bdt")[:, m:m + 1]).then_inc(S.dt_abs, 1)
                for m in range(EARLY):
                    exp_dt(m)
                for m in range(EARLY):
                    ln_dt(m)
                for m in range(DT_AT, 16):
                    in_out(m)
                act.wait_ge(S.dt_relu, MD * (h + 1))
                act.wait_ge(S.zero_done, 1)
                act.wait_ge(S.in_evac, 16 * (h + 1))
                for m in range(MD):
                    if m >= 2:
                        act.wait_ge(S.ysum, (h * MD + m - 1) * GS)
                    av(skip[:, m % 2, :], ident, ACT.Identity, scale=pc("dskip")[:, m:m + 1]).then_inc(S.skip_done, 1)
                    for q in range(GS):
                        i = (h * MD + m) * GS + q
                        if q == 0:
                            act.wait_ge(S.dt_done, h * MD + m + 1)
                        if i >= 3:
                            act.wait_ge(S.prod_done, i - 2)
                        av(dA[:, i % 3, :, :].rearrange("p n (b t) -> p (n b) t", b=HB)[:, :, 0:1],
                           zeros[:, :].unsqueeze(2), ACT.Identity)
                        for n in range(NG):
                            c = m * NS + q * NG + n
                            last = av(dA[:, i % 3, n, :].rearrange("p (b t) -> p b t", b=HB)[:, :, 1:],
                                      dt[:, m, :].rearrange("p (b t) -> p b t", b=HB)[:, :, 1:],
                                      ACT.Exp, scale=amat[:, c:c + 1])
                        last.then_inc(S.dA_done, 1)
                        if m == 0 and q + EARLY < MD:
                            exp_dt(q + EARLY)
                    if m == 0:
                        for k in range(EARLY, MD):
                            ln_dt(k)
                if h == 0:
                    act.wait_ge(S.tab_a, 1)
                    av(tsm[:, 8, :], tsm[:, 7, :], ACT.Tanh).then_inc(S.tab_b, 1)

            def spectra(b):
                act.wait_ge(S.qf_done, b + 1)
                if b >= 1:
                    act.wait_ge(S.m12_done, b)
                av(qf, bank[0][:, :], ACT.Identity).then_inc(S.qf_sb, 1)

            def weights(b):
                act.wait_ge(S.rep_done, b + 1)
                for t in range(KD):
                    last = av(ee[:, t * P:(t + 1) * P], bank[3][:, t * P:(t + 1) * P], ACT.Exp, bias=negmax[:, t:t + 1])
                last.then_inc(S.ee_done, 1)

            def products(b):
                act.wait_ge(S.vf_done, b + 1)
                if b >= 1:
                    act.wait_ge(S.m4_done, b)
                av(vri[:, 0, :], bank[5][:, :], ACT.Identity)
                av(vri[:, 1, :], bank[6][:, :], ACT.Identity).then_inc(S.vri_sb, 1)
                act.wait_ge(S.wT_done, b + 1)
                av(wT, bank[4][:, :], ACT.Identity).then_inc(S.wT_sb, 1)

            spectra(0)
            weights(0)
            for b in range(B):
                if b + 1 < B:
                    spectra(b + 1)
                products(b)
                if b + 1 < B:
                    weights(b + 1)

            def turned(b, n, bk):
                act.wait_ge(S.xTt, n + 1)
                av(x2T[:, :, b * L:(b + 1) * L], bank[bk][:, :].rearrange("p (k t) -> p k t", k=KD),
                   ACT.Identity).then_inc(S.xT_sb, 1)

            for b in range(B):
                turned(b, b, b % 2)
            for b in range(B):
                turned(b, B + b, b % 2)
            def keys_values(at):
                if at in KV_EMPTY:
                    return
                n = at - sum(at > e for e in KV_EMPTY)
                act.wait_ge(S.kv_ps, n + 1)
                o = bank[3 + 4 * (n % 2)][:, :]
                if n < 2 * NKV:
                    av(KT[:, n // 2, (n % 2) * HT:(n % 2 + 1) * HT], o, ACT.Identity,
                       bias=pc("bk")[:, n // 2:n // 2 + 1]).then_inc(S.kv_sb, 1)
                else:
                    b, c = (n - 2 * NKV) // 2, n % 2
                    av(V[:, b, c * 512:(c + 1) * 512], o, ACT.Identity).then_inc(S.kv_sb, 1)

            def split_q(n):
                if n < 2 * NKV * GQ:
                    act.wait_ge((S.wq_in0, S.wq_in1)[n % 2], 16 * (n // 2 + 1))
                    if n >= 3:
                        act.wait_ge(S.q_ps, n - 2)
                    av(wqs[:, 0, n % 3, :], wq_sb[:, n % 2, :], ACT.Identity).then_inc(S.wq_hi, 1)

            keys_values(0)
            for l in range(DEPTH + 1):
                if l == DEPTH:
                    keys_values(1 + KVL * DEPTH)
                    act.wait_ge(S.d_z, 2 * DEPTH)
                    for j in range(3):
                        split_q(j)
                if l < DEPTH:
                    for h in range(2):
                        act.wait_ge(S.d_tr, 4 * l + h + 1)
                        av(dys[:, h, :], bank[4 * h][:, :], ACT.Silu, scale=pc("ln1w")[:, l:l + 1],
                           bias=pc("ln1b")[:, l:l + 1]).then_inc(S.d_ys, 1)
                        keys_values(1 + KVL * l + h)
                    for h in range(2):
                        keys_values(1 + KVL * l + 2 + h)
                wn_, bn_ = (pc("ln2w")[0:DIM, l:l + 1], pc("ln2b")[0:DIM, l:l + 1]) if l < DEPTH else \
                    (pc("lnlw")[0:DIM, :], pc("lnlb")[0:DIM, :])
                for h in range(2):
                    act.wait_ge(S.d_tr, 4 * l + (2 if l < DEPTH else 0) + h + 1)
                    av(dys[0:DIM, h, :], bank[4 * h][0:DIM, :], ACT.Identity, scale=wn_, bias=bn_).then_inc(S.d_yT, 1)
                    if l < DEPTH:
                        keys_values(1 + KVL * l + 4 + h)
                if l < DEPTH:
                    for h in range(2):
                        act.wait_ge(S.d_f1, 2 * l + h + 1)
                        for k in range(2):
                            last = av(df[:, h, k, :], bank[4 * h + 2 * k][:, :], ACT.Silu,
                                      bias=pc("b1")[:, 2 * l + k:2 * l + k + 1])
                        last.then_inc(S.d_f, 1)
                    for h in range(2):
                        keys_values(1 + KVL * l + 6 + h)
            NU = 2 * NKV

            def split_o(n):
                act.wait_ge((S.wo_in0, S.wo_in1, S.wo_in2)[n % 3], 16 * (n // 3 + 1))
                if n >= 8:
                    act.wait_ge(S.op_ps, (n // GQ - 1) * HB)
                av(wos[:, 0, n % 8, :], wo_sb[:, n % 3, :], ACT.Identity).then_inc(S.wo_hi, 1)

            def turned_half(h, b, bk):
                gb = h * HB + b
                act.wait_ge(S.xTt, 2 * B + gb + 1)
                if h and b == 0:
                    act.wait_ge(S.q_ps, NKV * GQ)
                av(xs[:, 0, :, b * L:(b + 1) * L], bank[bk][:, :].rearrange("p (k t) -> p k t", k=KD),
                   ACT.Identity).then_inc(S.x4_hi, 1)

            for b in range(HB):
                turned_half(0, b, b % 2)

            def query_out(v, j):
                if v >= NU:
                    return
                act.wait_ge(S.q_ps, v * GQ + j + 1)
                av(qT[:, v % 2, j, :], bank[0][:, :], ACT.Identity,
                   bias=pc("bq")[:, (v % NKV) * GQ + j:(v % NKV) * GQ + j + 1]).then_inc(S.q_sb, 1)

            def routed(b, step, bk):
                if step == 0:
                    act.wait_ge(S.xTt, 3 * B + b + 1)
                    if b >= 2:
                        act.wait_ge(S.r_ps, b - 1)
                    av(x5T[:, b % 2, :, :], bank[bk][:, :].rearrange("p (k t) -> p k t", k=KD),
                       ACT.Identity).then_inc(S.xT_sb, 1)
                else:
                    act.wait_ge(S.wh_ps, b + 1)
                    if b >= 1:
                        act.wait_ge(S.rf_ps, b)
                    av(whT, bank[bk][:, 0:P], ACT.Identity).then_inc(S.whT_done, 1)

            for j in range(GQ):
                query_out(0, j)
                split_q(j + 3)
            for s in range(SLOTS):
                v, b = s // HB, s % HB
                if s < NU * HB:
                    act.wait_ge(S.p_es, s + 1)
                    av(pe_[:, s % 2, :], pe_[:, s % 2, :], ACT.Exp, scale=SQ).then_inc(S.p_exp, 1)
                    if s == (NKV - 1) * HB:
                        for i in range(HB):
                            turned_half(1, i, (2, 0)[i % 2])
                    query_out(v + 1, b)
                    split_q((v + 1) * GQ + b + 3)
                    split_o(s)
                if 1 <= s <= NU * HB:
                    r = s - 1
                    act.wait_ge(S.t_ps, r + 1)
                    if r >= 2:
                        act.wait_ge(S.av_ps, r - 1)
                    av(pT[:, r % 2, :], bank[2][:, :], ACT.Identity).then_inc(S.t_sb, 1)
                if 2 <= s < NU * HB + 2:
                    r = s - 2
                    rv, rb = r // HB, r % HB
                    act.wait_ge(S.av_ps, r + 1)
                    if r >= 3:
                        act.wait_ge(S.op_ps, r - 2)
                    av(osp[:, 0, r % 3, :], bank[3][:, :], ACT.Identity,
                       bias=pc("bv")[:, rv % NKV:rv % NKV + 1]).then_inc(S.o_hi, 1)
                for rb, step, bk in routed_at(s):
                    if step in (0, 2):
                        routed(rb, step, bk)

        def rstd(pool, stage, b):
            pool.wait_ge(S.ln_ve, lnc(stage, b))
            nc.gpsimd.tensor_tensor(lnrs[:, b:b + 1], lnve[:, b:b + 1], halfneg[:, 0:1], ALU.pow).then_inc(S.ln_rs, 1)

        @block.gpsimd
        def _(pool):
            gp = nc.gpsimd
            chain = [0]

            def link(ins):
                chain[0] += 1
                ins.then_inc(S.pool_chain, 1)
                pool.wait_ge(S.pool_chain, chain[0])

            def pad(h):
                gp.memset(xpad[:, :, :, 0:CV - 1], 0.0).then_inc(S.pad_zero, 1)

            link(gp.memset(halfneg[:, :], -0.5))
            pad(0)
            def rest_of(out_, whole, hi, ready, value, done):
                pool.wait_ge(ready, value)
                gp.tensor_tensor(out_, whole, hi.bitcast(F32), ALU.subtract).then_inc(done, 1)

            for h in range(2):
                if h:
                    pool.wait_ge(S.y_done, MD)
                    pad(1)
                for m in range(16):
                    i = h * 16 + m
                    rest_of(win_s[:, 1, i % 3, :], wring[:, i % 4, :], win_s[:, 0, i % 3, :], S.wi_hi, i + 1, S.wi_lo)
                    if m == BACK_AT + 1:
                        pool.wait_ge(S.ssm_ve, h + 1)
                        gp.tensor_tensor(ssm_rs[:, 0:3 * HB], ssm_ms[:, 0:3 * HB], halfneg[:, 0:3 * HB],
                                         ALU.pow).then_inc(S.ssm_rs, 1)

                def base(m):
                    pool.wait_ge(S.dt_relu, h * MD + m + 1)
                    pool.wait_ge(S.dt_w, h * MD + m + 1)
                    gp.tensor_tensor(sp_r[:, m, :], sp_r[:, m, :], dt[:, m, :], ALU.subtract).then_inc(S.dt_base, 1)

                for m in range(EARLY):
                    base(m)
                for m in range(MD):
                    pool.wait_ge(S.dtu_done, h * MD + m + 1)
                    for q in range(GS):
                        i = (h * MD + m) * GS + q
                        if EARLY <= m * GS + q - 1 < MD:
                            base(m * GS + q - 1)
                        if m == 0:
                            pool.wait_ge((S.b_in0, S.b_in1, S.b_in2, S.b_in3)[q * NG // 4], 16 * (h + 1))
                        if i >= 2:
                            pool.wait_ge(S.scan_done, i - 1)
                        gp.tensor_tensor(bu[:, i % 2, :, :], dtu[:, m % 2, :].unsqueeze(1).to_broadcast([P, NG, HT]),
                                         Brep[:, q * NG:(q + 1) * NG, :], ALU.mult).then_inc(S.bu_done, 1)
                if h == 0:
                    pool.wait_ge(S.tab_c, 1)
                    gp.tensor_tensor(tsm[:, 5, :], tsm[:, 4, :], halfneg[:, 0:DEPTH], ALU.pow).then_inc(S.tab_d, 1)
                for b in range(h * HB, (h + 1) * HB):
                    rstd(pool, 0, b)
            pool.wait_ge(S.sz_in, 64)
            for k in range(KD):
                pool.wait_ge(S.qw_in, 16 * (k + 1))
                link(gp.tensor_copy(weff[:, k, :], qw_sb[:, 0, :]))
                link(gp.tensor_tensor(weff[:, k, :], weff[:, k, :], sz[:, 1, k, :], ALU.subtract))
                gp.tensor_tensor(weff[:, k, :], weff[:, k, :], sz[:, 0, k, :], ALU.mult).then_inc(S.deq_done, 1)
                rstd(pool, 1, k)
            mod, ta, tb = tsm[:, 8, :], tsm[:, 2, :], tsm[:, 3, :]

            def table_start():
                pool.wait_ge(S.tab_e, 1)
                pool.wait_ge(S.wout_done, 2 * HB)
                gp.memset(ctab[:, :, 0:1], 1.0)
                gp.memset(stab[:, :, 0:1], 0.0)
                gp.tensor_copy(ctab[:, :, 1:2], ta.unsqueeze(2))
                link(gp.tensor_copy(stab[:, :, 1:2], tb.unsqueeze(2)))

            def table_round(k):
                sh = [P, DEPTH, k]
                cl, sl = ctab[:, :, 1:k + 1], stab[:, :, 1:k + 1]
                ck, sk = ctab[:, :, k:k + 1].to_broadcast(sh), stab[:, :, k:k + 1].to_broadcast(sh)
                cn, sn = ctab[:, :, k + 1:2 * k + 1], stab[:, :, k + 1:2 * k + 1]
                t0, t1 = ttmp[:, 0, :, 0:k], ttmp[:, 1, :, 0:k]
                gp.tensor_tensor(cn, cl, ck, ALU.mult)
                gp.tensor_tensor(t0, sl, sk, ALU.mult)
                gp.tensor_tensor(sn, sl, ck, ALU.mult)
                link(gp.tensor_tensor(t1, cl, sk, ALU.mult))
                gp.tensor_tensor(cn, cn, t0, ALU.subtract)
                link(gp.tensor_tensor(sn, sn, t1, ALU.add))

            def table_end():
                link(gp.memset(rtab.rearrange("p l (b t) -> p (l b) t", b=HB)[:, :, 0:1], 0.0))
                gp.tensor_tensor(dsc, rw("scl").rearrange("p (l o) -> p l o", l=DEPTH),
                                 pc("twoI").unsqueeze(1).to_broadcast([P, DEPTH, DIM]), ALU.mult).then_inc(S.tab_done, 1)

            table_start()
            rounds = [1 << r for r in range(7)]
            for b in range(KD, B):
                rstd(pool, 1, b)
                for k in rounds[2 * (b - KD):2 * (b - KD) + 2]:
                    table_round(k)
            link(gp.tensor_copy(ctab[DIM:P, :, :], stab[DIM:P, :, :]))

            def bias(b, n, name):
                pool.wait_ge(S.xTt, n + 1)
                gp.tensor_tensor(x_tok[:, b, :], x_tok[:, b, :], rw(name), ALU.add).then_inc(S.xbias, 1)

            bias(0, 0, "fbias")
            for b in range(B):
                if b + 1 < B:
                    bias(b + 1, b + 1, "fbias")
                rstd(pool, 2, b)
                if b < DEPTH:
                    link(gp.tensor_copy(rtab[:, b, :], mod[:, b:b + 1].to_broadcast([P, HT])))
                elif b == DEPTH:
                    table_end()
            for b in range(B):
                bias(b, B + b, "bout")

            def rest_q(n):
                if n < 2 * NKV * GQ:
                    rest_of(wqs[:, 1, n % 3, :], wq_sb[:, n % 2, :], wqs[:, 0, n % 3, :], S.wq_hi, n + 1, S.wq_lo)

            for i in range(2 * (2 * DEPTH + 1)):
                pool.wait_ge(S.d_ve, i + 1)
                h = i % 2
                gp.tensor_tensor(drs[:, h * HB:(h + 1) * HB], dve_[:, h * HB:(h + 1) * HB], halfneg[:, 0:HB],
                                 ALU.pow).then_inc(S.d_rs, 1)
            for n in range(3):
                rest_q(n)
            for b in range(B):
                rstd(pool, 3, b)
                if b >= HB:
                    rest_q(b - HB + 3)
            for s in range(SLOTS):
                if s < 2 * NKV * HB:
                    rest_q(s + 7)
                    rest_of(wos[:, 1, s % 8, :], wo_sb[:, s % 3, :], wos[:, 0, s % 8, :], S.wo_hi, s + 1, S.wo_lo)
                for b in range(B):
                    if s == (0 if b < HB else (NKV - 1) * HB) + b % HB:
                        bias(b, 2 * B + b, "bo")
                u, b = (s - 4) // HB, (s - 4) % HB
                if u % NKV == NKV - 1 and 4 <= s < 2 * NKV * HB + 4:
                    rstd(pool, 4, (u // NKV) * HB + b)
                for rb, step, bk in routed_at(s):
                    if step == 3:
                        rstd(pool, 5, rb)

        @block.vector
        def _(dve):
            v = nc.vector
            chain = [0]

            def link(ins):
                chain[0] += 1
                ins.then_inc(S.dve_chain, 1)
                dve.wait_ge(S.dve_chain, chain[0])

            def tables():
                pr, pi = pc("pre"), pc("pim")
                T = [tsm[:, i, :] for i in range(12)]
                z, m, a, b_, ssq, rsq, one, rmod, th, ta, tb, tc = T
                link(v.scalar_tensor_tensor(out=m, in0=pr, scalar=-1.0, in1=pr, op0=ALU.mult, op1=ALU.max))
                link(v.scalar_tensor_tensor(out=ta, in0=pi, scalar=-1.0, in1=pi, op0=ALU.mult, op1=ALU.max))
                link(v.tensor_tensor(m, m, ta, ALU.max))
                link(v.tensor_scalar(z, m, 0.0, None, ALU.is_equal))
                link(v.tensor_tensor(ta, m, z, ALU.add))
                link(v.reciprocal(tb, ta))
                link(v.tensor_tensor(a, pr, tb, ALU.mult))
                link(v.tensor_tensor(a, a, z, ALU.add))
                link(v.scalar_tensor_tensor(out=b_, in0=pi, scalar=-1.0, in1=tb, op0=ALU.mult, op1=ALU.mult))
                link(v.tensor_tensor(ta, a, a, ALU.mult))
                link(v.tensor_tensor(tb, b_, b_, ALU.mult))
                v.tensor_tensor(ssq, ta, tb, ALU.add).then_inc(S.tab_c, 1)
                dve.wait_ge(S.tab_d, 1)
                link(v.tensor_tensor(ta, ssq, rsq, ALU.mult))
                v.tensor_tensor(rmod, ta, m, ALU.mult).then_inc(S.tab_a, 1)
                link(v.tensor_tensor(a, a, rsq, ALU.mult))
                link(v.tensor_tensor(b_, b_, rsq, ALU.mult))
                link(v.tensor_tensor(ta, a, a, ALU.mult))
                link(v.tensor_tensor(tb, b_, b_, ALU.mult))
                link(v.tensor_tensor(ta, ta, tb, ALU.add))
                link(v.tensor_scalar(ta, ta, -0.5, 1.5, ALU.mult, ALU.add))
                link(v.tensor_tensor(a, a, ta, ALU.mult))
                link(v.tensor_tensor(b_, b_, ta, ALU.mult))
                dve.wait_ge(S.tab_b, 1)
                link(v.tensor_tensor(ta, th, a, ALU.mult))
                link(v.scalar_tensor_tensor(out=tb, in0=th, scalar=-1.0, in1=b_, op0=ALU.mult, op1=ALU.mult))
                lo, hi = slice(0, DIM), slice(DIM, P)
                lr, li = pc("lre"), pc("lim")
                link(v.tensor_tensor(tc[lo], tb[lo], li[lo], ALU.mult))
                link(v.tensor_tensor(one[lo], ta[lo], lr[lo], ALU.mult))
                link(v.tensor_tensor(z[lo], one[lo], tc[lo], ALU.subtract))
                link(v.tensor_tensor(tc[hi], tb[hi], lr[hi], ALU.mult))
                link(v.tensor_tensor(one[hi], ta[hi], li[hi], ALU.mult))
                v.tensor_tensor(z[hi], one[hi], tc[hi], ALU.add).then_inc(S.tab_e, 1)
                dve.wait_ge(S.tab_e, 1)
                return z

            def ln_a(stage, b, ps, ready, value):
                dve.wait_ge(ready, value)
                if stage == 0:
                    dve.wait_ge(S.xtok_in, 16)
                bias_n = {2: b + 1, 3: B + b + 1, 4: 2 * B + b + 1}.get(stage)
                if bias_n:
                    dve.wait_ge(S.xbias, bias_n)
                v.tensor_tensor(x_tok[:, b, :], x_tok[:, b, :], ps, ALU.add).then_inc(S.x_sum, 1)
                dve.wait_ge(S.x_sum, lnc(stage, b))
                link(v.bn_stats(lnst[:, b, :], x_tok[:, b, :]))
                link(v.bn_aggr(lnmv[:, b, :], lnst[:, b, :]))
                v.tensor_scalar(lnve[:, b:b + 1], lnmv[:, b, 1:2], 1e-5, None, ALU.add).then_inc(S.ln_ve, 1)

            def ln_b(stage, b):
                dve.wait_ge(S.ln_rs, lnc(stage, b))
                v.tensor_scalar(x_tok[:, b, :], x_tok[:, b, :], lnmv[:, b, 0:1], lnrs[:, b:b + 1],
                                ALU.subtract, ALU.mult).then_inc(S.x_done, 1)

            v.memset(zeros[:, :], 0.0).then_inc(S.zero_done, 1)
            dve.wait_ge(S.par_in, 16)
            dve.wait_ge(S.amat_done, 1)
            link(v.tensor_scalar(amat[:, :], amat[:, :], -1.0, None, ALU.mult))
            for h in range(2):
                for k in range(KD):
                    dve.wait_ge(S.xs_hi, h * KD + k + 1)
                    v.tensor_tensor(xin[:, 1, k, :], xTh[:, k, :], xin[:, 0, k, :].bitcast(F32),
                                    ALU.subtract).then_inc(S.xs_lo, 1)
                dve.wait_ge(S.pad_zero, h + 1)
                for m in range(MD):
                    dve.wait_ge(S.in_evac, h * 16 + m + 1)
                    if h * MD + m >= 2:
                        dve.wait_ge(S.u_done, h * MD + m - 1)
                    acc = conv[:, m % 2, :].rearrange("p (b t) -> p b t", b=HB)
                    w = pc("convw")[:, m * CV:(m + 1) * CV]
                    link(v.tensor_scalar(acc, xpad[:, m % 2, :, 0:L], w[:, 0:1], pc("convb")[:, m:m + 1],
                                         ALU.mult, ALU.add))
                    for j in range(1, CV):
                        ins = v.scalar_tensor_tensor(out=acc, in0=xpad[:, m % 2, :, j:j + L], scalar=w[:, j:j + 1],
                                                     in1=acc, op0=ALU.mult, op1=ALU.add)
                        if j < CV - 1:
                            link(ins)
                        else:
                            ins.then_inc(S.conv_done, 1)
                dve.wait_ge(S.ssm_sq, h + 1)
                link(v.tensor_reduce(ssm_ss[:, 0:4 * HB], ssmsq.rearrange("p (a c) -> p a c", c=NS), AX.X, ALU.add))
                ss = ssm_ss[:, 0:4 * HB].rearrange("p (b c) -> p b c", b=HB)
                ms = ssm_ms[:, 0:3 * HB].rearrange("p (b c) -> p b c", b=HB)
                rs = ssm_rs[:, 0:3 * HB].rearrange("p (b c) -> p b c", b=HB)
                link(v.tensor_tensor(ms[:, :, 0:1], ss[:, :, 0:1], ss[:, :, 1:2], ALU.add))
                link(v.tensor_scalar(ms[:, :, 0:1], ms[:, :, 0:1], 1.0 / RK, 1e-6, ALU.mult, ALU.add))
                v.tensor_scalar(ms[:, :, 1:3], ss[:, :, 2:4], 1.0 / NS, 1e-6, ALU.mult, ALU.add).then_inc(S.ssm_ve, 1)
                dve.wait_ge(S.ssm_rs, h + 1)
                pb = bank[2][:, 0:HB * SSM].rearrange("p (b c) -> p b c", b=HB)
                for i, (a, b_) in enumerate(((0, RK), (RK, RK + NS), (RK + NS, SSM))):
                    ins = v.tensor_tensor(ssmn[:, :, a:b_], pb[:, :, a:b_], rs[:, :, i:i + 1].to_broadcast([P, HB, b_ - a]),
                                          ALU.mult)
                    if i < 2:
                        link(ins)
                    else:
                        ins.then_inc(S.ssm_norm, 1)
                for m in range(MD):
                    dve.wait_ge(S.dt_abs, h * MD + m + 1)
                    v.tensor_scalar(sp_r[:, m, :], bank[4 + m % 4][:, :], pc("bdt")[:, m:m + 1], 0.0,
                                    ALU.add, ALU.max).then_inc(S.dt_relu, 1)

                def one_plus(m):
                    dve.wait_ge(S.dt_exp, h * MD + m + 1)
                    v.tensor_scalar(sp_w[:, m, :], dt[:, m, :], 1.0, None, ALU.add).then_inc(S.dt_w0, 1)
                    dve.wait_ge(S.dt_w0, h * MD + m + 1)
                    v.scalar_tensor_tensor(out=dt[:, m, :], in0=sp_w[:, m, :], scalar=1.0, in1=dt[:, m, :],
                                           op0=ALU.subtract, op1=ALU.subtract).then_inc(S.dt_w, 1)

                def step_size(m):
                    dve.wait_ge(S.dt_ln, h * MD + m + 1)
                    dve.wait_ge(S.dt_base, h * MD + m + 1)
                    v.tensor_tensor(dt[:, m, :], sp_r[:, m, :], sp_w[:, m, :], ALU.add).then_inc(S.dt_done, 1)

                def step_in(m):
                    if h * MD + m >= 2:
                        dve.wait_ge(S.bu_done, (h * MD + m - 1) * GS)
                    dve.wait_ge(S.dt_done, h * MD + m + 1)
                    v.tensor_tensor(dtu[:, m % 2, :], dt[:, m, :], u[:, m, :], ALU.mult).then_inc(S.dtu_done, 1)

                def c_times(i):
                    q = i % GS
                    if (i // GS) % MD == 0:
                        dve.wait_ge((S.c_in0, S.c_in1, S.c_in2, S.c_in3)[q * NG // 4], 16 * (h + 1))
                    if i >= 2:
                        dve.wait_ge(S.ysum, i - 1)
                    dve.wait_ge(S.scan_done, i + 1)
                    v.tensor_tensor(prod[:, i % 2, :, :], dA[:, i % 3, :, :], Crep[:, q * NG:(q + 1) * NG, :],
                                    ALU.mult).then_inc(S.prod_done, 1)

                def scan(i):
                    dve.wait_ge(S.dA_done, i + 1)
                    dve.wait_ge(S.bu_done, i + 1)
                    d = dA[:, i % 3, :, :].rearrange("p n t -> p (n t)")
                    v.tensor_tensor_scan(d, d, bu[:, i % 2, :, :].rearrange("p n t -> p (n t)"), 0.0,
                                         ALU.mult, ALU.add).then_inc(S.scan_done, 1)

                def finish_y(m):
                    dve.wait_ge(S.ysum, (h * MD + m + 1) * GS)
                    v.tensor_tensor(g[:, m, :], bank[6 + m % 2][:, :], g[:, m, :], ALU.mult).then_inc(S.y_done, 1)

                for m in range(EARLY):
                    one_plus(m)
                step_size(0)
                step_in(0)
                step_size(1)
                scan(h * MD * GS)
                for m in range(MD):
                    for q in range(GS):
                        i = (h * MD + m) * GS + q
                        if i + 1 < (h + 1) * MD * GS:
                            scan(i + 1)
                        if m == 0 and q + EARLY < MD:
                            one_plus(q + EARLY)
                        if q == 1 and 1 <= m < MD - 1:
                            step_size(m + 1)
                        if q == 3 and m + 1 < MD:
                            step_in(m + 1)
                        if q == 5 and m >= 1:
                            finish_y(m - 1)
                        c_times(i)
                finish_y(MD - 1)
                if h == 0:
                    plc = tables()
                for b in range(h * HB, (h + 1) * HB):
                    ln_a(0, b, bank[b % 2][:, :], S.wout_done, b + 1)
                    if b > h * HB:
                        ln_b(0, b - 1)
                ln_b(0, (h + 1) * HB - 1)

            link(v.memset(m9, -BIG))

            def spectra(b):
                dve.wait_ge(S.qf_sb, b + 1)
                dve.wait_ge(S.kf_done, b + 1)
                if b >= 1:
                    dve.wait_ge(S.corr, b)
                v.tensor_tensor(m12, qf.unsqueeze(1).to_broadcast([P, 2, D]),
                                psum[:, D:3 * D].rearrange("p (i n) -> p i n", i=2), ALU.mult).then_inc(S.m12_done, 1)

            def topk(b):
                dve.wait_ge(S.corr, b + 1)
                cor = bank[3][:, :]
                for t in range(KD):
                    o = slice(t * P, (t + 1) * P)
                    last = v.max(mx8[:, t * 8:t * 8 + 8], cor[:, o])
                link(last)
                v.tensor_scalar(negmax.unsqueeze(2), mx8.rearrange("p (t n) -> p t n", t=KD)[:, :, 0:1], -1.0, None,
                                ALU.mult)
                for t in range(KD):
                    o = slice(t * P, (t + 1) * P)
                    last = v.match_replace(rep1[:, o], mx8[:, t * 8:t * 8 + 8], cor[:, o], -BIG)
                last.then_inc(S.rep_done, 1)
                dve.wait_ge(S.rep_done, b + 1)
                for t in range(KD):
                    last = v.max(nx8[:, t * 8:t * 8 + 8], rep1[:, t * P:(t + 1) * P])
                link(last)
                link(v.tensor_copy(m9.rearrange("p (t n) -> p t n", t=KD)[:, :, 0:TOPK - 8],
                                   nx8.rearrange("p (t n) -> p t n", t=KD)[:, :, 0:TOPK - 8]))
                for t in range(KD):
                    o = slice(t * P, (t + 1) * P)
                    last = v.match_replace(rep2[:, o], m9[:, t * 8:t * 8 + 8], rep1[:, o], -BIG)
                link(last)
                dve.wait_ge(S.ee_done, b + 1)
                link(v.scalar_tensor_tensor(out=rep2, in0=rep2, scalar=-BIG, in1=ee, op0=ALU.is_equal, op1=ALU.mult))
                link(v.tensor_reduce(wsum[:, 0:KD], rep2.rearrange("p (t n) -> p t n", t=KD), AX.X, ALU.add))
                link(v.reciprocal(winv[:, 0:KD], wsum[:, 0:KD]))
                if b >= 2:
                    dve.wait_ge(S.wT_done, b - 1)
                v.tensor_tensor(wn[:, b % 2, :].rearrange("p (t n) -> p t n", t=KD),
                                rep2.rearrange("p (t n) -> p t n", t=KD),
                                winv[:, 0:KD].unsqueeze(2).to_broadcast([P, KD, P]), ALU.mult).then_inc(S.wn_done, 1)

            def products(b):
                dve.wait_ge(S.wf_done, b + 1)
                dve.wait_ge(S.vri_sb, b + 1)
                if b >= 1:
                    dve.wait_ge(S.xat_done, b)
                v.tensor_tensor(m4[:, 0:2, :], vri, bank[5][:, :].unsqueeze(1).to_broadcast([P, 2, D]), ALU.mult)
                v.tensor_tensor(m4[:, 2:4, :], vri, bank[6][:, :].unsqueeze(1).to_broadcast([P, 2, D]),
                                ALU.mult).then_inc(S.m4_done, 1)

            spectra(0)
            topk(0)
            for b in range(B):
                if b + 1 < B:
                    spectra(b + 1)
                if b >= 1:
                    ln_a(1, b - 1, bank[7][:, :], S.xat_done, b)
                products(b)
                if b >= 1:
                    ln_b(1, b - 1)
                if b + 1 < B:
                    topk(b + 1)
            for k in range(KD):
                dve.wait_ge(S.lora_done, k + 1)
                dve.wait_ge(S.deq_done, k + 1)
                v.scalar_tensor_tensor(out=weff[:, k, :], in0=bank[1 + k][:, :], scalar=1.0 / 16, in1=weff[:, k, :],
                                       op0=ALU.mult, op1=ALU.add).then_inc(S.weff_done, 1)
            ln_a(1, B - 1, bank[7][:, :], S.xat_done, B)
            ln_b(1, B - 1)
            for b in range(B):
                ln_a(2, b, bank[2 + b % 2][:, :], S.ffn_done, b + 1)
                if b >= 1:
                    ln_b(2, b - 1)
            ln_b(2, B - 1)
            dve.wait_ge(S.tab_done, 1)
            for h in range(2):
                dve.wait_ge(S.h0_done, h + 1)
                hs = slice(h * HB, (h + 1) * HB)
                v.tensor_tensor(dh[:, hs, :], bank[4 + h][:, 0:HB * DIM].rearrange("p (b c) -> p b c", b=HB),
                                rw("bin").unsqueeze(1).to_broadcast([P, HB, DIM]), ALU.add).then_inc(S.h0_read, 1)
            dve.wait_ge(S.h0_read, 2)

            def stats(h):
                for b in range(h * HB, (h + 1) * HB):
                    last = v.bn_stats(dst[:, b, :], dh[:, b, :])
                link(last)
                for b in range(h * HB, (h + 1) * HB):
                    last = v.bn_aggr(dmv[:, b, :], dst[:, b, :])
                link(last)
                hs = slice(h * HB, (h + 1) * HB)
                v.tensor_scalar(dve_[:, hs], dmv[:, hs, 1:2].rearrange("p b o -> p (b o)"), 1e-5, None,
                                ALU.add).then_inc(S.d_ve, 1)
                link(v.tensor_tensor(dhc[:, hs, :], dh[:, hs, :], dmv[:, hs, 0:1].to_broadcast([P, HB, DIM]),
                                     ALU.subtract))

            def norm(n, h, copies, free):
                dve.wait_ge(S.d_rs, n)
                if free:
                    dve.wait_ge(S.d_tr, free)
                hs = slice(h * HB, (h + 1) * HB)
                for c in range(copies):
                    last = v.tensor_tensor(dyn[:, h, :, c * DIM:(c + 1) * DIM], dhc[:, hs, :],
                                           drs[:, hs].unsqueeze(2).to_broadcast([P, HB, DIM]), ALU.mult)
                last.then_inc(S.d_yn, 1)

            for l in range(DEPTH):
                for h in range(2):
                    stats(h)
                for h in range(2):
                    norm(4 * l + h + 1, h, 2, 4 * l)
                for h in range(2):
                    dve.wait_ge(S.d_ys, 2 * l + h + 1)
                    if l:
                        dve.wait_ge(S.d_conv, 2 * l)
                    z3 = dz[:, h, :].rearrange("p (b t) -> p b t", b=HB)
                    tab = ctab[:, l, 0:L].unsqueeze(1).to_broadcast([P, HB, L])
                    link(v.tensor_tensor(z3, dys[:, h, :].rearrange("p (b t) -> p b t", b=HB), tab, ALU.mult))
                    link(v.tensor_scalar(z3[:, :, 0:1], z3[:, :, 0:1], plc[:, l:l + 1], None, ALU.add))
                    link(v.tensor_tensor_scan(dz[:, h, :], rtab[:, l, :], dz[:, h, :], 0.0, ALU.mult, ALU.add))
                    v.tensor_tensor(z3, z3, tab, ALU.mult).then_inc(S.d_z, 1)
                for h in range(2):
                    hs = slice(h * HB, (h + 1) * HB)
                    dve.wait_ge(S.d_conv, 2 * l + h + 1)
                    v.tensor_tensor(dh[:, hs, :], dh[:, hs, :],
                                    bank[4 * h + 1][:, 0:HB * DIM].rearrange("p (b c) -> p b c", b=HB),
                                    ALU.add).then_inc(S.d_hread, 1)
                    dve.wait_ge(S.d_hread, 2 * l + h + 1)
                    stats(h)
                for h in range(2):
                    norm(4 * l + 2 + h + 1, h, 1, 4 * l + 2)
                for h in range(2):
                    hs = slice(h * HB, (h + 1) * HB)
                    link(v.tensor_tensor(dh[:, hs, :], dh[:, hs, :],
                                         rw("b2")[:, l * DIM:(l + 1) * DIM].unsqueeze(1).to_broadcast([P, HB, DIM]),
                                         ALU.add))
                    dve.wait_ge(S.d_f2, 2 * l + h + 1)
                    v.tensor_tensor(dh[:, hs, :], dh[:, hs, :],
                                    bank[4 * h + 1][:, 0:HB * DIM].rearrange("p (b c) -> p b c", b=HB),
                                    ALU.add).then_inc(S.d_f2read, 1)
                    dve.wait_ge(S.d_f2read, 2 * l + h + 1)
            for h in range(2):
                stats(h)
            for h in range(2):
                norm(4 * DEPTH + h + 1, h, 1, 4 * DEPTH)
            def network_ln(h):
                for b in range(h * HB, (h + 1) * HB):
                    ln_a(3, b, bank[2 + 4 * (b % 2)][:, :], S.d_out, b + 1)
                    if b % HB:
                        ln_b(3, b - 1)
                ln_b(3, (h + 1) * HB - 1)

            network_ln(0)
            NU = 2 * NKV
            sh = [P, GQ, P]

            def soft_a(s):
                dve.wait_ge(S.s_ps, s + 1)
                ps = bank[1][:, :].rearrange("p (j m) -> p j m", j=GQ)
                link(v.tensor_reduce(amax[:, :], ps, AX.X, ALU.max))
                if s >= 2:
                    dve.wait_ge(S.p_norm, s - 1)
                v.tensor_tensor(pe_[:, s % 2, :].rearrange("p (j m) -> p j m", j=GQ), ps,
                                amax[:, :].unsqueeze(2).to_broadcast(sh), ALU.subtract).then_inc(S.p_es, 1)

            def soft_b(s):
                dve.wait_ge(S.p_exp, s + 1)
                pr = pe_[:, s % 2, :].rearrange("p (j m) -> p j m", j=GQ)
                link(v.tensor_reduce(asum[:, 0, :], pr, AX.X, ALU.add))
                link(v.reciprocal(ainv[:, :], asum[:, 0, :]))
                if s >= 1:
                    dve.wait_ge(S.t_ps, s)
                v.tensor_tensor(pn.rearrange("p (j m) -> p j m", j=GQ), pr, ainv[:, :].unsqueeze(2).to_broadcast(sh),
                                ALU.mult).then_inc(S.p_norm, 1)

            def x_rest(h, b, bk):
                dve.wait_ge(S.x4_hi, h * HB + b + 1)
                o = slice(b * L, (b + 1) * L)
                v.tensor_tensor(xs[:, 1, :, o], bank[bk][:, :].rearrange("p (k t) -> p k t", k=KD),
                                xs[:, 0, :, o].bitcast(F32), ALU.subtract).then_inc(S.x4_lo, 1)

            def o_rest(r):
                dve.wait_ge(S.o_hi, r + 1)
                u = r // HB % NKV
                v.scalar_tensor_tensor(out=osp[:, 1, r % 3, :], in0=bank[3][:, :], scalar=pc("bv")[:, u:u + 1],
                                       in1=osp[:, 0, r % 3, :].bitcast(F32), op0=ALU.add,
                                       op1=ALU.subtract).then_inc(S.o_sb, 1)

            def route(b):
                dve.wait_ge(S.r_ps, b + 1)
                link(v.tensor_copy(logits, bank[2][:, P:P + 8]))
                link(v.max(rt8, logits))
                link(v.max_index(ri8[:, :], rt8, logits))
                link(v.tensor_copy(rif, ri8[:, :]))
                link(v.tensor_scalar(rwt, pc("iota8"), rif[:, 0:1], rt8[:, 0:1], ALU.is_equal, ALU.mult))
                if b >= 1:
                    dve.wait_ge(S.wh_ps, b)
                v.tensor_tensor(wh.rearrange("p (e r) -> p e r", e=8), bank[2][:, 0:P].rearrange("p (e r) -> p e r", e=8),
                                rwt.unsqueeze(2).to_broadcast([P, 8, 16]), ALU.mult).then_inc(S.r_wh, 1)

            for b in range(HB):
                x_rest(0, b, b % 2)
            network_ln(1)
            for s in range(SLOTS):
                if s < NU * HB:
                    soft_a(s)
                    if s == (NKV - 1) * HB:
                        for b in range(HB):
                            x_rest(1, b, (2, 0)[b % 2])
                    soft_b(s)
                if 2 <= s <= NU * HB + 1:
                    o_rest(s - 2)
                if 4 <= s < NU * HB + 4:
                    r = s - 4
                    rv, rb = r // HB, r % HB
                    if rv % NKV == NKV - 1:
                        b = (rv // NKV) * HB + rb
                        ln_a(4, b, bank[4 + rb][:, :], S.op_ps, r + 1)
                        ln_b(4, b)
                for rb, step, bk in routed_at(s):
                    if step == 1:
                        route(rb)
                    elif step == 3:
                        ln_a(5, rb, bank[bk][:, :], S.rf_ps, rb + 1)
                        ln_b(5, rb)


def kernel(**inp):
    import concourse.bacc as bacc
    from concourse.bass_utils import run_bass_kernel_spmd

    a = {k: np.asarray(v) for k, v in inp.items()}
    cat = np.concatenate

    def cols(v):
        return v.reshape(-1, P).T

    def twice(v):
        return cat([v.T, v.T], 0)

    x, ctx = a["x"], a["ctx_4096"]
    xT = x.reshape(2, HT, KD, P).transpose(0, 3, 2, 1)
    bkv = a["L1_xattn_bkv"]
    vals = {
        "convw": a["L0_attn_conv_w"].reshape(MD, P, CV).transpose(1, 0, 2).reshape(P, MD * CV),
        "convb": cols(a["L0_attn_conv_b"]), "bdt": cols(a["L0_attn_b_dt"]),
        "alog": a["L0_attn_A_log"].reshape(MD, P, NS).transpose(1, 0, 2).reshape(P, MD * NS),
        "dskip": cols(a["L0_attn_D"]), "bq": cols(a["L1_xattn_bq"]),
        "bk": cols(bkv[:1024]), "bv": cols(bkv[1024:]),
        "ln1w": twice(a["L1_attn_ln1_w"]), "ln1b": twice(a["L1_attn_ln1_b"]),
        "ln2w": twice(a["L1_attn_ln2_w"]), "ln2b": twice(a["L1_attn_ln2_b"]),
        "lnlw": twice(a["L1_attn_lnl_w"][None]), "lnlb": twice(a["L1_attn_lnl_b"][None]),
        "b1": cols(a["L1_attn_b1"].reshape(-1)),
        "pre": twice(a["L1_attn_phz_re"]), "pim": twice(a["L1_attn_phz_im"]),
        "lre": twice(a["L1_attn_lc_re"]), "lim": twice(a["L1_attn_lc_im"]),
        "ident": np.eye(P, dtype=np.float32), "twoI": cat([np.eye(DIM, dtype=np.float32)] * 2, 0),
        "iota8": np.tile(np.arange(8, dtype=np.float32), (P, 1)),
    }
    par = cat([vals[n] for n, _ in _COLS], 1)
    rvals = {"fbias": a["L0_ffn_bias"], "bout": a["L1_attn_bout"], "bo": a["L1_xattn_bo"], "bin": a["L1_attn_bin"],
             "b2": a["L1_attn_b2"].reshape(-1), "scl": a["L1_attn_sc_lin"].reshape(-1)}
    wkv = a["L1_xattn_Wkv"]

    def groups(s):
        return s.T.reshape(KD, 2, D).transpose(1, 0, 2)

    arrays = {
        "xT": xT, "xtok": x.transpose(1, 0, 2),
        "ctxT": ctx.reshape(B * L, KD, P).transpose(2, 1, 0), "ctxtok": ctx.transpose(1, 0, 2),
        "par": par, "rows": cat([rvals[n] for n, _ in _ROWS]), "four": fourier(),
        "win": a["L0_attn_W_in"].reshape(16, P, KD, P).transpose(0, 3, 2, 1).reshape(16, P, 512),
        "wx": a["L0_attn_W_x"].reshape(SSM, MD, P).transpose(2, 1, 0),
        "wdt": a["L0_attn_W_dt"].T, "wout": a["L0_attn_W_out"].T.reshape(MD, P, D),
        "qw": a["L0_ffn_qweight"].T.reshape(KD, P, D), "sc": groups(a["L0_ffn_scales"]),
        "ze": groups(a["L0_ffn_zeros"]), "loraA": a["L0_ffn_lora_A"], "loraBT": a["L0_ffn_lora_B"].T,
        "dwin": a["L1_attn_Win"].reshape(DIM, KD, P).transpose(2, 1, 0),
        "dw1": a["L1_attn_W1"].transpose(2, 0, 1),
        "dw2": a["L1_attn_W2"].reshape(DEPTH, DIM, 2, P).transpose(3, 0, 2, 1),
        "dwout": a["L1_attn_Wout"].T,
        "wq": a["L1_xattn_Wq"].reshape(KD, P, NKV, GQ, P).transpose(2, 1, 3, 0, 4).reshape(NKV, P, GQ * 512),
        "wk": wkv[:, :1024].reshape(KD, P, NKV, P).transpose(2, 1, 0, 3).reshape(NKV, P, 512),
        "wv": wkv[:, 1024:].reshape(KD, P, 1024).transpose(1, 0, 2),
        "wo": a["L1_xattn_Wo"].reshape(NKV, GQ, P, D).transpose(0, 2, 1, 3),
        "ra": cat([a["L1_ffn_A"].reshape(P, D), a["L1_ffn_route_w"]], 0).T.reshape(KD, P, P + 8).transpose(1, 0, 2),
        "bwT": a["L1_ffn_Bw"].transpose(0, 2, 1).reshape(P, D),
    }
    arrays = {k: np.ascontiguousarray(v) for k, v in arrays.items()}
    nc = bacc.Bacc("TRN2", target_bir_lowering=False, num_devices=1)
    args = [nc.dram_tensor(n, v.shape, mybir.dt.from_np(v.dtype), kind="ExternalInput").ap() for n, v in arrays.items()]
    args.append(nc.dram_tensor("out", (B, L, D), F32, kind="ExternalOutput").ap())
    decoder_kernel(nc, *args)
    r = run_bass_kernel_spmd(nc, [arrays], core_ids=[0])
    return r.results[0]["out"]
```
